# Optimizing a Trainium2 kernel written in Bass

```python
import numpy as np
import jax
import jax.numpy as jnp

def _softmax(x, axis=-1):
    return jax.nn.softmax(x, axis=axis)

def _gelu(x):
    return jax.nn.gelu(x, approximate=True)

def _silu(x):
    return jax.nn.silu(x)

def _sigmoid(x):
    return jax.nn.sigmoid(x)

def _layernorm(x, axis=-1, eps=1e-05):
    m = jnp.mean(x, axis=axis, keepdims=True)
    v = jnp.var(x, axis=axis, keepdims=True)
    return (x - m) / jnp.sqrt(v + eps)

def _scatter_add(tgt, idx, src, axis=0):
    return tgt.at[idx].add(src)

def _segment_sum(src, seg, n):
    return jax.ops.segment_sum(src, seg, n)
kernel_name = 'mk_seq_preln_d1_jaxref_r4_5abbea'

def setup_inputs(seed: int=0):
    np.random.seed(seed)
    _w = jnp.asarray

    def _L0_attn_setup():
        import jax, jax.numpy as jnp
        import numpy as np
        import math
        B, T, C = (2, 512, 256)
        H, L = (16, 64)
        DH = C // H
        DHE = DH // 2
        THETA = 10000.0

        def _rope_cache(t, dim):
            inv_freq = 1.0 / THETA ** (jnp.arange(0, dim, 2, dtype=jnp.float32) / dim)
            freqs = jnp.arange(t, dtype=jnp.float32)[:, None] * inv_freq[None, :]
            emb = jnp.concatenate((freqs, freqs), axis=-1)
            return (jnp.cos(emb), jnp.sin(emb))

        def _apply_rope(x, cos, sin):
            x1 = x[..., 0::2]
            x2 = x[..., 1::2]
            rot = jnp.stack((-x2, x1), axis=-1).reshape(x.shape)
            return x * cos[None, None] + rot * sin[None, None]
        key = jax.random.key(seed)
        ks = jax.random.split(key, 10)
        s = 0.02
        return {'x': jax.random.normal(ks[0], (B, T, C), jnp.float32), 'Wq_down': jax.random.normal(ks[1], (C, H * L), jnp.float32) * s, 'Wk_down': jax.random.normal(ks[2], (C, H * L), jnp.float32) * s, 'Wv_down': jax.random.normal(ks[3], (C, H * L), jnp.float32) * s, 'Wq_up_c': jax.random.normal(ks[4], (L, DHE), jnp.float32) * s, 'Wq_up_e': jax.random.normal(ks[5], (L, DHE), jnp.float32) * s, 'Wk_up_c': jax.random.normal(ks[6], (L, DHE), jnp.float32) * s, 'Wk_up_e': jax.random.normal(ks[7], (L, DHE), jnp.float32) * s, 'Wv_up': jax.random.normal(ks[8], (L, DH), jnp.float32) * s, 'Wc': jax.random.normal(ks[9], (C, C), jnp.float32) * s}
    _L0_attn_in = _L0_attn_setup()

    def _L0_ffn_setup():
        import jax, jax.numpy as jnp
        import numpy as np
        HIDDEN = 256
        NUM_EXPERTS = 8
        TOP_K = 2
        B, S = (4, 256)
        key = jax.random.key(seed)
        ks = jax.random.split(key, 8)
        H, E = (HIDDEN, NUM_EXPERTS)
        sc = lambda fan_in: 1.0 / np.sqrt(fan_in)
        x = jax.random.normal(ks[0], (B, S, H), dtype=jnp.float32)
        Wr = jax.random.uniform(ks[1], (H, E), minval=-sc(H), maxval=sc(H), dtype=jnp.float32)
        br = jax.random.uniform(ks[2], (E,), minval=-sc(H), maxval=sc(H), dtype=jnp.float32)
        W1 = jax.random.uniform(ks[3], (E, H, 2 * H), minval=-sc(H), maxval=sc(H), dtype=jnp.float32)
        b1 = jax.random.uniform(ks[4], (E, 2 * H), minval=-sc(H), maxval=sc(H), dtype=jnp.float32)
        W2 = jax.random.uniform(ks[5], (E, 2 * H, H), minval=-sc(2 * H), maxval=sc(2 * H), dtype=jnp.float32)
        b2 = jax.random.uniform(ks[6], (E, H), minval=-sc(2 * H), maxval=sc(2 * H), dtype=jnp.float32)
        return {'x': x, 'Wr': Wr, 'br': br, 'W1': W1, 'b1': b1, 'W2': W2, 'b2': b2}
    _L0_ffn_in = _L0_ffn_setup()
    _d = {'L0_attn_x': _L0_attn_in['x'], 'L0_attn_Wq_down': _L0_attn_in['Wq_down'], 'L0_attn_Wk_down': _L0_attn_in['Wk_down'], 'L0_attn_Wv_down': _L0_attn_in['Wv_down'], 'L0_attn_Wq_up_c': _L0_attn_in['Wq_up_c'], 'L0_attn_Wq_up_e': _L0_attn_in['Wq_up_e'], 'L0_attn_Wk_up_c': _L0_attn_in['Wk_up_c'], 'L0_attn_Wk_up_e': _L0_attn_in['Wk_up_e'], 'L0_attn_Wv_up': _L0_attn_in['Wv_up'], 'L0_attn_Wc': _L0_attn_in['Wc'], 'L0_ffn_Wr': _L0_ffn_in['Wr'], 'L0_ffn_br': _L0_ffn_in['br'], 'L0_ffn_W1': _L0_ffn_in['W1'], 'L0_ffn_b1': _L0_ffn_in['b1'], 'L0_ffn_W2': _L0_ffn_in['W2'], 'L0_ffn_b2': _L0_ffn_in['b2']}
    _x0 = _d['L0_attn_x']
    _d['L0_attn_x'] = jax.random.normal(jax.random.fold_in(jax.random.key(seed), 1), (4, 2048, 256), dtype=_x0.dtype)
    del _x0
    return _d

def reference(L0_attn_x, L0_attn_Wq_down, L0_attn_Wk_down, L0_attn_Wv_down, L0_attn_Wq_up_c, L0_attn_Wq_up_e, L0_attn_Wk_up_c, L0_attn_Wk_up_e, L0_attn_Wv_up, L0_attn_Wc, L0_ffn_Wr, L0_ffn_br, L0_ffn_W1, L0_ffn_b1, L0_ffn_W2, L0_ffn_b2):

    def _L0_attn_ref(x, Wq_down, Wk_down, Wv_down, Wq_up_c, Wq_up_e, Wk_up_c, Wk_up_e, Wv_up, Wc):
        import jax, jax.numpy as jnp
        import numpy as np
        import math
        B, T, C = (2, 512, 256)
        H, L = (16, 64)
        DH = C // H
        DHE = DH // 2
        THETA = 10000.0

        def _rope_cache(t, dim):
            inv_freq = 1.0 / THETA ** (jnp.arange(0, dim, 2, dtype=jnp.float32) / dim)
            freqs = jnp.arange(t, dtype=jnp.float32)[:, None] * inv_freq[None, :]
            emb = jnp.concatenate((freqs, freqs), axis=-1)
            return (jnp.cos(emb), jnp.sin(emb))

        def _apply_rope(x, cos, sin):
            x1 = x[..., 0::2]
            x2 = x[..., 1::2]
            rot = jnp.stack((-x2, x1), axis=-1).reshape(x.shape)
            return x * cos[None, None] + rot * sin[None, None]
        b, t, c = x.shape
        q_lat = (x @ Wq_down).reshape(b, t, H, L)
        k_lat = (x @ Wk_down).reshape(b, t, H, L)
        v_lat = (x @ Wv_down).reshape(b, t, H, L)
        q_c = jnp.einsum('bthl,ld->bhtd', q_lat, Wq_up_c)
        q_e = jnp.einsum('bthl,ld->bhtd', q_lat, Wq_up_e)
        k_c = jnp.einsum('bthl,ld->bhtd', k_lat, Wk_up_c)
        k_e = jnp.einsum('bthl,ld->bhtd', k_lat, Wk_up_e)
        v = jnp.einsum('bthl,ld->bhtd', v_lat, Wv_up)
        cos, sin = _rope_cache(t, DHE)
        q = jnp.concatenate([q_c, _apply_rope(q_e, cos, sin)], axis=-1)
        k = jnp.concatenate([k_c, _apply_rope(k_e, cos, sin)], axis=-1)
        scale = 1.0 / math.sqrt(DH)
        scores = jnp.einsum('bhqd,bhkd->bhqk', q, k) * scale
        causal = jnp.tril(jnp.ones((t, t), dtype=bool))
        scores = jnp.where(causal[None, None], scores, -jnp.inf)
        att = jax.nn.softmax(scores, axis=-1)
        y = jnp.einsum('bhqk,bhkd->bhqd', att, v)
        y = y.transpose(0, 2, 1, 3).reshape(b, t, c)
        return y @ Wc

    def _L0_ffn_ref(x, Wr, br, W1, b1, W2, b2):
        import jax, jax.numpy as jnp
        import numpy as np
        HIDDEN = 256
        NUM_EXPERTS = 8
        TOP_K = 2
        B, S = (4, 256)
        B_, S_, H = x.shape
        xf = x.reshape(-1, H)
        logits = xf @ Wr + br
        topk_w, topk_idx = jax.lax.top_k(logits, TOP_K)
        topk_w = jax.nn.softmax(topk_w, axis=-1)
        gate = jnp.sum(jax.nn.one_hot(topk_idx, NUM_EXPERTS, dtype=xf.dtype) * topk_w[..., None], axis=1)
        h = jax.nn.relu(jnp.einsum('th,ehf->etf', xf, W1) + b1[:, None, :])
        y = jnp.einsum('etf,efh->eth', h, W2) + b2[:, None, :]
        out = jnp.einsum('te,eth->th', gate, y)
        return out.reshape(B_, S_, H)
    x = L0_attn_x
    x = x + _L0_attn_ref(_layernorm(x, axis=-1), L0_attn_Wq_down, L0_attn_Wk_down, L0_attn_Wv_down, L0_attn_Wq_up_c, L0_attn_Wq_up_e, L0_attn_Wk_up_c, L0_attn_Wk_up_e, L0_attn_Wv_up, L0_attn_Wc)
    x = x + _L0_ffn_ref(_layernorm(x, axis=-1), L0_ffn_Wr, L0_ffn_br, L0_ffn_W1, L0_ffn_b1, L0_ffn_W2, L0_ffn_b2)
    return x

_drawn_inputs = setup_inputs


def setup_inputs(seed=0):
    import zlib

    import numpy as np

    out = dict(_drawn_inputs(seed))
    spreads = {}
    factors = {'L0_attn_Wq_down': 8.0,
     'L0_attn_Wk_down': 8.0,
     'L0_attn_Wv_down': 8.0,
     'L0_attn_Wq_up_c': 8.0,
     'L0_attn_Wq_up_e': 8.0,
     'L0_attn_Wk_up_c': 8.0,
     'L0_attn_Wk_up_e': 8.0,
     'L0_attn_Wv_up': 8.0,
     'L0_attn_Wc': 8.0,
     'L0_ffn_b1': 39.026,
     'L0_ffn_b2': 21.235,
     'L0_ffn_br': 8.0,
     'L0_ffn_W1': 2.785}
    for name, (base, spread) in spreads.items():
        noise = np.random.default_rng([zlib.crc32(name.encode()), seed]).standard_normal(out[name].shape)
        drawn = base * np.exp(spread * noise) if base else spread * noise
        out[name] = jnp.asarray(drawn.astype(out[name].dtype))
    for name, factor in factors.items():
        out[name] = (out[name] * factor).astype(out[name].dtype)
    return out
```

```python
from contextlib import ExitStack

import concourse.bass as bass
from concourse import mybir

P = 128
B, T, C = 4, 2048, 256
H, L, DH = 16, 64, 16
DHE = DH // 2
E, F = 8, 512
EPS = 1e-5
TB = 512
TILES = TB // P
CH = T // TB
NB = B * CH
QT = T // P
CC = C // P
HP = H // 2
GH = 4
HG = H // GH
NG = B * HG
VW = DH + 1
PARTS = 3

PRIMED = 1

ALU = mybir.AluOpType
ACT = mybir.ActivationFunctionType
AX = mybir.AxisListType
F32 = mybir.dt.float32
F32R = mybir.dt.float32r
BF16 = mybir.dt.bfloat16
I32 = mybir.dt.int32
RSQRT_MAGIC = float(0x5F3759DF)


class Steps:

    def __init__(self, engine, sem, base=0):
        self.engine, self.sem, self.base, self.n = engine, sem, base, 0

    def done(self, instruction):
        instruction.then_inc(self.sem, 1)
        self.n += 1
        self.engine.wait_ge(self.sem, self.base + self.n)


def layer_norm_stats(nc, steps, x, stats, mv, var, rstd, tmp, alone):
    for j in range(TILES):
        last = nc.vector.bn_stats(stats[:, j, :], x[:, j, :])
    steps.done(last)
    steps.engine.sem_inc(alone, 1)
    for j in range(TILES):
        last = nc.vector.bn_aggr(mv[:, j, :], stats[:, j, :])
    steps.done(last)
    steps.done(nc.vector.tensor_scalar(var[:, :], mv[:, :, 1], EPS, None, ALU.add))
    steps.done(nc.vector.tensor_scalar(tmp[:, :].bitcast(I32), var[:, :].bitcast(I32), 1, None,
                                       ALU.logical_shift_right))
    steps.done(nc.vector.tensor_scalar(rstd[:, :].bitcast(I32), tmp[:, :].bitcast(I32), -1.0, RSQRT_MAGIC,
                                       ALU.mult, ALU.add))
    for _ in range(3):
        steps.done(nc.vector.tensor_tensor(tmp[:, :], rstd[:, :], rstd[:, :], ALU.mult))
        steps.done(nc.vector.scalar_tensor_tensor(out=tmp[:, :], in0=tmp[:, :], scalar=-0.5, in1=var[:, :],
                                                  op0=ALU.mult, op1=ALU.mult))
        steps.done(nc.vector.scalar_tensor_tensor(out=rstd[:, :], in0=tmp[:, :], scalar=1.5, in1=rstd[:, :],
                                                  op0=ALU.add, op1=ALU.mult))


LN_STEPS = 5 + 9


def three_products(nc, out, stationary, moving, first, last):
    (s_hi, s_lo), (m_hi, m_lo) = stationary, moving
    nc.tensor.matmul(out, s_lo, m_hi, start=first, stop=False, skip_group_check=True)
    nc.tensor.matmul(out, s_hi, m_lo, start=False, stop=False, skip_group_check=True)
    return nc.tensor.matmul(out, s_hi, m_hi, start=False, stop=last, skip_group_check=True)


def make_identity(nc, eng, ident, sem):
    nc.gpsimd.memset(ident[:, :], 0.0).then_inc(sem, 1)
    eng.wait_ge(sem, 1)
    nc.gpsimd.affine_select(out=ident[:, :], in_=ident[:, :], compare_op=ALU.not_equal, fill=1.0, base=0,
                            pattern=[[-1, P]], channel_multiplier=1).then_inc(sem, 1)


def project(nc, x, downs, ups, rope_cos, rope_sin, parts_dram, v_dram):
    NDOWN = 3
    with ExitStack() as ctx:
        def sb(name, shape, dt):
            return ctx.enter_context(nc.sbuf_tensor(name, shape, dt))

        def sem(name):
            return ctx.enter_context(nc.semaphore(name))

        def bank(name):
            return ctx.enter_context(nc.psum_tensor(name, [P, 512], F32))

        ident = sb("ident1", [P, P], F32)
        down = sb("down", [P, NDOWN, CC, H * L], F32)
        down_t = sb("down_t", [P, NDOWN, HP, C], F32)
        up = sb("up", [P, 2, 2, 2, DHE], F32)
        up_v = sb("up_v", [P, 2, DH], F32)
        w_hi = sb("w_hi", [P, NDOWN, CC, C], F32R)
        w_lo = sb("w_lo", [P, NDOWN, CC, C], F32R)
        cos = sb("cos", [P, T], F32)
        sin = sb("sin", [P, T], F32)
        xin = sb("xin", [P, 2, TILES, C], F32)
        xn = sb("xn", [P, 2, TILES, C], F32)
        stats = sb("stats", [P, TILES, 6], F32)
        mv = sb("mv", [P, TILES, 2], F32)
        var = sb("var", [P, TILES], F32)
        rstd = sb("rstd", [P, TILES], F32)
        tmp = sb("tmp", [P, TILES], F32)
        xt_hi = sb("xt_hi", [P, 2, CC, TB], F32R)
        xt_lo = sb("xt_lo", [P, 2, CC, TB], F32R)
        raw = sb("raw", [P, 2, TB], F32)
        swapped = sb("swapped", [P, 2, TB], F32)
        turned = sb("turned", [P, 2, TB], F32)
        rest = sb("rest", [P, 4, TB], F32)
        parts = sb("parts", [P, 2, 4, PARTS, TB], BF16)
        v_out = sb("v_out", [P, 2, HG, TILES, GH, VW], F32)

        ps_t = [bank(f"ps_t{i}") for i in range(CC)]
        ps_p = [bank(f"ps_p{i}") for i in range(4)]
        ps_v = [bank(f"ps_v{i}") for i in range(2)]

        ident_made = sem("ident_made")
        up_clear = sem("up_clear")
        ups_in = sem("ups_in")
        downs_in = sem("downs_in")
        rope_in = sem("rope_in")
        down_turned = sem("down_turned")
        down_copied = sem("down_copied")
        folded = sem("folded")
        w_hi_made = sem("w_hi_made")
        w_made = sem("w_made")
        ones_set = sem("ones_set")
        x_in = [sem(f"x_in{u}") for u in range(2)]
        dve_step = sem("dve_step1")
        dve_alone = sem("dve_alone1")
        pool_alone = sem("pool_alone1")
        xn_made = sem("xn_made1")
        xt_turned = sem("xt_turned1")
        xt_hi_made = sem("xt_hi_made1")
        xt_lo_made = sem("xt_lo_made1")
        projected = sem("projected")
        v_projected = sem("v_projected")
        raw_copied = sem("raw_copied")
        part1_made = sem("part1_made")
        plain_rest = sem("plain_rest")
        part2_made = sem("part2_made")
        part3_made = sem("part3_made")
        swap_made = sem("swap_made")
        sine_made = sem("sine_made")
        raw_read = sem("raw_read")
        turned_made = sem("turned_made")
        v_copied = sem("v_copied")
        parts_out = [sem(f"parts_out{u}") for u in range(2)]
        v_stored = [sem(f"v_stored{u}") for u in range(2)]

        x_v = x.rearrange("b (c j p) d -> (b c) p j d", p=P, j=TILES)
        PROJ = [(0, 0), (1, 0), (0, 1), (1, 1)]

        block = ctx.enter_context(nc.Block())

        @block.sync
        def _(sp):
            for u in range(2):
                sp.sem_inc(parts_out[u], 16 * PRIMED)
                sp.sem_inc(v_stored[u], 16 * PRIMED)
            for m in range(NDOWN):
                sp.dma_start(down[:, m, :, :], downs[m].rearrange("(a p) n -> p a n", p=P)).then_inc(downs_in, 16)
            sp.wait_ge(up_clear, 2)
            for m, halves in enumerate(ups):
                for half, w in enumerate(halves):
                    for h2 in range(2):
                        rows = slice(h2 * L, (h2 + 1) * L)
                        to = up[rows, m, half, h2, :] if m < 2 else up_v[rows, h2, :]
                        sp.dma_start(to, w).then_inc(ups_in, 16)

            def load_x(n, u):
                sp.dma_start(xin[:, u, :, :], x_v[n, :, :, :]).then_inc(x_in[u], 16)

            def store(n, u):
                sp.wait_ge(part3_made, 4 * n + 4 + PRIMED)
                for i, (t, half) in enumerate(PROJ):
                    to = parts_dram[t, :, half, :, :, bass.ds(n * TB, TB)]
                    sp.dma_start(to.rearrange("s j h n -> (j h) s n"),
                                 parts[:, u, i, :, :]).then_inc(parts_out[u], 16)
                sp.wait_ge(v_copied, 2 * n + 2 + PRIMED)
                sp.dma_start(v_dram[:, :, bass.ds(n * TILES, TILES), :, :].rearrange("a p j h d -> p a (j h d)"),
                             v_out[:, u, :, :, :, :].rearrange("p a j h d -> p a (j h d)")).then_inc(v_stored[u], 16)

            for u in range(2):
                load_x(u, u)
            with sp.Fori(0, NB // 2 - 1) as k:
                for u in range(2):
                    store(2 * k + u, u)
                    sp.wait_ge(xn_made, 2 * k + u + 1)
                    load_x(2 * k + 2 + u, u)
            for u in range(2):
                store(NB - 2 + u, u)
            for u in range(2):
                sp.wait_ge(parts_out[u], NB // 2 * 4 * 16 + 16 * PRIMED)
                sp.wait_ge(v_stored[u], NB // 2 * 16 + 16 * PRIMED)

        @block.gpsimd
        def _(pool):
            pool.sem_inc(part3_made, PRIMED)
            nc.gpsimd.memset(up[:, :, :, :, :], 0.0).then_inc(up_clear, 1)
            nc.gpsimd.memset(up_v[:, :, :], 0.0).then_inc(up_clear, 1)
            make_identity(nc, pool, ident, ident_made)
            nc.gpsimd.memset(v_out[:, :, :, :, :, :], 1.0).then_inc(ones_set, 1)
            for table, src in ((cos, rope_cos), (sin, rope_sin)):
                pool.dma_start(table[:, :], src).then_inc(rope_in, 16)
            pool.wait_ge(rope_in, 2 * 16)
            with pool.Fori(0, B) as b:
                with pool.Fori(0, CH // 2) as c2:
                    for u in range(2):
                        n = (b * (CH // 2) + c2) * 2 + u
                        for i in range(2):
                            pool.wait_ge(swap_made, 2 * n + i + 1)
                            pool.sem_inc(pool_alone, 1)
                            nc.gpsimd.tensor_tensor(out=swapped[:, i, :], in0=swapped[:, i, :],
                                                    in1=sin[:, bass.ds((c2 * 2 + u) * TB, TB)],
                                                    op=ALU.mult).then_inc(sine_made, 1)
                        for i in range(4):
                            pool.wait_ge(part2_made, 4 * n + i + 1)
                            if i == 0:
                                pool.wait_ge(parts_out[u], (b * (CH // 2) + c2) * (4 * 16) + 16 * PRIMED)
                            nc.gpsimd.tensor_tensor(out=parts[:, u, i, 2, :], in0=rest[:, i, :],
                                                    in1=parts[:, u, i, 1, :],
                                                    op=ALU.subtract).then_inc(part3_made, 1)

        @block.scalar
        def _(act):
            act.sem_inc(raw_copied, PRIMED)
            act.sem_inc(v_copied, PRIMED)
            for g in range(NDOWN * 4):
                act.wait_ge(down_turned, g + 1)
                nc.scalar.copy(down_t[:, g // 4, 2 * (g % 4):2 * (g % 4) + 2, :].rearrange("p a n -> p (a n)"),
                               ps_p[g % 4][:, :]).then_inc(down_copied, 1)
            for m in range(NDOWN):
                act.wait_ge(folded, m + 1)
                nc.scalar.copy(w_hi[:, m, :, :].rearrange("p a n -> p (a n)"), ps_p[m][:, :]).then_inc(w_hi_made, 1)
            act.wait_ge(ones_set, 1)
            with act.Fori(0, NB // 2) as k:
                for u in range(2):
                    n = 2 * k + u
                    for a in range(CC):
                        act.wait_ge(xt_turned, CC * n + a + 1 + PRIMED)
                        nc.scalar.copy(xt_hi[:, u, a, :], ps_t[a][:, :]).then_inc(xt_hi_made, 1)
                    act.wait_ge(parts_out[u], k * (4 * 16) + 16 * PRIMED)
                    act.wait_ge(v_stored[u], k * 16 + 16 * PRIMED)
                    for i in range(2):
                        act.wait_ge(projected, 4 * n + i + 1)
                        nc.scalar.copy(parts[:, u, i, 0, :], ps_p[i][:, :]).then_inc(part1_made, 1)
                    act.wait_ge(raw_read, 2 * n + PRIMED)
                    for i in range(2):
                        act.wait_ge(projected, 4 * n + i + 3)
                        nc.scalar.copy(raw[:, i, :], ps_p[2 + i][:, :]).then_inc(raw_copied, 1)
                    for j in range(2):
                        act.wait_ge(v_projected, 2 * n + j + 1)
                        for s in range(2):
                            last = nc.scalar.copy(
                                v_out[:, u, :, 2 * j + s, :, 0:DH],
                                ps_v[j][:, s * C:(s + 1) * C].rearrange("p (a h d) -> p a h d", a=HG, h=GH))
                        last.then_inc(v_copied, 1)
                    for i in range(2):
                        act.wait_ge(turned_made, 2 * n + i + 1)
                        nc.scalar.copy(parts[:, u, 2 + i, 0, :], turned[:, i, :]).then_inc(part1_made, 1)

        @block.vector
        def _(dve):
            for s in (raw_read, plain_rest, xt_lo_made):
                dve.sem_inc(s, PRIMED)
            for m in range(NDOWN):
                dve.wait_ge(w_hi_made, m + 1)
                nc.vector.tensor_tensor(out=w_lo[:, m, :, :].rearrange("p a n -> p (a n)"), in0=ps_p[m][:, :],
                                        in1=w_hi[:, m, :, :].bitcast(F32).rearrange("p a n -> p (a n)"),
                                        op=ALU.subtract).then_inc(w_made, 1)
            dve.wait_ge(rope_in, 2 * 16)
            STEPS = LN_STEPS + 2
            with dve.Fori(0, B) as b:
                with dve.Fori(0, CH // 2) as c2:
                    for u in range(2):
                        k = b * (CH // 2) + c2
                        n = 2 * k + u
                        steps = Steps(dve, dve_step, n * STEPS)
                        dve.wait_ge(x_in[u], 16 * k + 16)
                        layer_norm_stats(nc, steps, xin[:, u, :, :], stats, mv, var, rstd, tmp, dve_alone)
                        dve.wait_ge(xt_turned, CC * n + PRIMED)
                        for j in range(TILES):
                            last = nc.vector.tensor_scalar(xn[:, u, j, :], xin[:, u, j, :], mv[:, j, 0:1],
                                                           rstd[:, j:j + 1], ALU.subtract, ALU.mult)
                        last.then_inc(xn_made, 1)
                        for a in range(CC):
                            dve.wait_ge(xt_hi_made, CC * n + a + 1)
                            nc.vector.tensor_tensor(out=xt_lo[:, u, a, :], in0=ps_t[a][:, :],
                                                    in1=xt_hi[:, u, a, :].bitcast(F32),
                                                    op=ALU.subtract).then_inc(xt_lo_made, 1)
                        dve.wait_ge(part3_made, 4 * n + PRIMED)
                        for i in range(2):
                            dve.wait_ge(part1_made, 4 * n + i + 1)
                            last = nc.vector.tensor_tensor(out=rest[:, i, :], in0=ps_p[i][:, :],
                                                           in1=parts[:, u, i, 0, :], op=ALU.subtract)
                            last.then_inc(plain_rest, 1)
                            dve.wait_ge(plain_rest, 2 * n + i + 1 + PRIMED)
                            nc.vector.tensor_copy(parts[:, u, i, 1, :], rest[:, i, :]).then_inc(part2_made, 1)
                        for i in range(2):
                            dve.wait_ge(raw_copied, 2 * n + i + 1 + PRIMED)
                            dve.sem_inc(dve_alone, 1)
                            nc.vector.stream_shuffle(swapped[:, i, :], raw[:, i, :],
                                                     [j ^ H for j in range(32)]).then_inc(swap_made, 1)
                            nc.vector.tensor_tensor(out=turned[:, i, :], in0=raw[:, i, :],
                                                    in1=cos[:, bass.ds((c2 * 2 + u) * TB, TB)],
                                                    op=ALU.mult).then_inc(raw_read, 1)
                        for i in range(2):
                            dve.wait_ge(raw_read, 2 * n + i + 1 + PRIMED)
                            dve.wait_ge(sine_made, 2 * n + i + 1)
                            nc.vector.tensor_tensor(out=turned[:, i, :], in0=turned[:, i, :],
                                                    in1=swapped[:, i, :], op=ALU.add).then_inc(turned_made, 1)
                        for i in range(2):
                            dve.wait_ge(part1_made, 4 * n + i + 3)
                            steps.done(nc.vector.tensor_tensor(out=rest[:, 2 + i, :], in0=turned[:, i, :],
                                                               in1=parts[:, u, 2 + i, 0, :], op=ALU.subtract))
                            nc.vector.tensor_copy(parts[:, u, 2 + i, 1, :],
                                                  rest[:, 2 + i, :]).then_inc(part2_made, 1)
                        assert steps.n == STEPS

        @block.tensor
        def _(pe):
            pe.sem_inc(xt_turned, PRIMED)
            pe.wait_ge(ident_made, 2)
            pe.wait_ge(downs_in, NDOWN * 16)
            for g in range(NDOWN * 4):
                if g >= 4:
                    pe.wait_ge(down_copied, g - 3)
                for s in range(2):
                    pair = 2 * (g % 4) + s
                    for a in range(CC):
                        at = s * C + a * P
                        last = nc.tensor.transpose(ps_p[g % 4][:, at:at + P],
                                                   down[:, g // 4, a, pair * P:(pair + 1) * P], ident[:, :])
                last.then_inc(down_turned, 1)
            pe.wait_ge(down_copied, NDOWN * 4)
            pe.wait_ge(ups_in, 5 * 2 * 16)
            for m in range(NDOWN):
                for a in range(CC):
                    for pair in range(HP):
                        to = ps_p[m][:, a * C:(a + 1) * C]
                        if m < 2:
                            to = to.rearrange("p (f j h) -> p f j h", f=2, j=DHE)[:, :, :, 2 * pair:2 * pair + 2]
                        else:
                            to = to[:, pair * 2 * DH:(pair + 1) * 2 * DH]
                        last = nc.tensor.matmul(to, down_t[:, m, pair, a * P:(a + 1) * P],
                                                up[:, m, :, :, :].rearrange("p f h j -> p f j h") if m < 2 else
                                                up_v[:, :, :].rearrange("p h d -> p (h d)"),
                                                start=(a == 0 and pair == 0), stop=(a == 1 and pair == HP - 1),
                                                skip_group_check=True)
                last.then_inc(folded, 1)
            pe.wait_ge(w_made, NDOWN)
            with pe.Fori(0, NB // 2) as k:
                for u in range(2):
                    n = 2 * k + u
                    pe.wait_ge(xn_made, n + 1)
                    pe.wait_ge(xt_lo_made, CC * n + PRIMED)
                    for a in range(CC):
                        for j in range(TILES):
                            last = nc.tensor.transpose(ps_t[a][:, j * P:(j + 1) * P],
                                                       xn[:, u, j, a * P:(a + 1) * P], ident[:, :])
                        last.then_inc(xt_turned, 1)
                    pe.wait_ge(xt_lo_made, CC * n + CC + PRIMED)
                    for i, (m, half) in enumerate(PROJ):
                        pe.wait_ge(plain_rest if i < 2 else raw_copied, 2 * n + PRIMED)
                        for a in range(CC):
                            cols = slice(half * P, (half + 1) * P)
                            last = three_products(nc, ps_p[i][:, :],
                                                  (w_hi[:, m, a, cols], w_lo[:, m, a, cols]),
                                                  (xt_hi[:, u, a, :], xt_lo[:, u, a, :]), a == 0, a == CC - 1)
                        last.then_inc(projected, 1)
                    pe.wait_ge(v_copied, 2 * n + PRIMED)
                    for j in range(TILES):
                        for a in range(CC):
                            cols = slice(j * P, (j + 1) * P)
                            last = three_products(nc, ps_v[j // 2][:, (j % 2) * C:(j % 2 + 1) * C],
                                                  (xt_hi[:, u, a, cols], xt_lo[:, u, a, cols]),
                                                  (w_hi[:, 2, a, :], w_lo[:, 2, a, :]),
                                                  a == 0 and j % 2 == 0, a == CC - 1)
                        if j % 2:
                            last.then_inc(v_projected, 1)


STACK = 6 * DH
ROWS = STACK + PARTS
EARLY = 12
NEG = -3.0e38


def attention_plan():
    steps = [(c, kt) for c in range(CH) for kt in range((c + 1) * TILES)]

    def pieces(tiles):
        return [("max", late, h, qt, kc) for qt in tiles for h in range(GH) for kc in range(qt // TILES + 1)
                for late in (tiles.start > 0,)]

    def width(e):
        _, _, _, qt, kc = e
        return TB if kc < qt // TILES else (qt % TILES + 1) * P

    late, early = pieces(range(EARLY, QT)), pieces(range(EARLY))
    maxes = late + [("chain", True)] + early[:6] + [("turn_max", True)] + early[6:] + [
        ("chain", False), ("turn_max", False)]
    total = sum(width(e) for e in maxes if e[0] == "max")
    work = [sum(TB - max(0, kt - c * TILES) * P for c, kt in steps[:s + 1]) for s in range(len(steps))]
    plan, at, spent = [], 0, 0
    for s, (c, kt) in enumerate(steps):
        plan.append(("scores", s))
        if s:
            plan.append(("sum", s - 1))
        if s > 1 and steps[s - 2][1] == (steps[s - 2][0] + 1) * TILES - 1:
            plan.append(("turn_out", steps[s - 2][0]))
        while at < len(maxes) and (spent < total * work[s] / work[-1] / 0.97 or s == len(steps) - 1):
            plan.append(maxes[at])
            spent += width(maxes[at]) if maxes[at][0] == "max" else 0
            at += 1
    plan += [("sum", len(steps) - 1), ("turn_out", CH - 1)]
    return steps, plan, early, width


def attend(nc, parts_dram, v_dram, minus_dram, y_dram):
    STEPS, PLAN, EARLY_PIECES, width = attention_plan()
    NSTEP = len(STEPS)
    NITEM = 2 * NSTEP
    NRING = sum(e[0] in ("max", "turn_max") for e in PLAN)
    NHEAD = len(EARLY_PIECES) + 1
    NDIAG = 2 * QT
    assert NRING % 2 == 0 and NSTEP % 4 == 0
    RING0 = NHEAD
    CHAIN_STEPS = 4
    LOADS = 10

    with ExitStack() as ctx:
        def sb(name, shape, dt):
            return ctx.enter_context(nc.sbuf_tensor(name, shape, dt))

        def sem(name):
            return ctx.enter_context(nc.semaphore(name))

        q_st = sb("q_st", [ROWS, 2, GH, T], BF16)
        k_st = sb("k_st", [ROWS, 2, GH, T], BF16)
        v_sb = sb("v_sb", [P, 2, QT, GH, VW], F32)
        prob = sb("prob", [P, 4, GH, TB], F32)
        out_sb = sb("out_sb", [P, 2, TB], F32)
        y_sb = sb("y_sb", [P, 2, TILES, GH, DH], F32)
        rec = sb("rec", [P, 2, TILES, GH], F32)
        ident = sb("ident2", [P, P], F32)
        ident_bf = sb("ident_bf", [P, P], BF16)
        causal = sb("causal", [P, TB], F32)
        junk = sb("junk", [P, 2, TB], F32)
        maxes = sb("maxes", [P, GH, QT, CH], F32)
        minus = sb("minus", [P, GH, EARLY], F32)
        left = sb("left", [P, GH, EARLY], F32)
        minus_parts = sb("minus_parts", [P, PARTS, GH * EARLY], BF16)
        minus_rows = sb("minus_rows", [GH * EARLY, PARTS, P], BF16)

        ps_s = [ctx.enter_context(nc.psum_tensor(f"ps_s{i}", [P, 2, 512], F32)) for i in range(2)]
        ps_m = [ctx.enter_context(nc.psum_tensor(f"ps_m{i}", [P, 512], F32)) for i in range(2)]
        ps_o = [ctx.enter_context(nc.psum_tensor(f"ps_o{i}", [P, 512], F32)) for i in range(2)]

        ident_made = sem("ident_made2")
        ident_bf_made = sem("ident_bf_made2")
        causal_made = sem("causal_made")
        ones_made = sem("ones_made")
        maxes_clear = sem("maxes_clear")
        banks_clear = sem("banks_clear")
        loaded = sem("loaded")
        scores_made = sem("scores_made")
        exp_made = sem("exp_made")
        masked = sem("masked")
        summed = sem("summed")
        out_copied = sem("out_copied")
        out_turned = sem("out_turned")
        y_made = sem("y_made")
        y_stored = [sem(f"y_stored{i}") for i in range(2)]
        rec_made = sem("rec_made")
        pe_alone = sem("pe_alone2")
        dve_alone = sem("dve_alone2")
        pool_alone = sem("pool_alone2")
        piece_made = sem("piece_made")
        piece_taken = sem("piece_taken")
        minus_made = sem("minus_made")
        rows_out = sem("rows_out")
        rows_in = sem("rows_in")
        dve_step = sem("dve_step2")

        block = ctx.enter_context(nc.Block())

        def windows(eng, body):
            with eng.Fori(0, NG // 2 - 1) as k:
                for u in range(2):
                    body(2 * k + u, u, False)
            for u in range(2):
                body(NG - 2 + u, u, u == 1)

        def plan_of(last):
            ring = 0
            for e in PLAN:
                if last and (e[0] == "max" and not e[1] or e[0] in ("chain", "turn_max") and not e[1]):
                    continue
                yield e, ring
                ring += e[0] in ("max", "turn_max")

        @block.sync
        def _(sp):
            for i in range(2):
                sp.sem_inc(y_stored[i], 16 * PRIMED)
            sp.sem_inc(rows_in, 16 * PRIMED)

            def load(g, u):
                b, hg = g // HG, g % HG
                at = 0
                for i in range(PARTS):
                    n = PARTS - i
                    q_rows, k_rows = (parts_dram[t, :, :, :, bass.ds(hg * GH, GH), bass.ds(b * T, T)]
                                      for t in range(2))
                    for _ in range(n):
                        sp.dma_start(q_st[at:at + DH, u, :, :],
                                     q_rows[i].rearrange("f j h n -> (f j) h n")).then_inc(loaded, 16)
                        at += DH
                    sp.dma_start(k_st[at - n * DH:at, u, :, :],
                                 k_rows[0:n].rearrange("s f j h n -> (s f j) h n")).then_inc(loaded, 16)
                sp.dma_start(v_sb[:, u, :, :, :].rearrange("p k h d -> p (k h d)"),
                             v_dram[hg, :, bass.ds(b * QT, QT), :, :].rearrange("p k h d -> p (k h d)")
                             ).then_inc(loaded, 16)

            def place_minus(u, late, number):
                lo, n = (EARLY, QT - EARLY) if late else (0, EARLY)
                sp.dma_start(minus_dram[late][:, :, :, :].rearrange("s h k n -> (h k) s n"),
                             minus_rows[0:GH * n, :, :]).then_inc(rows_out, 16)
                sp.wait_ge(rows_out, 16 * number)
                sp.dma_start(q_st[STACK:ROWS, u, :, lo * P:(lo + n) * P],
                             minus_dram[late][:, :, :, :].rearrange("s h k n -> s h (k n)")).then_inc(rows_in, 16)

            load(0, 0)
            sp.wait_ge(piece_taken, NHEAD + 2 * PRIMED)
            place_minus(0, False, 1)

            def body(w, u, last):
                if not last:
                    sp.wait_ge(summed, NSTEP * w + 4 * PRIMED)
                    load(w + 1, 1 - u)
                for e, ring in plan_of(last):
                    if e[0] == "turn_max":
                        sp.wait_ge(piece_taken, RING0 + NRING * w + ring + 1 + 2 * PRIMED)
                        place_minus(u if e[1] else 1 - u, e[1], 2 * w + (2 if e[1] else 3))
                    elif e[0] == "turn_out":
                        c = e[1]
                        sp.wait_ge(y_made, CH * w + c + 1 + 2 * PRIMED)
                        to = y_dram[bass.ds((w // HG) * T + c * TB, TB), bass.ds((w % HG) * (GH * DH), GH * DH)]
                        sp.dma_start(to.rearrange("(j p) n -> p j n", p=P),
                                     y_sb[:, c % 2, :, :, :].rearrange("p j h d -> p j (h d)")
                                     ).then_inc(y_stored[c % 2], 16)
            windows(sp, body)
            for i in range(2):
                sp.wait_ge(y_stored[i], 16 * (NG * CH // 2 + PRIMED))

        @block.gpsimd
        def _(pool):
            make_identity(nc, pool, ident, ident_made)
            nc.gpsimd.memset(maxes[:, :, :, :], NEG).then_inc(maxes_clear, 1)
            nc.gpsimd.memset(causal[:, :], 0.0).then_inc(causal_made, 1)
            pool.wait_ge(causal_made, 1)
            nc.gpsimd.affine_select(out=causal[:, TB - P:TB], in_=causal[:, TB - P:TB], compare_op=ALU.is_ge,
                                    fill=NEG, base=0, pattern=[[-1, P]],
                                    channel_multiplier=1).then_inc(causal_made, 1)

            def body(w, u, last):
                diag = 0
                for s, (c, kt) in enumerate(STEPS):
                    r = kt - c * TILES
                    if r < 0:
                        continue
                    for pair in range(2):
                        pool.wait_ge(exp_made, NITEM * w + 2 * s + pair + 1 + 2 * PRIMED)
                        pool.sem_inc(pool_alone, 1)
                        tile = prob[:, s % 4, 2 * pair:2 * pair + 2, r * P:(r + 1) * P]
                        nc.gpsimd.affine_select(out=tile, in_=tile, compare_op=ALU.is_ge, fill=0.0, base=0,
                                                pattern=[[0, 2], [1, P]],
                                                channel_multiplier=-1).then_inc(masked, 1)
                        diag += 1
                assert diag == NDIAG
            windows(pool, body)

        @block.scalar
        def _(act):
            act.sem_inc(exp_made, 2 * PRIMED)

            def copy_out(w, c):
                steps_in = sum(TILES * (i + 1) for i in range(c + 1))
                act.wait_ge(summed, NSTEP * w + steps_in + 4 * PRIMED)
                nc.scalar.copy(out_sb[:, c % 2, :], ps_o[c % 2][:, :]).then_inc(out_copied, 1)

            def body(w, u, last):
                for s, (c, kt) in enumerate(STEPS):
                    lo = max(0, kt - c * TILES) * P
                    act.wait_ge(summed, NSTEP * w + s + PRIMED)
                    for pair in range(2):
                        n = 2 * s + pair
                        act.wait_ge(scores_made, NITEM * w + n + 1)
                        nc.scalar.activation(prob[:, s % 4, 2 * pair:2 * pair + 2, lo:TB],
                                             ps_s[n % 2][:, :, lo:TB], ACT.Exp,
                                             scale=DH ** -0.5).then_inc(exp_made, 1)
                    if kt == 0 and c > 0:
                        copy_out(w, c - 1)
                copy_out(w, CH - 1)
            windows(act, body)

        @block.vector
        def _(dve):
            dve.sem_inc(piece_taken, 2 * PRIMED)
            dve.sem_inc(y_made, 2 * PRIMED)
            for bank in ps_o:
                nc.vector.memset(bank[:, :], 0.0).then_inc(banks_clear, 1)
            nc.vector.memset(k_st[STACK:ROWS, :, :, :], 1.0).then_inc(ones_made, 1)
            dve.wait_ge(ident_made, 2)
            nc.vector.tensor_copy(ident_bf[:, :], ident[:, :]).then_inc(ident_bf_made, 1)
            dve.wait_ge(causal_made, 2)
            dve.wait_ge(maxes_clear, 1)

            def take(e, parity):
                _, _, h, qt, kc = e
                w = width(e)
                to = maxes[:, h, qt, kc:kc + 1]
                bank = ps_m[parity]
                if kc < qt // TILES:
                    return nc.vector.tensor_reduce(to, bank[:, 0:w], AX.X, ALU.max)
                return nc.vector.tensor_tensor_reduce(junk[:, parity, 0:w], bank[:, 0:w], causal[:, TB - w:TB], 1.0, NEG,
                                                      ALU.add, ALU.max, to)

            def split_minus(steps, late):
                lo, n = (EARLY, QT - EARLY) if late else (0, EARLY)
                m, rest = minus[:, :, 0:n], left[:, :, 0:n]
                parts = [minus_parts[:, i, 0:GH * n].rearrange("p (h n) -> p h n", h=GH) for i in range(PARTS)]
                steps.done(nc.vector.tensor_reduce(m, maxes[:, :, lo:lo + n, :], AX.X, ALU.max, negate=True))
                steps.done(nc.vector.tensor_copy(parts[0], m))
                steps.done(nc.vector.tensor_tensor(out=rest, in0=m, in1=parts[0], op=ALU.subtract))
                steps.done(nc.vector.tensor_copy(parts[1], rest))
                nc.vector.tensor_tensor(out=parts[2], in0=rest, in1=parts[1], op=ALU.subtract).then_inc(minus_made, 1)

            def copy_minus(bank, late):
                n = QT - EARLY if late else EARLY
                src = bank[:, :].bitcast(BF16)[0:GH * n, 0:PARTS * P].rearrange("p (s n) -> p s n", s=PARTS)
                nc.vector.tensor_copy(minus_rows[0:GH * n, :, :], src).then_inc(piece_taken, 1)

            for i, e in enumerate(EARLY_PIECES):
                dve.wait_ge(piece_made, i + 1)
                take(e, i % 2).then_inc(piece_taken, 1)
            dve.wait_ge(piece_taken, len(EARLY_PIECES) + 2 * PRIMED)
            steps = Steps(dve, dve_step)
            split_minus(steps, False)
            dve.wait_ge(piece_made, NHEAD)
            copy_minus(ps_m[(NHEAD - 1) % 2], False)

            def body(w, u, last):
                steps = Steps(dve, dve_step, CHAIN_STEPS + 2 * CHAIN_STEPS * w)
                for e, ring in plan_of(last):
                    n = RING0 + NRING * w + ring
                    bank = ps_m[(RING0 + ring) % 2]
                    if e[0] == "max":
                        dve.wait_ge(piece_made, n + 1)
                        if e[4] == e[3] // TILES:
                            dve.sem_inc(dve_alone, 1)
                        take(e, (RING0 + ring) % 2).then_inc(piece_taken, 1)
                    elif e[0] == "chain":
                        dve.wait_ge(piece_taken, n + 2 * PRIMED)
                        split_minus(steps, e[1])
                    elif e[0] == "turn_max":
                        dve.wait_ge(piece_made, n + 1)
                        k = 2 * w + (1 if e[1] else 2)
                        dve.wait_ge(rows_in, 16 * k + 16 * PRIMED)
                        copy_minus(bank, e[1])
                    elif e[0] == "turn_out":
                        c = e[1]
                        src = ps_o[c % 2][:, :].rearrange("p (j h d) -> p j h d", j=TILES, h=GH)
                        dve.wait_ge(out_turned, CH * w + c + 1)
                        nc.vector.reciprocal(rec[:, c % 2, :, :], src[:, :, :, DH]).then_inc(rec_made, 1)
                        dve.wait_ge(rec_made, CH * w + c + 1)
                        dve.wait_ge(y_stored[c % 2], 16 * (2 * w + c // 2) + 16 * PRIMED)
                        nc.vector.tensor_tensor(out=y_sb[:, c % 2, :, :, :], in0=src[:, :, :, 0:DH],
                                                in1=rec[:, c % 2, :, :].unsqueeze(3).broadcast_to([P, TILES, GH, DH]),
                                                op=ALU.mult).then_inc(y_made, 1)
            windows(dve, body)

        @block.tensor
        def _(pe):
            pe.sem_inc(summed, 4 * PRIMED)
            pe.wait_ge(ident_bf_made, 1)
            pe.wait_ge(ones_made, 1)
            pe.wait_ge(banks_clear, 2)

            def piece(e, bank, u):
                _, _, h, qt, kc = e
                return nc.tensor.matmul(bank[:, 0:width(e)], q_st[0:STACK, u, h, qt * P:(qt + 1) * P],
                                        k_st[0:STACK, u, h, kc * TB:kc * TB + width(e)], start=True, stop=True)

            def turn_max(bank, late):
                n = GH * (QT - EARLY if late else EARLY)
                for part in range(PARTS):
                    last = nc.tensor.transpose(bank[:, :].bitcast(BF16)[0:n, part * P:(part + 1) * P],
                                               minus_parts[:, part, 0:n], ident_bf[:, :])
                return last

            pe.wait_ge(loaded, LOADS * 16)
            for i, e in enumerate(EARLY_PIECES):
                pe.wait_ge(piece_taken, i + 1)
                piece(e, ps_m[i % 2], 0).then_inc(piece_made, 1)
            pe.wait_ge(minus_made, 1)
            pe.wait_ge(piece_taken, NHEAD)
            turn_max(ps_m[(NHEAD - 1) % 2], False).then_inc(piece_made, 1)

            def body(w, u, last):
                pe.wait_ge(rows_in, 16 * (2 * w + 1) + 16 * PRIMED)
                ahead = False
                for e, ring in plan_of(last):
                    n = RING0 + NRING * w + ring
                    bank = ps_m[(RING0 + ring) % 2]
                    if e[0] == "scores":
                        s = e[1]
                        c, kt = STEPS[s]
                        lo = max(0, kt - c * TILES) * P
                        if c == EARLY // TILES and kt == 0:
                            pe.wait_ge(rows_in, 16 * (2 * w + 2) + 16 * PRIMED)
                        for pair in range(2):
                            i = 2 * s + pair
                            pe.wait_ge(exp_made, NITEM * w + i + 1)
                            for h2 in range(2):
                                h = 2 * pair + h2
                                mm = nc.tensor.matmul(ps_s[i % 2][:, h2, lo:TB], k_st[:, u, h, kt * P:(kt + 1) * P],
                                                      q_st[:, u, h, c * TB + lo:(c + 1) * TB], start=True, stop=True)
                            mm.then_inc(scores_made, 1)
                    elif e[0] == "sum":
                        s = e[1]
                        c, kt = STEPS[s]
                        r = kt - c * TILES
                        lo = max(0, r) * P
                        if kt == 0:
                            pe.wait_ge(y_made, CH * w + c + PRIMED)
                        pe.wait_ge(exp_made, NITEM * w + 2 * s + 2 + 2 * PRIMED)
                        if r >= 0:
                            pe.wait_ge(masked, NDIAG * w + 2 * (c * TILES + r) + 2)
                        for h in range(GH):
                            mm = nc.tensor.matmul(ps_o[c % 2][32 * h:32 * h + VW, lo:TB], v_sb[:, u, kt, h, :],
                                                  prob[:, s % 4, h, lo:TB], start=(kt == 0),
                                                  stop=(r == TILES - 1), skip_group_check=True)
                        mm.then_inc(summed, 1)
                    elif e[0] == "turn_out":
                        c = e[1]
                        pe.wait_ge(out_copied, CH * w + c + 1)
                        for j in range(TILES):
                            mm = nc.tensor.transpose(ps_o[c % 2][:, j * P:(j + 1) * P],
                                                     out_sb[:, c % 2, j * P:(j + 1) * P], ident[:, :])
                        mm.then_inc(out_turned, 1)
                    elif e[0] == "max":
                        if not e[1] and not ahead:
                            pe.wait_ge(loaded, LOADS * 16 * (w + 2))
                            ahead = True
                        pe.wait_ge(piece_taken, n + 1)
                        piece(e, bank, u if e[1] else 1 - u).then_inc(piece_made, 1)
                    elif e[0] == "turn_max":
                        pe.wait_ge(minus_made, 2 * w + (2 if e[1] else 3))
                        pe.wait_ge(piece_taken, n + 1)
                        pe.sem_inc(pe_alone, 1)
                        turn_max(bank, e[1]).then_inc(piece_made, 1)
            windows(pe, body)


WCH = 512
W_PER_LOOP = 2


def mix(nc, x, y_dram, wc, wr, br, w1, w2, w_sb, logits, xt_dram, x1_dram):
    w_hi, w_lo = w_sb
    with ExitStack() as ctx:
        def sb(name, shape, dt):
            return ctx.enter_context(nc.sbuf_tensor(name, shape, dt))

        def sem(name):
            return ctx.enter_context(nc.semaphore(name))

        def bank(name):
            return ctx.enter_context(nc.psum_tensor(name, [P, 512], F32))

        ident = sb("ident3", [P, P], F32)
        wc_sb = sb("wc_sb", [P, CC, C], F32)
        wr_sb = sb("wr_sb", [P, CC, E], F32)
        br_sb = sb("br_sb", [E, 1], F32)
        raw = sb("w_raw", [P, 2 * W_PER_LOOP, WCH], F32)
        y_in = sb("y_in", [P, 2, TILES, C], F32)
        x_in = sb("x_in", [P, 2, TILES, C], F32)
        yt = sb("yt", [P, 1, CC, TB], F32)
        stats = sb("stats3", [P, TILES, 6], F32)
        mv = sb("mv3", [P, TILES, 2], F32)
        var = sb("var3", [P, TILES], F32)
        rstd = sb("rstd3", [P, TILES], F32)
        tmp = sb("tmp3", [P, TILES], F32)
        xt = sb("xt", [P, 1, CC, TB], F32)
        xt_hi = sb("xt_hi3", [P, 1, CC, TB], F32R)
        xt_lo = sb("xt_lo3", [P, 1, CC, TB], F32R)
        by_expert = sb("by_expert", [E, TB], F32)

        ps_t = [bank(f"ps_yt{i}") for i in range(CC)]
        ps_x = [bank(f"ps_x{i}") for i in range(2)]
        ps_u = [bank(f"ps_u{i}") for i in range(CC)]
        ps_r = bank("ps_r")
        ps_l = bank("ps_l")

        ident_made = sem("ident_made3")
        weights_in = sem("weights_in3")
        y_loaded = [sem(f"y_loaded{u}") for u in range(2)]
        raw_in = sem("raw_in")
        w_hi_made = sem("w_hi_made3")
        w_lo_made = sem("w_lo_made3")
        y_turned = sem("y_turned")
        yt_made = sem("yt_made")
        mixed = sem("mixed")
        x1_made = sem("x1_made")
        dve_step = sem("dve_step3")
        dve_alone = sem("dve_alone3")
        sp_alone = sem("sp_alone3")
        pool_alone = sem("pool_alone3")
        pe_alone = sem("pe_alone3")
        xn_made = sem("xn_made3")
        xn_turned = sem("xn_turned")
        xt_made = sem("xt_made")
        xt_free = sem("xt_free")
        hi_made = sem("hi_made3")
        lo_made = sem("lo_made3")
        routed = sem("routed")
        by_expert_made = sem("by_expert_made")
        logits_turned = sem("logits_turned")
        logits_made = sem("logits_made")
        x1_stored = sem("x1_stored")
        xt_stored = sem("xt_stored")

        x_v = x.rearrange("b (c j p) d -> (b c) p j d", p=P, j=TILES)
        y_v = y_dram.rearrange("(n j p) d -> n p j d", p=P, j=TILES)
        x1_v = x1_dram.rearrange("(n j p) d -> n p j d", p=P, j=TILES)
        w1_v = w1.rearrange("e (a p) f -> (e a) p f", p=P)
        w2_v = w2.rearrange("e (a o p) c -> (e a) p o c", p=P, o=WCH // C)

        block = ctx.enter_context(nc.Block())

        @block.sync
        def _(sp):
            sp.sem_inc(x1_stored, 16 * PRIMED)
            sp.sem_inc(xt_stored, 32 * PRIMED)
            sp.dma_start(wc_sb[:, :, :], wc.rearrange("(a p) n -> p a n", p=P)).then_inc(weights_in, 16)
            sp.dma_start(wr_sb[:, :, :], wr.rearrange("(a p) n -> p a n", p=P)).then_inc(weights_in, 16)
            sp.dma_start(br_sb[:, :], br.rearrange("(e a) -> e a", a=1)).then_inc(weights_in, 16)

            def load(n, u):
                sp.dma_start(y_in[:, u, :, :], y_v[n, :, :, :]).then_inc(y_loaded[u], 16)
                sp.dma_start(x_in[:, u, :, :], x_v[n, :, :, :]).then_inc(y_loaded[u], 16)

            def load_weights(k):
                sp.wait_ge(w_lo_made, 2 * W_PER_LOOP * k + PRIMED)
                sp.sem_inc(sp_alone, 1)
                for i in range(W_PER_LOOP):
                    sp.dma_start(raw[:, i, :], w1_v[W_PER_LOOP * k + i, :, :]).then_inc(raw_in, 16)
                    sp.dma_start(raw[:, W_PER_LOOP + i, :].rearrange("p (o c) -> p o c", c=C),
                                 w2_v[W_PER_LOOP * k + i, :, :, :]).then_inc(raw_in, 16)

            def store(n, u):
                sp.wait_ge(x1_made, 2 * n + 2)
                sp.sem_inc(sp_alone, 1)
                sp.dma_start(x1_v[n, :, :, :], x_in[:, u, :, :]).then_inc(x1_stored, 16)
                sp.wait_ge(lo_made, CC * n + CC)
                sp.sem_inc(sp_alone, 1)
                sp.dma_start(xt_dram[0, n, :, :, :], xt_hi[:, 0, :, :].bitcast(F32)).then_inc(xt_stored, 16)
                sp.dma_start(xt_dram[1, n, :, :, :], xt_lo[:, 0, :, :].bitcast(F32)).then_inc(xt_stored, 16)

            for u in range(2):
                load(u, u)
            with sp.Fori(0, NB // 2 - 1) as k:
                load_weights(k)
                for u in range(2):
                    store(2 * k + u, u)
                    sp.wait_ge(x1_stored, 16 * (2 * k + u + 1) + 16 * PRIMED)
                    sp.sem_inc(sp_alone, 1)
                    sp.wait_ge(xn_turned, CC * (2 * k + u + 1))
                    sp.sem_inc(sp_alone, 1)
                    load(2 * k + 2 + u, u)
            load_weights(NB // 2 - 1)
            for u in range(2):
                store(NB - 2 + u, u)
            sp.wait_ge(x1_stored, 16 * (NB + PRIMED))
            sp.wait_ge(xt_stored, 32 * (NB + PRIMED))

        @block.gpsimd
        def _(pool):
            pool.sem_inc(w_lo_made, PRIMED)
            make_identity(nc, pool, ident, ident_made)
            with pool.Fori(0, NB // 2) as k:
                def split(i):
                    chunk = W_PER_LOOP * k + (i % W_PER_LOOP) + (i // W_PER_LOOP) * (NB // 2 * W_PER_LOOP)
                    pool.wait_ge(raw_in, 16 * 2 * W_PER_LOOP * (k + 1))
                    pool.sem_inc(pool_alone, 1)
                    nc.gpsimd.tensor_copy(w_hi[:, bass.ds(chunk, 1), :].rearrange("p a n -> p (a n)"),
                                          raw[:, i, :]).then_inc(w_hi_made, 1)
                    pool.wait_ge(w_hi_made, 2 * W_PER_LOOP * k + i + 1)
                    pool.sem_inc(pool_alone, 1)
                    nc.gpsimd.tensor_tensor(
                        out=w_lo[:, bass.ds(chunk, 1), :].rearrange("p a n -> p (a n)"), in0=raw[:, i, :],
                        in1=w_hi[:, bass.ds(chunk, 1), :].bitcast(F32).rearrange("p a n -> p (a n)"),
                        op=ALU.subtract).then_inc(w_lo_made, 1)

                for u in range(2):
                    n = 2 * k + u
                    for i in range(W_PER_LOOP):
                        split(W_PER_LOOP * u + i)
                    for a in range(CC):
                        pool.wait_ge(hi_made, CC * n + a + 1)
                        nc.gpsimd.tensor_tensor(out=xt_lo[:, 0, a, :], in0=xt[:, 0, a, :],
                                                in1=xt_hi[:, 0, a, :].bitcast(F32),
                                                op=ALU.subtract).then_inc(lo_made, 1)

        @block.scalar
        def _(act):
            act.wait_ge(weights_in, 3 * 16)
            with act.Fori(0, NB // 2) as k:
                for u in range(2):
                    n = 2 * k + u
                    for a in range(CC):
                        act.wait_ge(y_turned, CC * n + a + 1)
                        nc.scalar.copy(yt[:, 0, a, :], ps_t[a][:, :]).then_inc(yt_made, 1)
                    for a in range(CC):
                        act.wait_ge(xn_turned, CC * n + a + 1)
                        if a == 0:
                            act.wait_ge(xt_free, n + PRIMED)
                        nc.scalar.copy(xt[:, 0, a, :], ps_u[a][:, :]).then_inc(xt_made, 1)
                    act.wait_ge(routed, n + 1)
                    nc.scalar.activation(by_expert[:, :], ps_r[0:E, :], ACT.Identity,
                                         bias=br_sb[:, 0:1]).then_inc(by_expert_made, 1)

        @block.vector
        def _(dve):
            NSTEP = LN_STEPS
            dve.sem_inc(logits_made, PRIMED)
            dve.sem_inc(xt_free, PRIMED)
            with dve.Fori(0, NB // 2) as k:
                for u in range(2):
                    n = 2 * k + u
                    steps = Steps(dve, dve_step, n * NSTEP)
                    dve.wait_ge(y_loaded[u], 32 * (k + 1))
                    for i in range(2):
                        dve.wait_ge(mixed, 2 * n + i + 1)
                        part = x_in[:, u, 2 * i:2 * i + 2, :].rearrange("p j d -> p (j d)")
                        last = nc.vector.tensor_tensor(out=part, in0=ps_x[i][:, :], in1=part, op=ALU.add)
                        last.then_inc(x1_made, 1)
                    dve.wait_ge(x1_made, 2 * n + 2)
                    dve.sem_inc(dve_alone, 1)
                    layer_norm_stats(nc, steps, x_in[:, u, :, :], stats, mv, var, rstd, tmp, dve_alone)
                    for j in range(TILES):
                        last = nc.vector.tensor_scalar(y_in[:, u, j, :], x_in[:, u, j, :], mv[:, j, 0:1],
                                                       rstd[:, j:j + 1], ALU.subtract, ALU.mult)
                    last.then_inc(xn_made, 1)
                    dve.wait_ge(xt_stored, 32 * n + 32 * PRIMED)
                    for a in range(CC):
                        dve.wait_ge(xt_made, CC * n + a + 1)
                        nc.vector.tensor_copy(xt_hi[:, 0, a, :], xt[:, 0, a, :]).then_inc(hi_made, 1)
                    dve.wait_ge(logits_turned, n + 1)
                    nc.vector.tensor_copy(logits[:, bass.ds(n * TILES, TILES), :],
                                          ps_l[:, 0:TILES * E].rearrange("p (j e) -> p j e", e=E)
                                          ).then_inc(logits_made, 1)
                    dve.wait_ge(lo_made, CC * n + CC)
                    dve.sem_inc(xt_free, 1)

        @block.tensor
        def _(pe):
            pe.wait_ge(ident_made, 2)
            pe.wait_ge(weights_in, 3 * 16)
            with pe.Fori(0, NB // 2) as k:
                for u in range(2):
                    n = 2 * k + u
                    pe.wait_ge(y_loaded[u], 32 * (k + 1))
                    for a in range(CC):
                        for j in range(TILES):
                            last = nc.tensor.transpose(ps_t[a][:, j * P:(j + 1) * P],
                                                       y_in[:, u, j, a * P:(a + 1) * P], ident[:, :])
                        last.then_inc(y_turned, 1)
                    pe.wait_ge(yt_made, CC * n + CC)
                    for j in range(TILES):
                        for a in range(CC):
                            last = nc.tensor.matmul(ps_x[j // 2][:, (j % 2) * C:(j % 2 + 1) * C],
                                                    yt[:, 0, a, j * P:(j + 1) * P], wc_sb[:, a, :],
                                                    start=(j % 2 == 0 and a == 0), stop=(a == CC - 1),
                                                    skip_group_check=True)
                        if j % 2:
                            last.then_inc(mixed, 1)
                    pe.wait_ge(xn_made, n + 1)
                    for a in range(CC):
                        for j in range(TILES):
                            last = nc.tensor.transpose(ps_u[a][:, j * P:(j + 1) * P],
                                                       y_in[:, u, j, a * P:(a + 1) * P], ident[:, :])
                        last.then_inc(xn_turned, 1)
                    pe.wait_ge(xt_made, CC * n + CC)
                    for a in range(CC):
                        last = nc.tensor.matmul(ps_r[0:E, :], wr_sb[:, a, :], xt[:, 0, a, :],
                                                start=(a == 0), stop=(a == CC - 1))
                    last.then_inc(routed, 1)
                    pe.wait_ge(by_expert_made, n + 1)
                    pe.sem_inc(pe_alone, 1)
                    pe.wait_ge(logits_made, n + PRIMED)
                    pe.sem_inc(pe_alone, 1)
                    for j in range(TILES):
                        last = nc.tensor.transpose(ps_l[:, j * E:(j + 1) * E], by_expert[:, j * P:(j + 1) * P],
                                                   ident[0:E, 0:E])
                    last.then_inc(logits_turned, 1)


def experts(nc, w_sb, logits, b1, b2, xt_dram, x1_dram, out):
    w_hi, w_lo = w_sb
    FO = F // P
    HALF = NB // 2 * W_PER_LOOP
    with ExitStack() as ctx:
        def sb(name, shape, dt):
            return ctx.enter_context(nc.sbuf_tensor(name, shape, dt))

        def sem(name):
            return ctx.enter_context(nc.semaphore(name))

        b1_sb = sb("b1_sb", [P, E, FO], F32)
        b2_sb = sb("b2_sb", [P, E, C], F32)
        rank = sb("rank", [P, E], F32)
        hot = [sb(f"hot{i}", [P, NB * TILES, E], F32) for i in range(2)]
        score = sb("score", [P, NB * TILES, E], F32)
        rest = sb("rest4", [P, NB * TILES, E], F32)
        best = [sb(f"best{i}", [P, NB * TILES], F32) for i in range(2)]
        top = sb("top", [P, NB * TILES], F32)
        ratio = sb("ratio", [P, NB * TILES], F32)
        share = [sb(f"share{i}", [P, NB * TILES], F32) for i in range(2)]
        gates = sb("gates", [P, NB * TILES, E], F32)
        gate = sb("gate", [P, 2, TILES, E], F32)
        xt_hi = sb("xt_hi4", [P, 2, CC, TB], F32R)
        xt_lo = sb("xt_lo4", [P, 2, CC, TB], F32R)
        acc = sb("acc", [P, 2, TILES, C], F32)
        h = sb("h", [P, 2, TB], F32)
        h_hi = sb("h_hi", [P, 2, TB], F32R)
        h_lo = sb("h_lo", [P, 2, TB], F32R)
        ps_h = [ctx.enter_context(nc.psum_tensor(f"ps_h{i}", [P, 512], F32)) for i in range(2)]
        ps_y = [ctx.enter_context(nc.psum_tensor(f"ps_y{i}", [P, 512], F32)) for i in range(4)]

        biases_in = sem("biases_in")
        block_in = [sem(f"block_in{u}") for u in range(2)]
        rank_set = sem("rank_set")
        gate_step = sem("gate_step")
        distance_made = sem("distance_made")
        ratio_made = sem("ratio_made")
        gate_copied = sem("gate_copied")
        h_psum = sem("h_psum")
        h_made = sem("h_made")
        lo_made = sem("lo_made4")
        y_complete = sem("y_complete")
        acc_step = sem("acc_step")
        sp_alone = sem("sp_alone4")
        out_stored = [sem(f"out_stored{u}") for u in range(2)]

        out_v = out.rearrange("b (c j p) d -> (b c) p j d", p=P, j=TILES)
        x1_v = x1_dram.rearrange("(n j p) d -> n p j d", p=P, j=TILES)
        LAYERS = [(e, f) for e in range(E) for f in range(FO)]
        NL = len(LAYERS)
        GATHER = 2 * TILES
        ACCS = GATHER * E

        block = ctx.enter_context(nc.Block())

        @block.sync
        def _(sp):
            def load(n, u):
                sp.dma_start(xt_hi[:, u, :, :].bitcast(F32), xt_dram[0, n, :, :, :]).then_inc(block_in[u], 16)
                sp.dma_start(xt_lo[:, u, :, :].bitcast(F32), xt_dram[1, n, :, :, :]).then_inc(block_in[u], 16)
                sp.dma_start(acc[:, u, :, :], x1_v[n, :, :, :]).then_inc(block_in[u], 16)

            def store(n, u, k):
                sp.wait_ge(acc_step, ACCS * n + ACCS + 2 * GATHER)
                sp.sem_inc(sp_alone, 1)
                sp.dma_start(out_v[n, :, :, :], acc[:, u, :, :]).then_inc(out_stored[u], 16)

            load(0, 0)
            with nc.allow_non_contiguous_dma(reason="small biases, turned once"):
                sp.dma_start(b1_sb[:, :, :].rearrange("p e f -> p (e f)"),
                             b1.rearrange("e (f p) -> p (e f)", p=P)).then_inc(biases_in, 16)
            sp.dma_start(b2_sb[:, :, :].rearrange("p e c -> p (e c)"),
                         b2.rearrange("(a e) c -> a (e c)", a=1).broadcast_to([P, E * C])).then_inc(biases_in, 16)
            load(1, 1)
            with sp.Fori(0, NB // 2 - 1) as k:
                for u in range(2):
                    store(2 * k + u, u, k)
                    sp.wait_ge(out_stored[u], 16 * (k + 1))
                    sp.sem_inc(sp_alone, 1)
                    load(2 * k + 2 + u, u)
            for u in range(2):
                store(NB - 2 + u, u, NB // 2 - 1)
            for u in range(2):
                sp.wait_ge(out_stored[u], 16 * NB // 2)

        @block.scalar
        def _(act):
            act.wait_ge(distance_made, 1)
            nc.scalar.activation(ratio[:, :], ratio[:, :], ACT.Exp).then_inc(ratio_made, 1)
            act.wait_ge(biases_in, 32)
            act.sem_inc(h_made, 2 * PRIMED)
            with act.Fori(0, NB // 2) as k:
                for u in range(2):
                    n = 2 * k + u
                    for i, (e, f) in enumerate(LAYERS):
                        act.wait_ge(lo_made, NL * n + i - 1 + 2 * PRIMED)
                        act.wait_ge(h_psum, NL * n + i + 1)
                        nc.scalar.activation(h_hi[:, i % 2, :], ps_h[i % 2][:, :], ACT.Relu,
                                             bias=b1_sb[:, e, f:f + 1])
                        nc.scalar.activation(h[:, i % 2, :], ps_h[i % 2][:, :], ACT.Relu,
                                             bias=b1_sb[:, e, f:f + 1]).then_inc(h_made, 1)

        @block.vector
        def _(dve):
            dve.sem_inc(lo_made, 2 * PRIMED)
            dve.sem_inc(acc_step, 2 * GATHER)
            steps = Steps(dve, gate_step)
            for e in range(E):
                last = nc.vector.memset(rank[:, e:e + 1], float(E - e))
            steps.done(last)
            tokens = [P, NB * TILES, E]
            for i in range(2):
                values = logits if i == 0 else rest
                steps.done(nc.vector.tensor_reduce(best[i][:, :], values[:, :, :], AX.X, ALU.max))
                steps.done(nc.vector.tensor_tensor(out=score[:, :, :], in0=values[:, :, :],
                                                   in1=best[i][:, :].unsqueeze(2).broadcast_to(tokens),
                                                   op=ALU.is_equal))
                steps.done(nc.vector.tensor_tensor(out=score[:, :, :], in0=score[:, :, :],
                                                   in1=rank[:, :].unsqueeze(1).broadcast_to(tokens), op=ALU.mult))
                steps.done(nc.vector.tensor_reduce(top[:, :], score[:, :, :], AX.X, ALU.max))
                steps.done(nc.vector.tensor_tensor(out=hot[i][:, :, :], in0=score[:, :, :],
                                                   in1=top[:, :].unsqueeze(2).broadcast_to(tokens),
                                                   op=ALU.is_equal))
                if i == 0:
                    steps.done(nc.vector.scalar_tensor_tensor(out=rest[:, :, :], in0=hot[0][:, :, :], scalar=NEG,
                                                              in1=logits[:, :, :], op0=ALU.mult, op1=ALU.add))
            nc.vector.tensor_tensor(out=ratio[:, :], in0=best[1][:, :], in1=best[0][:, :],
                                    op=ALU.subtract).then_inc(distance_made, 1)
            dve.wait_ge(ratio_made, 1)
            steps.done(nc.vector.tensor_scalar(share[1][:, :], ratio[:, :], 1.0, None, ALU.add))
            steps.done(nc.vector.reciprocal(share[0][:, :], share[1][:, :]))
            steps.done(nc.vector.tensor_tensor(out=share[1][:, :], in0=ratio[:, :], in1=share[0][:, :], op=ALU.mult))
            for i in range(2):
                steps.done(nc.vector.tensor_tensor(out=hot[i][:, :, :], in0=hot[i][:, :, :],
                                                   in1=share[i][:, :].unsqueeze(2).broadcast_to(tokens),
                                                   op=ALU.mult))
            steps.done(nc.vector.tensor_tensor(out=gates[:, :, :], in0=hot[0][:, :, :], in1=hot[1][:, :, :],
                                               op=ALU.add))
            dve.wait_ge(biases_in, 32)
            with dve.Fori(0, NB // 2) as k:
                for u in range(2):
                    n = 2 * k + u
                    m = 0
                    dve.wait_ge(block_in[u], 3 * 16 * (k + 1))
                    nc.vector.tensor_copy(gate[:, u, :, :],
                                          gates[:, bass.ds(n * TILES, TILES), :]).then_inc(gate_copied, 1)

                    def gather(e, m):
                        for product in range(2):
                            for j in range(TILES):
                                if m >= TILES:
                                    dve.wait_ge(acc_step, ACCS * n + m - TILES + 1 + 2 * GATHER)
                                src = (b2_sb[:, e, :] if product == 0 else
                                       ps_y[2 * (e % 2) + j // 2][:, (j % 2) * C:(j % 2 + 1) * C])
                                if product == 1 and j % 2 == 0:
                                    dve.wait_ge(y_complete, E * n + e + 1)
                                last = nc.vector.scalar_tensor_tensor(
                                    out=acc[:, u, j, :], in0=src, scalar=gate[:, u, j, e:e + 1],
                                    in1=acc[:, u, j, :], op0=ALU.mult, op1=ALU.add)
                                last.then_inc(acc_step, 1)
                                m += 1
                        return m

                    for i, (e, f) in enumerate(LAYERS):
                        if i == 0:
                            dve.wait_ge(gate_copied, n + 1)
                        dve.wait_ge(h_made, NL * n + i + 1 + 2 * PRIMED)
                        nc.vector.tensor_tensor(out=h_lo[:, i % 2, :], in0=h[:, i % 2, :],
                                                in1=h_hi[:, i % 2, :].bitcast(F32),
                                                op=ALU.subtract).then_inc(lo_made, 1)
                        if f == 0 and e > 0:
                            m = gather(e - 1, m)
                    m = gather(E - 1, m)
                    assert m == ACCS

        @block.tensor
        def _(pe):
            def first_layer(n, u, i):
                e, f = LAYERS[i]
                pe.wait_ge(h_made, NL * n + i - 1 + 2 * PRIMED)
                for a in range(CC):
                    cols = slice(f * P, (f + 1) * P)
                    last = three_products(nc, ps_h[i % 2][:, :],
                                          (w_hi[:, e * CC + a, cols], w_lo[:, e * CC + a, cols]),
                                          (xt_hi[:, u, a, :], xt_lo[:, u, a, :]), a == 0, a == CC - 1)
                last.then_inc(h_psum, 1)

            def second_layer(n, i):
                e, f = LAYERS[i]
                pe.wait_ge(lo_made, NL * n + i + 1 + 2 * PRIMED)
                if f == 0:
                    pe.wait_ge(acc_step, ACCS * n + GATHER * (e - 1) + 2 * GATHER)
                chunk = HALF + e * 2 + f // 2
                cols = slice((f % 2) * C, (f % 2 + 1) * C)
                for j in range(TILES):
                    rows = slice(j * P, (j + 1) * P)
                    last = three_products(nc, ps_y[2 * (e % 2) + j // 2][:, (j % 2) * C:(j % 2 + 1) * C],
                                          (h_hi[:, i % 2, rows], h_lo[:, i % 2, rows]),
                                          (w_hi[:, chunk, cols], w_lo[:, chunk, cols]),
                                          f == 0 and j % 2 == 0, f == FO - 1)
                if f == FO - 1:
                    last.then_inc(y_complete, 1)

            with pe.Fori(0, NB // 2) as k:
                for u in range(2):
                    n = 2 * k + u
                    pe.wait_ge(block_in[u], 3 * 16 * (k + 1))
                    first_layer(n, u, 0)
                    for i in range(1, NL):
                        first_layer(n, u, i)
                        second_layer(n, i - 1)
                    second_layer(n, NL - 1)


def transformer_block(nc, w, out):
    parts_dram = nc.dram_tensor("parts_dram", (2, PARTS, 2, DHE, H, B * T), BF16).ap()
    v_dram = nc.dram_tensor("v_dram", (HG, P, B * T // P, GH, VW), F32).ap()
    minus_dram = [nc.dram_tensor(f"minus_dram{late}", (PARTS, GH, n, P), BF16).ap()
                  for late, n in enumerate((EARLY, QT - EARLY))]
    y_dram = nc.dram_tensor("y_dram", (B * T, C), F32).ap()
    project(nc, w["L0_attn_x"], (w["L0_attn_Wq_down"], w["L0_attn_Wk_down"], w["L0_attn_Wv_down"]),
            ((w["L0_attn_Wq_up_c"], w["L0_attn_Wq_up_e"]), (w["L0_attn_Wk_up_c"], w["L0_attn_Wk_up_e"]),
             (w["L0_attn_Wv_up"],)), w["rope_cos"], w["rope_sin"], parts_dram, v_dram)
    attend(nc, parts_dram, v_dram, minus_dram, y_dram)
    xt_dram = nc.dram_tensor("xt_dram", (2, NB, P, CC, TB), F32).ap()
    x1_dram = nc.dram_tensor("x1_dram", (B * T, C), F32).ap()
    with ExitStack() as ctx:
        w_sb = [ctx.enter_context(nc.sbuf_tensor(f"experts_{half}", [P, 2 * E * F * C // (P * WCH), WCH], F32R))
                for half in ("hi", "lo")]
        logits = ctx.enter_context(nc.sbuf_tensor("logits", [P, NB * TILES, E], F32))
        mix(nc, w["L0_attn_x"], y_dram, w["L0_attn_Wc"], w["L0_ffn_Wr"], w["L0_ffn_br"], w["L0_ffn_W1"],
            w["L0_ffn_W2"], w_sb, logits, xt_dram, x1_dram)
        experts(nc, w_sb, logits, w["L0_ffn_b1"], w["L0_ffn_b2"], xt_dram, x1_dram, out)


_INS = ["L0_attn_x", "L0_attn_Wq_down", "L0_attn_Wk_down", "L0_attn_Wv_down", "L0_attn_Wq_up_c",
        "L0_attn_Wq_up_e", "L0_attn_Wk_up_c", "L0_attn_Wk_up_e", "L0_attn_Wv_up", "L0_attn_Wc",
        "L0_ffn_Wr", "L0_ffn_br", "L0_ffn_W1", "L0_ffn_b1", "L0_ffn_W2", "L0_ffn_b2"]


def kernel(**inputs):
    import numpy as np
    import concourse.bacc as bacc
    from concourse.bass_utils import run_bass_kernel_spmd

    nc = bacc.Bacc("TRN2", target_bir_lowering=False, num_devices=1)
    arrays = {name: np.ascontiguousarray(inputs[name]) for name in _INS}
    inverse = np.float32(1.0) / np.float32(10000.0) ** (np.arange(0, DHE, 2, dtype=np.float32) / np.float32(DHE))
    angle = np.arange(T, dtype=np.float32)[None, :] * np.concatenate((inverse, inverse))[:, None]
    sign = np.where(np.arange(DHE) % 2 == 0, np.float32(-1.0), np.float32(1.0))
    arrays["rope_cos"] = np.repeat(np.cos(angle).astype(np.float32), H, axis=0)
    arrays["rope_sin"] = np.repeat((np.sin(angle) * sign[:, None]).astype(np.float32), H, axis=0)
    args = {name: nc.dram_tensor(f"in_{name}", a.shape, mybir.dt.from_np(a.dtype), kind="ExternalInput").ap()
            for name, a in arrays.items()}
    out = nc.dram_tensor("out_0", (B, T, C), F32, kind="ExternalOutput").ap()
    transformer_block(nc, args, out)
    feeds = {f"in_{name}": a for name, a in arrays.items()}
    return run_bass_kernel_spmd(nc, [feeds], core_ids=[0]).results[0]["out_0"]
```

```python
from contextlib import ExitStack

import concourse.bass as bass
from concourse import mybir

P = 128
B, T, C = 4, 2048, 256
H, L, DH = 16, 64, 16
DHE = DH // 2
E, F = 8, 512
EPS = 1e-5
TB = 512
TILES = TB // P
CH = T // TB
NB = B * CH
QT = T // P
CC = C // P
HP = H // 2
GH = 4
HG = H // GH
NG = B * HG
VW = DH + 1
PARTS = 3

PRIMED = 1

ALU = mybir.AluOpType
ACT = mybir.ActivationFunctionType
AX = mybir.AxisListType
F32 = mybir.dt.float32
F32R = mybir.dt.float32r
BF16 = mybir.dt.bfloat16
I32 = mybir.dt.int32
RSQRT_MAGIC = float(0x5F3759DF)


class Steps:

    def __init__(self, engine, sem, base=0):
        self.engine, self.sem, self.base, self.n = engine, sem, base, 0

    def done(self, instruction):
        instruction.then_inc(self.sem, 1)
        self.n += 1
        self.engine.wait_ge(self.sem, self.base + self.n)


def layer_norm_stats(nc, steps, x, stats, mv, var, rstd, tmp, alone):
    for j in range(TILES):
        last = nc.vector.bn_stats(stats[:, j, :], x[:, j, :])
    steps.done(last)
    steps.engine.sem_inc(alone, 1)
    for j in range(TILES):
        last = nc.vector.bn_aggr(mv[:, j, :], stats[:, j, :])
    steps.done(last)
    steps.done(nc.vector.tensor_scalar(var[:, :], mv[:, :, 1], EPS, None, ALU.add))
    steps.done(nc.vector.tensor_scalar(tmp[:, :].bitcast(I32), var[:, :].bitcast(I32), 1, None,
                                       ALU.logical_shift_right))
    steps.done(nc.vector.tensor_scalar(rstd[:, :].bitcast(I32), tmp[:, :].bitcast(I32), -1.0, RSQRT_MAGIC,
                                       ALU.mult, ALU.add))
    for _ in range(3):
        steps.done(nc.vector.tensor_tensor(tmp[:, :], rstd[:, :], rstd[:, :], ALU.mult))
        steps.done(nc.vector.scalar_tensor_tensor(out=tmp[:, :], in0=tmp[:, :], scalar=-0.5, in1=var[:, :],
                                                  op0=ALU.mult, op1=ALU.mult))
        steps.done(nc.vector.scalar_tensor_tensor(out=rstd[:, :], in0=tmp[:, :], scalar=1.5, in1=rstd[:, :],
                                                  op0=ALU.add, op1=ALU.mult))


LN_STEPS = 5 + 9


def three_products(nc, out, stationary, moving, first, last):
    (s_hi, s_lo), (m_hi, m_lo) = stationary, moving
    nc.tensor.matmul(out, s_lo, m_hi, start=first, stop=False, skip_group_check=True)
    nc.tensor.matmul(out, s_hi, m_lo, start=False, stop=False, skip_group_check=True)
    return nc.tensor.matmul(out, s_hi, m_hi, start=False, stop=last, skip_group_check=True)


def make_identity(nc, eng, ident, sem):
    nc.gpsimd.memset(ident[:, :], 0.0).then_inc(sem, 1)
    eng.wait_ge(sem, 1)
    nc.gpsimd.affine_select(out=ident[:, :], in_=ident[:, :], compare_op=ALU.not_equal, fill=1.0, base=0,
                            pattern=[[-1, P]], channel_multiplier=1).then_inc(sem, 1)


def pipeline(eng, first, body):
    first(0, 0, 0)
    with eng.Fori(0, NB // 2 - 1) as k:
        body(2 * k, 0, k, lambda: first(2 * k + 1, 1, k))
        body(2 * k + 1, 1, k, lambda: first(2 * k + 2, 0, k + 1))
    last = NB // 2 - 1
    body(NB - 2, 0, last, lambda: first(NB - 1, 1, last))
    body(NB - 1, 1, last, lambda: None)


def project(nc, x, downs, ups, rope_cos, rope_sin, parts_dram, v_dram):
    NDOWN = 3
    with ExitStack() as ctx:
        def sb(name, shape, dt):
            return ctx.enter_context(nc.sbuf_tensor(name, shape, dt))

        def sem(name):
            return ctx.enter_context(nc.semaphore(name))

        def bank(name):
            return ctx.enter_context(nc.psum_tensor(name, [P, 512], F32))

        ident = sb("ident1", [P, P], F32)
        down = sb("down", [P, NDOWN, CC, H * L], F32)
        down_t = sb("down_t", [P, NDOWN, HP, C], F32)
        up = sb("up", [P, 2, 2, 2, DHE], F32)
        up_v = sb("up_v", [P, 2, DH], F32)
        w_hi = sb("w_hi", [P, NDOWN, CC, C], F32R)
        w_lo = sb("w_lo", [P, NDOWN, CC, C], F32R)
        cos = sb("cos", [P, T], F32)
        sin = sb("sin", [P, T], F32)
        xin = sb("xin", [P, 2, TILES, C], F32)
        xn = sb("xn", [P, 2, TILES, C], F32)
        stats = sb("stats", [P, TILES, 6], F32)
        mv = sb("mv", [P, TILES, 2], F32)
        var = sb("var", [P, TILES], F32)
        rstd = sb("rstd", [P, TILES], F32)
        tmp = sb("tmp", [P, TILES], F32)
        xt_hi = sb("xt_hi", [P, 2, CC, TB], F32R)
        xt_lo = sb("xt_lo", [P, 2, CC, TB], F32R)
        raw = sb("raw", [P, 2, TB], F32)
        swapped = sb("swapped", [P, 2, TB], F32)
        turned = sb("turned", [P, 2, TB], F32)
        rest = sb("rest", [P, 4, TB], F32)
        parts = sb("parts", [P, 2, 4, PARTS, TB], BF16)
        v_out = sb("v_out", [P, 2, HG, TILES, GH, VW], F32)

        ps_t = [bank(f"ps_t{i}") for i in range(CC)]
        ps_p = [bank(f"ps_p{i}") for i in range(4)]
        ps_v = [bank(f"ps_v{i}") for i in range(2)]

        ident_made = sem("ident_made")
        up_clear = sem("up_clear")
        ups_in = sem("ups_in")
        downs_in = sem("downs_in")
        rope_in = sem("rope_in")
        down_turned = sem("down_turned")
        down_copied = sem("down_copied")
        folded = sem("folded")
        w_hi_made = sem("w_hi_made")
        w_made = sem("w_made")
        ones_set = sem("ones_set")
        x_in = [sem(f"x_in{u}") for u in range(2)]
        dve_step = sem("dve_step1")
        rest_step = sem("rest_step")
        dve_alone = sem("dve_alone1")
        pool_alone = sem("pool_alone1")
        xn_made = sem("xn_made1")
        xt_turned = sem("xt_turned1")
        xt_hi_made = sem("xt_hi_made1")
        xt_lo_made = sem("xt_lo_made1")
        projected = sem("projected")
        v_projected = sem("v_projected")
        raw_copied = sem("raw_copied")
        part1_made = sem("part1_made")
        plain_rest = sem("plain_rest")
        part2_made = sem("part2_made")
        part3_made = sem("part3_made")
        swap_made = sem("swap_made")
        sine_made = sem("sine_made")
        raw_read = sem("raw_read")
        turned_made = sem("turned_made")
        v_copied = sem("v_copied")
        parts_out = [sem(f"parts_out{u}") for u in range(2)]
        v_stored = [sem(f"v_stored{u}") for u in range(2)]

        x_v = x.rearrange("b (c j p) d -> (b c) p j d", p=P, j=TILES)
        PROJ = [(0, 0), (1, 0), (0, 1), (1, 1)]

        block = ctx.enter_context(nc.Block())

        @block.sync
        def _(sp):
            for u in range(2):
                sp.sem_inc(parts_out[u], 16 * PRIMED)
                sp.sem_inc(v_stored[u], 16 * PRIMED)
            for m in range(NDOWN):
                sp.dma_start(down[:, m, :, :], downs[m].rearrange("(a p) n -> p a n", p=P)).then_inc(downs_in, 16)
            for u in range(2):
                sp.dma_start(xin[:, u, :, :], x_v[u, :, :, :]).then_inc(x_in[u], 16)
            sp.wait_ge(up_clear, 2)
            for m, halves in enumerate(ups):
                for half, w in enumerate(halves):
                    for h2 in range(2):
                        rows = slice(h2 * L, (h2 + 1) * L)
                        to = up[rows, m, half, h2, :] if m < 2 else up_v[rows, h2, :]
                        sp.dma_start(to, w).then_inc(ups_in, 16)

            def load_x(n, u):
                sp.dma_start(xin[:, u, :, :], x_v[n, :, :, :]).then_inc(x_in[u], 16)

            def store(n, u):
                sp.wait_ge(part3_made, 4 * n + 4 + PRIMED)
                for i, (t, half) in enumerate(PROJ):
                    to = parts_dram[t, :, half, :, :, bass.ds(n * TB, TB)]
                    sp.dma_start(to.rearrange("s j h n -> (j h) s n"),
                                 parts[:, u, i, :, :]).then_inc(parts_out[u], 16)
                sp.wait_ge(v_copied, 2 * n + 2 + PRIMED)
                sp.dma_start(v_dram[:, :, bass.ds(n * TILES, TILES), :, :].rearrange("a p j h d -> p a (j h d)"),
                             v_out[:, u, :, :, :, :].rearrange("p a j h d -> p a (j h d)")).then_inc(v_stored[u], 16)

            with sp.Fori(0, NB // 2 - 1) as k:
                for u in range(2):
                    sp.wait_ge(xn_made, 2 * k + u + 1)
                    load_x(2 * k + 2 + u, u)
                    store(2 * k + u, u)
            for u in range(2):
                store(NB - 2 + u, u)
            for u in range(2):
                sp.wait_ge(parts_out[u], NB // 2 * 4 * 16 + 16 * PRIMED)
                sp.wait_ge(v_stored[u], NB // 2 * 16 + 16 * PRIMED)

        @block.gpsimd
        def _(pool):
            pool.sem_inc(part3_made, PRIMED)
            nc.gpsimd.memset(up[:, :, :, :, :], 0.0).then_inc(up_clear, 1)
            nc.gpsimd.memset(up_v[:, :, :], 0.0).then_inc(up_clear, 1)
            make_identity(nc, pool, ident, ident_made)
            nc.gpsimd.memset(v_out[:, :, :, :, :, :], 1.0).then_inc(ones_set, 1)
            for table, src in ((cos, rope_cos), (sin, rope_sin)):
                pool.dma_start(table[:, :], src).then_inc(rope_in, 16)
            pool.wait_ge(rope_in, 2 * 16)
            with pool.Fori(0, B) as b:
                with pool.Fori(0, CH // 2) as c2:
                    for u in range(2):
                        n = (b * (CH // 2) + c2) * 2 + u
                        for i in range(2):
                            pool.wait_ge(swap_made, 2 * n + i + 1)
                            pool.sem_inc(pool_alone, 1)
                            nc.gpsimd.tensor_tensor(out=swapped[:, i, :], in0=swapped[:, i, :],
                                                    in1=sin[:, bass.ds((c2 * 2 + u) * TB, TB)],
                                                    op=ALU.mult).then_inc(sine_made, 1)
                        for i in range(4):
                            pool.wait_ge(part2_made, 4 * n + i + 1)
                            if i == 0:
                                pool.wait_ge(parts_out[u], (b * (CH // 2) + c2) * (4 * 16) + 16 * PRIMED)
                            nc.gpsimd.tensor_tensor(out=parts[:, u, i, 2, :], in0=rest[:, i, :],
                                                    in1=parts[:, u, i, 1, :],
                                                    op=ALU.subtract).then_inc(part3_made, 1)

        @block.scalar
        def _(act):
            act.sem_inc(raw_copied, PRIMED)
            act.sem_inc(v_copied, PRIMED)
            for g in range(NDOWN * 4):
                act.wait_ge(down_turned, g + 1)
                nc.scalar.copy(down_t[:, g // 4, 2 * (g % 4):2 * (g % 4) + 2, :].rearrange("p a n -> p (a n)"),
                               ps_p[g % 4][:, :]).then_inc(down_copied, 1)
            for m in range(NDOWN):
                act.wait_ge(folded, m + 1)
                nc.scalar.copy(w_hi[:, m, :, :].rearrange("p a n -> p (a n)"), ps_p[m][:, :]).then_inc(w_hi_made, 1)
            act.wait_ge(ones_set, 1)

            def turn_rows(n, u, k):
                for a in range(CC):
                    act.wait_ge(xt_turned, CC * n + a + 1 + PRIMED)
                    nc.scalar.copy(xt_hi[:, u, a, :], ps_t[a][:, :]).then_inc(xt_hi_made, 1)

            def body(n, u, k, start_next):
                act.wait_ge(parts_out[u], k * (4 * 16) + 16 * PRIMED)
                act.wait_ge(v_stored[u], k * 16 + 16 * PRIMED)
                for i in range(2):
                    act.wait_ge(projected, 4 * n + i + 1)
                    nc.scalar.copy(parts[:, u, i, 0, :], ps_p[i][:, :]).then_inc(part1_made, 1)
                act.wait_ge(raw_read, 2 * n + PRIMED)
                for i in range(2):
                    act.wait_ge(projected, 4 * n + i + 3)
                    nc.scalar.copy(raw[:, i, :], ps_p[2 + i][:, :]).then_inc(raw_copied, 1)
                for j in range(2):
                    act.wait_ge(v_projected, 2 * n + j + 1)
                    for s in range(2):
                        last = nc.scalar.copy(
                            v_out[:, u, :, 2 * j + s, :, 0:DH],
                            ps_v[j][:, s * C:(s + 1) * C].rearrange("p (a h d) -> p a h d", a=HG, h=GH))
                    last.then_inc(v_copied, 1)
                start_next()
                for i in range(2):
                    act.wait_ge(turned_made, 2 * n + i + 1)
                    nc.scalar.copy(parts[:, u, 2 + i, 0, :], turned[:, i, :]).then_inc(part1_made, 1)
            pipeline(act, turn_rows, body)

        @block.vector
        def _(dve):
            for s in (raw_read, plain_rest, xt_lo_made):
                dve.sem_inc(s, PRIMED)

            def fold_low():
                for m in range(NDOWN):
                    dve.wait_ge(w_hi_made, m + 1)
                    nc.vector.tensor_tensor(out=w_lo[:, m, :, :].rearrange("p a n -> p (a n)"), in0=ps_p[m][:, :],
                                            in1=w_hi[:, m, :, :].bitcast(F32).rearrange("p a n -> p (a n)"),
                                            op=ALU.subtract).then_inc(w_made, 1)
                dve.wait_ge(rope_in, 2 * 16)

            def normalise(n, u, k):
                steps = Steps(dve, dve_step, n * LN_STEPS)
                dve.wait_ge(x_in[u], 16 * k + 16)
                layer_norm_stats(nc, steps, xin[:, u, :, :], stats, mv, var, rstd, tmp, dve_alone)
                dve.wait_ge(xt_turned, CC * n + PRIMED)
                for j in range(TILES):
                    last = nc.vector.tensor_scalar(xn[:, u, j, :], xin[:, u, j, :], mv[:, j, 0:1],
                                                   rstd[:, j:j + 1], ALU.subtract, ALU.mult)
                last.then_inc(xn_made, 1)
                if isinstance(n, int) and n == 0:
                    fold_low()

            def body(n, u, k, start_next):
                for a in range(CC):
                    dve.wait_ge(xt_hi_made, CC * n + a + 1)
                    nc.vector.tensor_tensor(out=xt_lo[:, u, a, :], in0=ps_t[a][:, :],
                                            in1=xt_hi[:, u, a, :].bitcast(F32),
                                            op=ALU.subtract).then_inc(xt_lo_made, 1)
                start_next()
                for i in range(2):
                    dve.wait_ge(raw_copied, 2 * n + i + 1 + PRIMED)
                    dve.sem_inc(dve_alone, 1)
                    nc.vector.stream_shuffle(swapped[:, i, :], raw[:, i, :],
                                             [j ^ H for j in range(32)]).then_inc(swap_made, 1)
                    nc.vector.tensor_tensor(out=turned[:, i, :], in0=raw[:, i, :],
                                            in1=cos[:, bass.ds(n % CH * TB, TB)],
                                            op=ALU.mult).then_inc(raw_read, 1)
                dve.wait_ge(part3_made, 4 * n + PRIMED)
                for i in range(2):
                    dve.wait_ge(part1_made, 4 * n + i + 1)
                    last = nc.vector.tensor_tensor(out=rest[:, i, :], in0=ps_p[i][:, :],
                                                   in1=parts[:, u, i, 0, :], op=ALU.subtract)
                    last.then_inc(plain_rest, 1)
                    dve.wait_ge(plain_rest, 2 * n + i + 1 + PRIMED)
                    nc.vector.tensor_copy(parts[:, u, i, 1, :], rest[:, i, :]).then_inc(part2_made, 1)
                for i in range(2):
                    dve.wait_ge(raw_read, 2 * n + i + 1 + PRIMED)
                    dve.wait_ge(sine_made, 2 * n + i + 1)
                    nc.vector.tensor_tensor(out=turned[:, i, :], in0=turned[:, i, :],
                                            in1=swapped[:, i, :], op=ALU.add).then_inc(turned_made, 1)
                steps = Steps(dve, rest_step, 2 * n)
                for i in range(2):
                    dve.wait_ge(part1_made, 4 * n + i + 3)
                    steps.done(nc.vector.tensor_tensor(out=rest[:, 2 + i, :], in0=turned[:, i, :],
                                                       in1=parts[:, u, 2 + i, 0, :], op=ALU.subtract))
                    nc.vector.tensor_copy(parts[:, u, 2 + i, 1, :], rest[:, 2 + i, :]).then_inc(part2_made, 1)
            pipeline(dve, normalise, body)

        @block.tensor
        def _(pe):
            pe.sem_inc(xt_turned, PRIMED)
            pe.wait_ge(ident_made, 2)
            pe.wait_ge(downs_in, NDOWN * 16)
            for g in range(NDOWN * 4):
                if g >= 4:
                    pe.wait_ge(down_copied, g - 3)
                for s in range(2):
                    pair = 2 * (g % 4) + s
                    for a in range(CC):
                        at = s * C + a * P
                        last = nc.tensor.transpose(ps_p[g % 4][:, at:at + P],
                                                   down[:, g // 4, a, pair * P:(pair + 1) * P], ident[:, :])
                last.then_inc(down_turned, 1)
            pe.wait_ge(down_copied, NDOWN * 4)
            pe.wait_ge(ups_in, 5 * 2 * 16)
            for m in range(NDOWN):
                for a in range(CC):
                    for pair in range(HP):
                        to = ps_p[m][:, a * C:(a + 1) * C]
                        if m < 2:
                            to = to.rearrange("p (f j h) -> p f j h", f=2, j=DHE)[:, :, :, 2 * pair:2 * pair + 2]
                        else:
                            to = to[:, pair * 2 * DH:(pair + 1) * 2 * DH]
                        last = nc.tensor.matmul(to, down_t[:, m, pair, a * P:(a + 1) * P],
                                                up[:, m, :, :, :].rearrange("p f h j -> p f j h") if m < 2 else
                                                up_v[:, :, :].rearrange("p h d -> p (h d)"),
                                                start=(a == 0 and pair == 0), stop=(a == 1 and pair == HP - 1),
                                                skip_group_check=True)
                last.then_inc(folded, 1)
            pe.wait_ge(w_made, NDOWN)
            with pe.Fori(0, NB // 2) as k:
                for u in range(2):
                    n = 2 * k + u
                    pe.wait_ge(xn_made, n + 1)
                    pe.wait_ge(xt_lo_made, CC * n + PRIMED)
                    for a in range(CC):
                        for j in range(TILES):
                            last = nc.tensor.transpose(ps_t[a][:, j * P:(j + 1) * P],
                                                       xn[:, u, j, a * P:(a + 1) * P], ident[:, :])
                        last.then_inc(xt_turned, 1)
                    pe.wait_ge(xt_lo_made, CC * n + CC + PRIMED)
                    for i, (m, half) in enumerate(PROJ):
                        pe.wait_ge(plain_rest if i < 2 else raw_copied, 2 * n + PRIMED)
                        for a in range(CC):
                            cols = slice(half * P, (half + 1) * P)
                            last = three_products(nc, ps_p[i][:, :],
                                                  (w_hi[:, m, a, cols], w_lo[:, m, a, cols]),
                                                  (xt_hi[:, u, a, :], xt_lo[:, u, a, :]), a == 0, a == CC - 1)
                        last.then_inc(projected, 1)
                    pe.wait_ge(v_copied, 2 * n + PRIMED)
                    for j in range(TILES):
                        for a in range(CC):
                            cols = slice(j * P, (j + 1) * P)
                            last = three_products(nc, ps_v[j // 2][:, (j % 2) * C:(j % 2 + 1) * C],
                                                  (xt_hi[:, u, a, cols], xt_lo[:, u, a, cols]),
                                                  (w_hi[:, 2, a, :], w_lo[:, 2, a, :]),
                                                  a == 0 and j % 2 == 0, a == CC - 1)
                        if j % 2:
                            last.then_inc(v_projected, 1)


STACK = 6 * DH
ROWS = STACK + PARTS
EARLY = 12
NEG = -3.0e38
RING = 3
AHEAD = 12


def attention_plan():
    steps = [(c, kt) for c in range(CH) for kt in range((c + 1) * TILES)]

    def pieces(tiles):
        return [("max", qt, h, kc) for qt in tiles for h in range(GH) for kc in range(qt // TILES + 1)]

    def width(e):
        _, qt, _, kc = e[:4]
        return TB if kc < qt // TILES else (qt % TILES + 1) * P

    late = [e + (False,) for e in pieces(range(EARLY, QT))]
    early = [e + (True,) for e in pieces(range(EARLY))]
    late_ahead = [e[:4] + (True,) for e in late[:AHEAD]]
    maxes = late[AHEAD:] + [("chain", True)] + early[:3] + [("turn_max", True)] + early[3:] + [
        ("chain", False)] + late_ahead[:3] + [("turn_max", False)] + late_ahead[3:]
    scores = [(s, pair) for s in range(len(steps)) for pair in range(2)]
    lo = [max(0, kt - c * TILES) * P for c, kt in steps]
    plan, now, vector, scalar = [], 0.0, 0.0, 0.0
    exp_end, taken = [0.0, 0.0], [0.0] * RING
    outs, i, s, at, copied = [], 0, 0, 0, 0.0
    out_ready, rows_ready, late_ready = 0.0, 0.0, 0.0
    while i < len(scores) or s < len(steps) or at < len(maxes) or outs:
        ready = {}
        if outs:
            ready["turn_out"] = max(out_ready, taken[-RING])
        if at < len(maxes):
            ready["max"] = (0.0 if maxes[at][0] == "chain" else taken[-RING] if maxes[at][0] == "max" else
                            max(taken[-RING], rows_ready))
        if i < len(scores) and scores[i][0] < s + 4:
            ready["scores"] = max(exp_end[-2], late_ready if steps[scores[i][0]][0] == CH - 1 else 0.0)
        if s < len(steps) and i > 2 * s + 1:
            ready["sum"] = exp_end[2 * s + 3] + (900 if lo[s] or steps[s][1] == steps[s][0] * TILES else 0)
            if steps[s][1] == 0:
                ready["sum"] = max(ready["sum"], copied)
        kind = min(ready, key=lambda k: (max(now, ready[k]), list(ready).index(k)))
        now = max(now, ready[kind])
        if kind == "max":
            e = maxes[at]
            at += 1
            plan.append(e)
            if e[0] == "chain":
                rows_ready = taken[-1] + 1000
                vector = max(vector, taken[-1]) + 600
            else:
                now += width(e) / 2.4 if e[0] == "max" else 200
                vector = max(vector, now + 130) + (width(e) if e[0] == "max" else 400) / 0.96 + 70
                taken.append(vector + 60)
                if e[0] == "turn_max" and e[1]:
                    late_ready = vector + 6000
        elif kind == "scores":
            plan.append(("scores",) + scores[i])
            w = TB - lo[scores[i][0]]
            i += 1
            now += 2 * w / 2.4
            scalar = max(scalar, now + 100) + 2 * w / 1.2 + 50
            exp_end.append(scalar + 60)
        elif kind == "sum":
            plan.append(("sum", s))
            now += 4 * (TB - lo[s]) / 2.2
            if lo[s] == (TILES - 1) * P:
                outs.append(steps[s][0])
                scalar = max(scalar, now + 150) + 480
                copied = scalar + 60
                out_ready = copied
            s += 1
        else:
            plan.append(("turn_out", outs.pop(0)))
            now += 450
            vector = max(vector, now + 100) + 900
            taken.append(vector + 60)
    return steps, plan, early, late_ahead, width


def attend(nc, parts_dram, v_dram, minus_dram, y_dram):
    STEPS, PLAN, EARLY_PIECES, LATE_AHEAD, width = attention_plan()
    NSTEP = len(STEPS)
    NITEM = 2 * NSTEP
    PLACES = {"max": 1, "turn_max": 2, "turn_out": 1}
    NRING = sum(PLACES.get(e[0], 0) for e in PLAN)
    NDIAG = 2 * QT
    assert NRING % RING == 0 and NSTEP % 4 == 0
    NEARLY = len(EARLY_PIECES) + PLACES["turn_max"]
    RING0 = NEARLY + AHEAD
    CHAIN_STEPS = 4
    LOADS = 10

    with ExitStack() as ctx:
        def sb(name, shape, dt):
            return ctx.enter_context(nc.sbuf_tensor(name, shape, dt))

        def sem(name):
            return ctx.enter_context(nc.semaphore(name))

        q_st = sb("q_st", [ROWS, 2, GH, T], BF16)
        k_st = sb("k_st", [ROWS, 2, GH, T], BF16)
        v_sb = sb("v_sb", [P, 2, QT, GH, VW], F32)
        prob = sb("prob", [P, 4, GH, TB], F32)
        out_sb = sb("out_sb", [P, 2, TB], F32)
        y_sb = sb("y_sb", [P, 2, TILES, GH, DH], F32)
        rec = sb("rec", [P, 2, TILES, GH], F32)
        ident = sb("ident2", [P, P], F32)
        ident_bf = sb("ident_bf", [P, P], BF16)
        causal = sb("causal", [P, TB], F32)
        junk = sb("junk", [P, RING, TB], F32)
        maxes = sb("maxes", [P, GH, QT, CH], F32)
        minus = sb("minus", [P, GH, EARLY], F32)
        left = sb("left", [P, GH, EARLY], F32)
        minus_parts = sb("minus_parts", [P, PARTS, GH * EARLY], BF16)
        minus_rows = sb("minus_rows", [GH * EARLY, PARTS, P], BF16)

        ps_s = [ctx.enter_context(nc.psum_tensor(f"ps_s{i}", [P, 2, 512], F32)) for i in range(2)]
        ps_m = [ctx.enter_context(nc.psum_tensor(f"ps_m{i}", [P, 512], F32)) for i in range(RING)]
        ps_o = ctx.enter_context(nc.psum_tensor("ps_o", [P, 512], F32))

        ident_made = sem("ident_made2")
        ident_bf_made = sem("ident_bf_made2")
        causal_made = sem("causal_made")
        ones_made = sem("ones_made")
        maxes_clear = sem("maxes_clear")
        banks_clear = sem("banks_clear")
        loaded = sem("loaded")
        scores_made = sem("scores_made")
        exp_made = sem("exp_made")
        masked = sem("masked")
        summed = sem("summed")
        out_copied = sem("out_copied")
        y_stored = [sem(f"y_stored{i}") for i in range(2)]
        rec_made = sem("rec_made")
        pe_alone = sem("pe_alone2")
        dve_alone = sem("dve_alone2")
        pool_alone = sem("pool_alone2")
        piece_made = sem("piece_made")
        piece_taken = sem("piece_taken")
        minus_made = sem("minus_made")
        rows_out = sem("rows_out")
        rows_in = sem("rows_in")
        dve_step = sem("dve_step2")

        block = ctx.enter_context(nc.Block())

        def windows(eng, body):
            with eng.Fori(0, NG // 2 - 1) as k:
                for u in range(2):
                    body(2 * k + u, u, False)
            for u in range(2):
                body(NG - 2 + u, u, u == 1)

        def plan_of(last):
            ring = 0
            for e in PLAN:
                if last and (e[0] == "max" and e[4] or e[0] in ("chain", "turn_max") and not e[1]):
                    continue
                yield e, ring
                ring += PLACES.get(e[0], 0)

        @block.sync
        def _(sp):
            for i in range(2):
                sp.sem_inc(y_stored[i], 16 * PRIMED)
            sp.sem_inc(rows_in, 16 * PRIMED)

            def load(g, u):
                b, hg = g // HG, g % HG
                at = 0
                for i in range(PARTS):
                    n = PARTS - i
                    q_rows, k_rows = (parts_dram[t, :, :, :, bass.ds(hg * GH, GH), bass.ds(b * T, T)]
                                      for t in range(2))
                    for _ in range(n):
                        sp.dma_start(q_st[at:at + DH, u, :, :],
                                     q_rows[i].rearrange("f j h n -> (f j) h n")).then_inc(loaded, 16)
                        at += DH
                    sp.dma_start(k_st[at - n * DH:at, u, :, :],
                                 k_rows[0:n].rearrange("s f j h n -> (s f j) h n")).then_inc(loaded, 16)
                sp.dma_start(v_sb[:, u, :, :, :].rearrange("p k h d -> p (k h d)"),
                             v_dram[hg, :, bass.ds(b * QT, QT), :, :].rearrange("p k h d -> p (k h d)")
                             ).then_inc(loaded, 16)

            def place_minus(u, late, number):
                lo, n = (EARLY, QT - EARLY) if late else (0, EARLY)
                sp.dma_start(minus_dram[late][:, :, :, :].rearrange("s h k n -> (h k) s n"),
                             minus_rows[0:GH * n, :, :]).then_inc(rows_out, 16)
                sp.wait_ge(rows_out, 16 * number)
                sp.dma_start(q_st[STACK:ROWS, u, :, lo * P:(lo + n) * P],
                             minus_dram[late][:, :, :, :].rearrange("s h k n -> s h (k n)")).then_inc(rows_in, 16)

            load(0, 0)
            sp.wait_ge(piece_taken, NEARLY + RING * PRIMED)
            place_minus(0, False, 1)

            def body(w, u, last):
                if not last:
                    sp.wait_ge(summed, NSTEP * w + 4 * PRIMED)
                    load(w + 1, 1 - u)
                for e, ring in plan_of(last):
                    if e[0] == "turn_max":
                        sp.wait_ge(piece_taken, RING0 + NRING * w + ring + 2 + RING * PRIMED)
                        place_minus(u if e[1] else 1 - u, e[1], 2 * w + (2 if e[1] else 3))
                    elif e[0] == "turn_out":
                        c = e[1]
                        sp.wait_ge(piece_taken, RING0 + NRING * w + ring + 1 + RING * PRIMED)
                        to = y_dram[bass.ds((w // HG) * T + c * TB, TB), bass.ds((w % HG) * (GH * DH), GH * DH)]
                        sp.dma_start(to.rearrange("(j p) n -> p j n", p=P),
                                     y_sb[:, c % 2, :, :, :].rearrange("p j h d -> p j (h d)")
                                     ).then_inc(y_stored[c % 2], 16)
            windows(sp, body)
            for i in range(2):
                sp.wait_ge(y_stored[i], 16 * (NG * CH // 2 + PRIMED))

        @block.gpsimd
        def _(pool):
            make_identity(nc, pool, ident, ident_made)
            nc.gpsimd.memset(maxes[:, :, :, :], NEG).then_inc(maxes_clear, 1)
            nc.gpsimd.memset(causal[:, :], 0.0).then_inc(causal_made, 1)
            pool.wait_ge(causal_made, 1)
            nc.gpsimd.affine_select(out=causal[:, TB - P:TB], in_=causal[:, TB - P:TB], compare_op=ALU.is_ge,
                                    fill=NEG, base=0, pattern=[[-1, P]],
                                    channel_multiplier=1).then_inc(causal_made, 1)

            def body(w, u, last):
                diag = 0
                for s, (c, kt) in enumerate(STEPS):
                    r = kt - c * TILES
                    if r < 0:
                        continue
                    for pair in range(2):
                        pool.wait_ge(exp_made, NITEM * w + 2 * s + pair + 1 + 2 * PRIMED)
                        pool.sem_inc(pool_alone, 1)
                        tile = prob[:, s % 4, 2 * pair:2 * pair + 2, r * P:(r + 1) * P]
                        nc.gpsimd.affine_select(out=tile, in_=tile, compare_op=ALU.is_ge, fill=0.0, base=0,
                                                pattern=[[0, 2], [1, P]],
                                                channel_multiplier=-1).then_inc(masked, 1)
                        diag += 1
                assert diag == NDIAG
            windows(pool, body)

        @block.scalar
        def _(act):
            act.sem_inc(exp_made, 2 * PRIMED)

            act.sem_inc(out_copied, PRIMED)

            def body(w, u, last):
                for e, _ in plan_of(last):
                    if e[0] == "scores":
                        _, s, pair = e
                        c, kt = STEPS[s]
                        lo = max(0, kt - c * TILES) * P
                        n = 2 * s + pair
                        if pair == 0:
                            act.wait_ge(summed, NSTEP * w + s + PRIMED)
                        act.wait_ge(scores_made, NITEM * w + n + 1)
                        nc.scalar.activation(prob[:, s % 4, 2 * pair:2 * pair + 2, lo:TB],
                                             ps_s[n % 2][:, :, lo:TB], ACT.Exp,
                                             scale=DH ** -0.5).then_inc(exp_made, 1)
                    elif e[0] == "sum" and STEPS[e[1]][1] == (STEPS[e[1]][0] + 1) * TILES - 1:
                        s = e[1]
                        act.wait_ge(summed, NSTEP * w + s + 1 + 4 * PRIMED)
                        nc.scalar.copy(out_sb[:, STEPS[s][0] % 2, :], ps_o[:, :]).then_inc(out_copied, 1)
            windows(act, body)

        @block.vector
        def _(dve):
            dve.sem_inc(piece_taken, RING * PRIMED)
            nc.vector.memset(ps_o[:, :], 0.0).then_inc(banks_clear, 1)
            nc.vector.memset(k_st[STACK:ROWS, :, :, :], 1.0).then_inc(ones_made, 1)
            dve.wait_ge(ident_made, 2)
            nc.vector.tensor_copy(ident_bf[:, :], ident[:, :]).then_inc(ident_bf_made, 1)
            dve.wait_ge(causal_made, 2)
            dve.wait_ge(maxes_clear, 1)

            def take(e, parity):
                _, qt, h, kc = e[:4]
                w = width(e)
                to = maxes[:, h, qt, kc:kc + 1]
                bank = ps_m[parity]
                if kc < qt // TILES:
                    return nc.vector.tensor_reduce(to, bank[:, 0:w], AX.X, ALU.max)
                return nc.vector.tensor_tensor_reduce(junk[:, parity, 0:w], bank[:, 0:w], causal[:, TB - w:TB], 1.0, NEG,
                                                      ALU.add, ALU.max, to)

            def split_minus(steps, late):
                lo, n = (EARLY, QT - EARLY) if late else (0, EARLY)
                m, rest = minus[:, :, 0:n], left[:, :, 0:n]
                parts = [minus_parts[:, i, 0:GH * n].rearrange("p (h n) -> p h n", h=GH) for i in range(PARTS)]
                steps.done(nc.vector.tensor_reduce(m, maxes[:, :, lo:lo + n, :], AX.X, ALU.max, negate=True))
                steps.done(nc.vector.tensor_copy(parts[0], m))
                steps.done(nc.vector.tensor_tensor(out=rest, in0=m, in1=parts[0], op=ALU.subtract))
                steps.done(nc.vector.tensor_copy(parts[1], rest))
                nc.vector.tensor_tensor(out=parts[2], in0=rest, in1=parts[1], op=ALU.subtract).then_inc(minus_made, 1)

            def copy_minus(bank, late):
                n = QT - EARLY if late else EARLY
                src = bank[:, :].bitcast(BF16)[0:GH * n, 0:PARTS * P].rearrange("p (s n) -> p s n", s=PARTS)
                nc.vector.tensor_copy(minus_rows[0:GH * n, :, :], src).then_inc(piece_taken, 2)

            for i, e in enumerate(EARLY_PIECES):
                dve.wait_ge(piece_made, i + 1)
                take(e, i % RING).then_inc(piece_taken, 1)
            dve.wait_ge(piece_taken, len(EARLY_PIECES) + RING * PRIMED)
            steps = Steps(dve, dve_step)
            split_minus(steps, False)
            dve.wait_ge(piece_made, NEARLY)
            copy_minus(ps_m[len(EARLY_PIECES) % RING], False)
            for i, e in enumerate(LATE_AHEAD, NEARLY):
                dve.wait_ge(piece_made, i + 1)
                take(e, i % RING).then_inc(piece_taken, 1)

            def body(w, u, last):
                steps = Steps(dve, dve_step, CHAIN_STEPS + 2 * CHAIN_STEPS * w)
                for e, ring in plan_of(last):
                    n = RING0 + NRING * w + ring
                    bank = ps_m[(RING0 + ring) % RING]
                    if e[0] == "max":
                        dve.wait_ge(piece_made, n + 1)
                        if e[3] == e[1] // TILES:
                            dve.sem_inc(dve_alone, 1)
                        take(e, (RING0 + ring) % RING).then_inc(piece_taken, 1)
                    elif e[0] == "chain":
                        dve.wait_ge(piece_taken, n + RING * PRIMED)
                        split_minus(steps, e[1])
                    elif e[0] == "turn_max":
                        dve.wait_ge(piece_made, n + 2)
                        k = 2 * w + (1 if e[1] else 2)
                        dve.wait_ge(rows_in, 16 * k + 16 * PRIMED)
                        copy_minus(bank, e[1])
                    elif e[0] == "turn_out":
                        c = e[1]
                        src = bank[:, :].rearrange("p (j h d) -> p j h d", j=TILES, h=GH)
                        dve.wait_ge(piece_made, n + 1)
                        nc.vector.reciprocal(rec[:, c % 2, :, :], src[:, :, :, DH]).then_inc(rec_made, 1)
                        dve.wait_ge(rec_made, CH * w + c + 1)
                        dve.wait_ge(y_stored[c % 2], 16 * (2 * w + c // 2) + 16 * PRIMED)
                        nc.vector.tensor_tensor(out=y_sb[:, c % 2, :, :, :], in0=src[:, :, :, 0:DH],
                                                in1=rec[:, c % 2, :, :].unsqueeze(3).broadcast_to([P, TILES, GH, DH]),
                                                op=ALU.mult).then_inc(piece_taken, 1)
            windows(dve, body)

        @block.tensor
        def _(pe):
            pe.sem_inc(summed, 4 * PRIMED)
            pe.wait_ge(ident_bf_made, 1)
            pe.wait_ge(ones_made, 1)
            pe.wait_ge(banks_clear, 1)

            def piece(e, bank, u):
                _, qt, h, kc = e[:4]
                return nc.tensor.matmul(bank[:, 0:width(e)], q_st[0:STACK, u, h, qt * P:(qt + 1) * P],
                                        k_st[0:STACK, u, h, kc * TB:kc * TB + width(e)], start=True, stop=True)

            def turn_max(bank, late):
                n = GH * (QT - EARLY if late else EARLY)
                for part in range(PARTS):
                    last = nc.tensor.transpose(bank[:, :].bitcast(BF16)[0:n, part * P:(part + 1) * P],
                                               minus_parts[:, part, 0:n], ident_bf[:, :])
                return last

            pe.wait_ge(loaded, LOADS * 16)
            for i, e in enumerate(EARLY_PIECES):
                pe.wait_ge(piece_taken, i + 1)
                piece(e, ps_m[i % RING], 0).then_inc(piece_made, 1)
            pe.wait_ge(minus_made, 1)
            pe.wait_ge(piece_taken, len(EARLY_PIECES) + 1)
            turn_max(ps_m[len(EARLY_PIECES) % RING], False).then_inc(piece_made, PLACES["turn_max"])
            for i, e in enumerate(LATE_AHEAD, NEARLY):
                pe.wait_ge(piece_taken, i + 1)
                piece(e, ps_m[i % RING], 0).then_inc(piece_made, 1)

            def body(w, u, last):
                ahead = False
                for e, ring in plan_of(last):
                    n = RING0 + NRING * w + ring
                    bank = ps_m[(RING0 + ring) % RING]
                    if e[0] == "scores":
                        s = e[1]
                        c, kt = STEPS[s]
                        lo = max(0, kt - c * TILES) * P
                        if s == 0 and e[2] == 0:
                            pe.wait_ge(rows_in, 16 * (2 * w + 1) + 16 * PRIMED)
                        if c == EARLY // TILES and kt == 0 and e[2] == 0:
                            pe.wait_ge(rows_in, 16 * (2 * w + 2) + 16 * PRIMED)
                        i = 2 * s + e[2]
                        pe.wait_ge(exp_made, NITEM * w + i + 1)
                        for h2 in range(2):
                            h = 2 * e[2] + h2
                            mm = nc.tensor.matmul(ps_s[i % 2][:, h2, lo:TB], k_st[:, u, h, kt * P:(kt + 1) * P],
                                                  q_st[:, u, h, c * TB + lo:(c + 1) * TB], start=True, stop=True)
                        mm.then_inc(scores_made, 1)
                    elif e[0] == "sum":
                        s = e[1]
                        c, kt = STEPS[s]
                        r = kt - c * TILES
                        lo = max(0, r) * P
                        if kt == 0:
                            pe.wait_ge(out_copied, CH * w + c + PRIMED)
                        pe.wait_ge(exp_made, NITEM * w + 2 * s + 2 + 2 * PRIMED)
                        if r >= 0:
                            pe.wait_ge(masked, NDIAG * w + 2 * (c * TILES + r) + 2)
                        for h in range(GH):
                            mm = nc.tensor.matmul(ps_o[32 * h:32 * h + VW, lo:TB], v_sb[:, u, kt, h, :],
                                                  prob[:, s % 4, h, lo:TB], start=(kt == 0),
                                                  stop=(r == TILES - 1), skip_group_check=True)
                        mm.then_inc(summed, 1)
                    elif e[0] == "turn_out":
                        c = e[1]
                        pe.wait_ge(out_copied, CH * w + c + 1 + PRIMED)
                        pe.wait_ge(piece_taken, n + 1)
                        pe.sem_inc(pe_alone, 1)
                        for j in range(TILES):
                            mm = nc.tensor.transpose(bank[:, j * P:(j + 1) * P],
                                                     out_sb[:, c % 2, j * P:(j + 1) * P], ident[:, :])
                        mm.then_inc(piece_made, 1)
                    elif e[0] == "max":
                        if e[4] and not ahead:
                            pe.wait_ge(loaded, LOADS * 16 * (w + 2))
                            ahead = True
                        pe.wait_ge(piece_taken, n + 1)
                        piece(e, bank, 1 - u if e[4] else u).then_inc(piece_made, 1)
                    elif e[0] == "turn_max":
                        pe.wait_ge(minus_made, 2 * w + (2 if e[1] else 3))
                        pe.wait_ge(piece_taken, n + 1)
                        pe.sem_inc(pe_alone, 1)
                        turn_max(bank, e[1]).then_inc(piece_made, PLACES["turn_max"])
            windows(pe, body)


WCH = 512
W_PER_LOOP = 2


def mix(nc, x, y_dram, wc, wr, br, w1, w2, w_sb, logits, xt_dram, x1_dram):
    w_hi, w_lo = w_sb
    with ExitStack() as ctx:
        def sb(name, shape, dt):
            return ctx.enter_context(nc.sbuf_tensor(name, shape, dt))

        def sem(name):
            return ctx.enter_context(nc.semaphore(name))

        def bank(name):
            return ctx.enter_context(nc.psum_tensor(name, [P, 512], F32))

        ident = sb("ident3", [P, P], F32)
        wc_sb = sb("wc_sb", [P, CC, C], F32)
        wr_sb = sb("wr_sb", [P, CC, E], F32)
        br_sb = sb("br_sb", [E, 1], F32)
        raw = sb("w_raw", [P, 2 * W_PER_LOOP, WCH], F32)
        y_in = sb("y_in", [P, 2, TILES, C], F32)
        x_in = sb("x_in", [P, 2, TILES, C], F32)
        yt = sb("yt", [P, 1, CC, TB], F32)
        stats = sb("stats3", [P, TILES, 6], F32)
        mv = sb("mv3", [P, TILES, 2], F32)
        var = sb("var3", [P, TILES], F32)
        rstd = sb("rstd3", [P, TILES], F32)
        tmp = sb("tmp3", [P, TILES], F32)
        xt = sb("xt", [P, 1, CC, TB], F32)
        xt_hi = sb("xt_hi3", [P, 1, CC, TB], F32R)
        xt_lo = sb("xt_lo3", [P, 1, CC, TB], F32R)
        by_expert = sb("by_expert", [E, TB], F32)

        ps_t = [bank(f"ps_yt{i}") for i in range(CC)]
        ps_x = [bank(f"ps_x{i}") for i in range(2)]
        ps_u = [bank(f"ps_u{i}") for i in range(CC)]
        ps_r = bank("ps_r")
        ps_l = bank("ps_l")

        ident_made = sem("ident_made3")
        weights_in = sem("weights_in3")
        y_loaded = [sem(f"y_loaded{u}") for u in range(2)]
        raw_in = sem("raw_in")
        w_hi_made = sem("w_hi_made3")
        w_lo_made = sem("w_lo_made3")
        y_turned = sem("y_turned")
        yt_made = sem("yt_made")
        mixed = sem("mixed")
        x1_made = sem("x1_made")
        dve_step = sem("dve_step3")
        dve_alone = sem("dve_alone3")
        sp_alone = sem("sp_alone3")
        pool_alone = sem("pool_alone3")
        pe_alone = sem("pe_alone3")
        xn_made = sem("xn_made3")
        xn_turned = sem("xn_turned")
        xt_made = sem("xt_made")
        hi_made = sem("hi_made3")
        lo_made = sem("lo_made3")
        routed = sem("routed")
        by_expert_made = sem("by_expert_made")
        logits_turned = sem("logits_turned")
        logits_made = sem("logits_made")
        x1_stored = sem("x1_stored")
        xt_stored = sem("xt_stored")

        x_v = x.rearrange("b (c j p) d -> (b c) p j d", p=P, j=TILES)
        y_v = y_dram.rearrange("(n j p) d -> n p j d", p=P, j=TILES)
        x1_v = x1_dram.rearrange("(n j p) d -> n p j d", p=P, j=TILES)
        w1_v = w1.rearrange("e (a p) f -> (e a) p f", p=P)
        w2_v = w2.rearrange("e (a o p) c -> (e a) p o c", p=P, o=WCH // C)

        block = ctx.enter_context(nc.Block())

        def staged(eng, first, second):
            first(0, 0, 0)
            with eng.Fori(0, NB // 2 - 1) as k:
                first(2 * k + 1, 1, k)
                second(2 * k, 0, k)
                first(2 * k + 2, 0, k + 1)
                second(2 * k + 1, 1, k)
            first(NB - 1, 1, NB // 2 - 1)
            second(NB - 2, 0, NB // 2 - 1)
            second(NB - 1, 1, NB // 2 - 1)

        @block.sync
        def _(sp):
            sp.sem_inc(x1_stored, 16 * PRIMED)
            sp.sem_inc(xt_stored, 32 * PRIMED)
            sp.dma_start(wc_sb[:, :, :], wc.rearrange("(a p) n -> p a n", p=P)).then_inc(weights_in, 16)
            sp.dma_start(wr_sb[:, :, :], wr.rearrange("(a p) n -> p a n", p=P)).then_inc(weights_in, 16)
            sp.dma_start(br_sb[:, :], br.rearrange("(e a) -> e a", a=1)).then_inc(weights_in, 16)

            def load(n, u):
                sp.dma_start(y_in[:, u, :, :], y_v[n, :, :, :]).then_inc(y_loaded[u], 16)
                sp.dma_start(x_in[:, u, :, :], x_v[n, :, :, :]).then_inc(y_loaded[u], 16)

            def load_weights(k):
                sp.wait_ge(w_lo_made, 2 * W_PER_LOOP * k + PRIMED)
                sp.sem_inc(sp_alone, 1)
                for i in range(W_PER_LOOP):
                    sp.dma_start(raw[:, i, :], w1_v[W_PER_LOOP * k + i, :, :]).then_inc(raw_in, 16)
                    sp.dma_start(raw[:, W_PER_LOOP + i, :].rearrange("p (o c) -> p o c", c=C),
                                 w2_v[W_PER_LOOP * k + i, :, :, :]).then_inc(raw_in, 16)

            def store_x1(n, u):
                sp.wait_ge(x1_made, 2 * n + 2 + PRIMED)
                sp.sem_inc(sp_alone, 1)
                sp.dma_start(x1_v[n, :, :, :], x_in[:, u, :, :]).then_inc(x1_stored, 16)

            def store_xt(n):
                sp.wait_ge(lo_made, CC * n + CC + PRIMED)
                sp.sem_inc(sp_alone, 1)
                sp.dma_start(xt_dram[0, n, :, :, :], xt_hi[:, 0, :, :].bitcast(F32)).then_inc(xt_stored, 16)
                sp.dma_start(xt_dram[1, n, :, :, :], xt_lo[:, 0, :, :].bitcast(F32)).then_inc(xt_stored, 16)

            def turn_over(n, u):
                store_x1(n, u)
                sp.wait_ge(x1_stored, 16 * (n + 1) + 16 * PRIMED)
                sp.sem_inc(sp_alone, 1)
                sp.wait_ge(xn_turned, CC * (n + 1))
                sp.sem_inc(sp_alone, 1)
                load(n + 2, u)

            for u in range(2):
                load(u, u)
            load_weights(0)
            turn_over(0, 0)
            with sp.Fori(1, NB // 2 - 1) as k:
                turn_over(2 * k - 1, 1)
                store_xt(2 * k - 2)
                load_weights(k)
                turn_over(2 * k, 0)
                store_xt(2 * k - 1)
            turn_over(NB - 3, 1)
            store_xt(NB - 4)
            load_weights(NB // 2 - 1)
            store_x1(NB - 2, 0)
            store_xt(NB - 3)
            store_x1(NB - 1, 1)
            store_xt(NB - 2)
            store_xt(NB - 1)
            sp.wait_ge(x1_stored, 16 * (NB + PRIMED))
            sp.wait_ge(xt_stored, 32 * (NB + PRIMED))

        @block.gpsimd
        def _(pool):
            pool.sem_inc(w_lo_made, PRIMED)
            pool.sem_inc(lo_made, PRIMED)
            make_identity(nc, pool, ident, ident_made)
            with pool.Fori(0, NB // 2) as k:
                def split(i):
                    chunk = W_PER_LOOP * k + (i % W_PER_LOOP) + (i // W_PER_LOOP) * (NB // 2 * W_PER_LOOP)
                    pool.wait_ge(raw_in, 16 * 2 * W_PER_LOOP * (k + 1))
                    pool.sem_inc(pool_alone, 1)
                    nc.gpsimd.tensor_copy(w_hi[:, bass.ds(chunk, 1), :].rearrange("p a n -> p (a n)"),
                                          raw[:, i, :]).then_inc(w_hi_made, 1)
                    pool.wait_ge(w_hi_made, 2 * W_PER_LOOP * k + i + 1)
                    pool.sem_inc(pool_alone, 1)
                    nc.gpsimd.tensor_tensor(
                        out=w_lo[:, bass.ds(chunk, 1), :].rearrange("p a n -> p (a n)"), in0=raw[:, i, :],
                        in1=w_hi[:, bass.ds(chunk, 1), :].bitcast(F32).rearrange("p a n -> p (a n)"),
                        op=ALU.subtract).then_inc(w_lo_made, 1)

                for u in range(2):
                    n = 2 * k + u
                    for i in range(W_PER_LOOP):
                        split(W_PER_LOOP * u + i)
                    for a in range(CC):
                        pool.wait_ge(hi_made, CC * n + a + 1)
                        nc.gpsimd.tensor_tensor(out=xt_lo[:, 0, a, :], in0=xt[:, 0, a, :],
                                                in1=xt_hi[:, 0, a, :].bitcast(F32),
                                                op=ALU.subtract).then_inc(lo_made, 1)

        @block.scalar
        def _(act):
            act.wait_ge(weights_in, 3 * 16)

            def first(n, u, k):
                for a in range(CC):
                    act.wait_ge(y_turned, CC * n + a + 1)
                    nc.scalar.copy(yt[:, 0, a, :], ps_t[a][:, :]).then_inc(yt_made, 1)

            def second(n, u, k):
                act.wait_ge(lo_made, CC * n + PRIMED)
                for a in range(CC):
                    act.wait_ge(xn_turned, CC * n + a + 1)
                    nc.scalar.copy(xt[:, 0, a, :], ps_u[a][:, :]).then_inc(xt_made, 1)
                act.wait_ge(routed, n + 1)
                nc.scalar.activation(by_expert[:, :], ps_r[0:E, :], ACT.Identity,
                                     bias=br_sb[:, 0:1]).then_inc(by_expert_made, 1)
            staged(act, first, second)

        @block.vector
        def _(dve):
            NSTEP = LN_STEPS
            dve.sem_inc(logits_made, PRIMED)
            dve.sem_inc(x1_made, PRIMED)

            def first(n, u, k):
                steps = Steps(dve, dve_step, n * NSTEP)
                dve.wait_ge(y_loaded[u], 32 * (k + 1))
                for i in range(2):
                    dve.wait_ge(mixed, 2 * n + i + 1)
                    part = x_in[:, u, 2 * i:2 * i + 2, :].rearrange("p j d -> p (j d)")
                    nc.vector.tensor_tensor(out=part, in0=ps_x[i][:, :], in1=part, op=ALU.add).then_inc(x1_made, 1)
                dve.wait_ge(x1_made, 2 * n + 2 + PRIMED)
                dve.sem_inc(dve_alone, 1)
                layer_norm_stats(nc, steps, x_in[:, u, :, :], stats, mv, var, rstd, tmp, dve_alone)
                for j in range(TILES):
                    last = nc.vector.tensor_scalar(y_in[:, u, j, :], x_in[:, u, j, :], mv[:, j, 0:1],
                                                   rstd[:, j:j + 1], ALU.subtract, ALU.mult)
                last.then_inc(xn_made, 1)
                dve.wait_ge(xn_made, n + 1)
                dve.sem_inc(dve_alone, 1)

            def second(n, u, k):
                dve.wait_ge(xt_stored, 32 * n + 32 * PRIMED)
                for a in range(CC):
                    dve.wait_ge(xt_made, CC * n + a + 1)
                    nc.vector.tensor_copy(xt_hi[:, 0, a, :], xt[:, 0, a, :]).then_inc(hi_made, 1)
                dve.wait_ge(logits_turned, n + 1)
                nc.vector.tensor_copy(logits[:, bass.ds(n * TILES, TILES), :],
                                      ps_l[:, 0:TILES * E].rearrange("p (j e) -> p j e", e=E)
                                      ).then_inc(logits_made, 1)
            staged(dve, first, second)

        @block.tensor
        def _(pe):
            pe.wait_ge(ident_made, 2)
            pe.wait_ge(weights_in, 3 * 16)

            def turn(banks, u):
                for a in range(CC):
                    for j in range(TILES):
                        last = nc.tensor.transpose(banks[a][:, j * P:(j + 1) * P],
                                                   y_in[:, u, j, a * P:(a + 1) * P], ident[:, :])
                    yield last

            def first(n, u, k):
                pe.wait_ge(y_loaded[u], 32 * (k + 1))
                for last in turn(ps_t, u):
                    last.then_inc(y_turned, 1)
                pe.wait_ge(yt_made, CC * n + CC)
                pe.sem_inc(pe_alone, 1)
                pe.wait_ge(x1_made, 2 * n + PRIMED)
                for j in range(TILES):
                    for a in range(CC):
                        last = nc.tensor.matmul(ps_x[j // 2][:, (j % 2) * C:(j % 2 + 1) * C],
                                                yt[:, 0, a, j * P:(j + 1) * P], wc_sb[:, a, :],
                                                start=(j % 2 == 0 and a == 0), stop=(a == CC - 1),
                                                skip_group_check=True)
                    if j % 2:
                        last.then_inc(mixed, 1)

            def second(n, u, k):
                pe.wait_ge(xn_made, n + 1)
                for last in turn(ps_u, u):
                    last.then_inc(xn_turned, 1)
                pe.wait_ge(xt_made, CC * n + CC)
                for a in range(CC):
                    last = nc.tensor.matmul(ps_r[0:E, :], wr_sb[:, a, :], xt[:, 0, a, :],
                                            start=(a == 0), stop=(a == CC - 1))
                last.then_inc(routed, 1)
                pe.wait_ge(by_expert_made, n + 1)
                pe.sem_inc(pe_alone, 1)
                pe.wait_ge(logits_made, n + PRIMED)
                pe.sem_inc(pe_alone, 1)
                for j in range(TILES):
                    last = nc.tensor.transpose(ps_l[:, j * E:(j + 1) * E], by_expert[:, j * P:(j + 1) * P],
                                               ident[0:E, 0:E])
                last.then_inc(logits_turned, 1)
            staged(pe, first, second)


def experts(nc, w_sb, logits, b1, b2, xt_dram, x1_dram, out):
    w_hi, w_lo = w_sb
    FO = F // P
    HALF = NB // 2 * W_PER_LOOP
    with ExitStack() as ctx:
        def sb(name, shape, dt):
            return ctx.enter_context(nc.sbuf_tensor(name, shape, dt))

        def sem(name):
            return ctx.enter_context(nc.semaphore(name))

        b1_sb = sb("b1_sb", [P, E, FO], F32)
        b2_sb = sb("b2_sb", [P, E, C], F32)
        rank = sb("rank", [P, E], F32)
        hot = [sb(f"hot{i}", [P, NB * TILES, E], F32) for i in range(2)]
        score = sb("score", [P, NB * TILES, E], F32)
        rest = sb("rest4", [P, NB * TILES, E], F32)
        best = [sb(f"best{i}", [P, NB * TILES], F32) for i in range(2)]
        top = sb("top", [P, NB * TILES], F32)
        ratio = sb("ratio", [P, NB * TILES], F32)
        share = [sb(f"share{i}", [P, NB * TILES], F32) for i in range(2)]
        gates = sb("gates", [P, NB * TILES, E], F32)
        gate = sb("gate", [P, 2, TILES, E], F32)
        xt_hi = sb("xt_hi4", [P, 2, CC, TB], F32R)
        xt_lo = sb("xt_lo4", [P, 2, CC, TB], F32R)
        acc = sb("acc", [P, 2, TILES, C], F32)
        h = sb("h", [P, 2, TB], F32)
        h_hi = sb("h_hi", [P, 2, TB], F32R)
        h_lo = sb("h_lo", [P, 2, TB], F32R)
        ps_h = [ctx.enter_context(nc.psum_tensor(f"ps_h{i}", [P, 512], F32)) for i in range(2)]
        ps_y = [ctx.enter_context(nc.psum_tensor(f"ps_y{i}", [P, 512], F32)) for i in range(4)]

        biases_in = sem("biases_in")
        block_in = [sem(f"block_in{u}") for u in range(2)]
        rank_set = sem("rank_set")
        gate_step = sem("gate_step")
        distance_made = sem("distance_made")
        ratio_made = sem("ratio_made")
        gate_copied = sem("gate_copied")
        h_psum = sem("h_psum")
        h_made = sem("h_made")
        lo_made = sem("lo_made4")
        y_complete = sem("y_complete")
        acc_step = sem("acc_step")
        sp_alone = sem("sp_alone4")
        out_stored = [sem(f"out_stored{u}") for u in range(2)]

        out_v = out.rearrange("b (c j p) d -> (b c) p j d", p=P, j=TILES)
        x1_v = x1_dram.rearrange("(n j p) d -> n p j d", p=P, j=TILES)
        LAYERS = [(e, f) for e in range(E) for f in range(FO)]
        NL = len(LAYERS)
        GATHER = 2 * TILES
        ACCS = GATHER * E

        block = ctx.enter_context(nc.Block())

        @block.sync
        def _(sp):
            def load(n, u):
                sp.dma_start(xt_hi[:, u, :, :].bitcast(F32), xt_dram[0, n, :, :, :]).then_inc(block_in[u], 16)
                sp.dma_start(xt_lo[:, u, :, :].bitcast(F32), xt_dram[1, n, :, :, :]).then_inc(block_in[u], 16)
                sp.dma_start(acc[:, u, :, :], x1_v[n, :, :, :]).then_inc(block_in[u], 16)

            def store(n, u, k):
                sp.wait_ge(acc_step, ACCS * n + ACCS + 2 * GATHER)
                sp.sem_inc(sp_alone, 1)
                sp.dma_start(out_v[n, :, :, :], acc[:, u, :, :]).then_inc(out_stored[u], 16)

            load(0, 0)
            with nc.allow_non_contiguous_dma(reason="small biases, turned once"):
                sp.dma_start(b1_sb[:, :, :].rearrange("p e f -> p (e f)"),
                             b1.rearrange("e (f p) -> p (e f)", p=P)).then_inc(biases_in, 16)
            sp.dma_start(b2_sb[:, :, :].rearrange("p e c -> p (e c)"),
                         b2.rearrange("(a e) c -> a (e c)", a=1).broadcast_to([P, E * C])).then_inc(biases_in, 16)
            load(1, 1)
            with sp.Fori(0, NB // 2 - 1) as k:
                for u in range(2):
                    store(2 * k + u, u, k)
                    sp.wait_ge(out_stored[u], 16 * (k + 1))
                    sp.sem_inc(sp_alone, 1)
                    load(2 * k + 2 + u, u)
            for u in range(2):
                store(NB - 2 + u, u, NB // 2 - 1)
            for u in range(2):
                sp.wait_ge(out_stored[u], 16 * NB // 2)

        @block.scalar
        def _(act):
            act.wait_ge(distance_made, 1)
            nc.scalar.activation(ratio[:, :], ratio[:, :], ACT.Exp).then_inc(ratio_made, 1)
            act.wait_ge(biases_in, 32)
            act.sem_inc(h_made, 2 * PRIMED)
            with act.Fori(0, NB // 2) as k:
                for u in range(2):
                    n = 2 * k + u
                    for i, (e, f) in enumerate(LAYERS):
                        act.wait_ge(lo_made, NL * n + i - 1 + 2 * PRIMED)
                        act.wait_ge(h_psum, NL * n + i + 1)
                        nc.scalar.activation(h_hi[:, i % 2, :], ps_h[i % 2][:, :], ACT.Relu,
                                             bias=b1_sb[:, e, f:f + 1])
                        nc.scalar.activation(h[:, i % 2, :], ps_h[i % 2][:, :], ACT.Relu,
                                             bias=b1_sb[:, e, f:f + 1]).then_inc(h_made, 1)

        @block.vector
        def _(dve):
            dve.sem_inc(lo_made, 2 * PRIMED)
            dve.sem_inc(acc_step, 2 * GATHER)
            steps = Steps(dve, gate_step)
            for e in range(E):
                last = nc.vector.memset(rank[:, e:e + 1], float(E - e))
            steps.done(last)
            tokens = [P, NB * TILES, E]
            for i in range(2):
                values = logits if i == 0 else rest
                steps.done(nc.vector.tensor_reduce(best[i][:, :], values[:, :, :], AX.X, ALU.max))
                steps.done(nc.vector.tensor_tensor(out=score[:, :, :], in0=values[:, :, :],
                                                   in1=best[i][:, :].unsqueeze(2).broadcast_to(tokens),
                                                   op=ALU.is_equal))
                steps.done(nc.vector.tensor_tensor(out=score[:, :, :], in0=score[:, :, :],
                                                   in1=rank[:, :].unsqueeze(1).broadcast_to(tokens), op=ALU.mult))
                steps.done(nc.vector.tensor_reduce(top[:, :], score[:, :, :], AX.X, ALU.max))
                steps.done(nc.vector.tensor_tensor(out=hot[i][:, :, :], in0=score[:, :, :],
                                                   in1=top[:, :].unsqueeze(2).broadcast_to(tokens),
                                                   op=ALU.is_equal))
                if i == 0:
                    steps.done(nc.vector.scalar_tensor_tensor(out=rest[:, :, :], in0=hot[0][:, :, :], scalar=NEG,
                                                              in1=logits[:, :, :], op0=ALU.mult, op1=ALU.add))
            nc.vector.tensor_tensor(out=ratio[:, :], in0=best[1][:, :], in1=best[0][:, :],
                                    op=ALU.subtract).then_inc(distance_made, 1)
            dve.wait_ge(ratio_made, 1)
            steps.done(nc.vector.tensor_scalar(share[1][:, :], ratio[:, :], 1.0, None, ALU.add))
            steps.done(nc.vector.reciprocal(share[0][:, :], share[1][:, :]))
            steps.done(nc.vector.tensor_tensor(out=share[1][:, :], in0=ratio[:, :], in1=share[0][:, :], op=ALU.mult))
            for i in range(2):
                steps.done(nc.vector.tensor_tensor(out=hot[i][:, :, :], in0=hot[i][:, :, :],
                                                   in1=share[i][:, :].unsqueeze(2).broadcast_to(tokens),
                                                   op=ALU.mult))
            steps.done(nc.vector.tensor_tensor(out=gates[:, :, :], in0=hot[0][:, :, :], in1=hot[1][:, :, :],
                                               op=ALU.add))
            dve.wait_ge(biases_in, 32)

            def low_half(n, i):
                dve.wait_ge(h_made, NL * n + i + 1 + 2 * PRIMED)
                nc.vector.tensor_tensor(out=h_lo[:, i % 2, :], in0=h[:, i % 2, :],
                                        in1=h_hi[:, i % 2, :].bitcast(F32),
                                        op=ALU.subtract).then_inc(lo_made, 1)

            def gather(n, u, e, product, tiles):
                if product:
                    dve.wait_ge(y_complete, E * n + e + 1)
                for j in tiles:
                    m = GATHER * e + TILES * product + j
                    if m >= TILES:
                        dve.wait_ge(acc_step, ACCS * n + m - TILES + 1 + 2 * GATHER)
                    src = (ps_y[2 * (e % 2) + j // 2][:, (j % 2) * C:(j % 2 + 1) * C] if product else
                           b2_sb[:, e, :])
                    nc.vector.scalar_tensor_tensor(out=acc[:, u, j, :], in0=src, scalar=gate[:, u, j, e:e + 1],
                                                   in1=acc[:, u, j, :], op0=ALU.mult,
                                                   op1=ALU.add).then_inc(acc_step, 1)

            def body(n, u, k, start_next):
                dve.wait_ge(block_in[u], 3 * 16 * (k + 1))
                nc.vector.tensor_copy(gate[:, u, :, :],
                                      gates[:, bass.ds(n * TILES, TILES), :]).then_inc(gate_copied, 1)
                dve.wait_ge(gate_copied, n + 1)
                for i, (e, f) in enumerate(LAYERS):
                    if i:
                        low_half(n, i)
                    if f in (1, 2) and e > 0:
                        gather(n, u, e - 1, 1, range(2 * f - 2, 2 * f))
                    if f == FO - 1:
                        gather(n, u, e, 0, range(TILES))
                start_next()
                gather(n, u, E - 1, 1, range(TILES))
            pipeline(dve, lambda n, u, k: low_half(n, 0), body)

        @block.tensor
        def _(pe):
            def first_layer(n, u, i):
                e, f = LAYERS[i]
                pe.wait_ge(h_made, NL * n + i - 1 + 2 * PRIMED)
                for a in range(CC):
                    cols = slice(f * P, (f + 1) * P)
                    last = three_products(nc, ps_h[i % 2][:, :],
                                          (w_hi[:, e * CC + a, cols], w_lo[:, e * CC + a, cols]),
                                          (xt_hi[:, u, a, :], xt_lo[:, u, a, :]), a == 0, a == CC - 1)
                last.then_inc(h_psum, 1)

            def second_layer(n, i):
                e, f = LAYERS[i]
                pe.wait_ge(lo_made, NL * n + i + 1 + 2 * PRIMED)
                if f == 0:
                    pe.wait_ge(acc_step, ACCS * n + GATHER * (e - 1) + 2 * GATHER)
                chunk = HALF + e * 2 + f // 2
                cols = slice((f % 2) * C, (f % 2 + 1) * C)
                for j in range(TILES):
                    rows = slice(j * P, (j + 1) * P)
                    last = three_products(nc, ps_y[2 * (e % 2) + j // 2][:, (j % 2) * C:(j % 2 + 1) * C],
                                          (h_hi[:, i % 2, rows], h_lo[:, i % 2, rows]),
                                          (w_hi[:, chunk, cols], w_lo[:, chunk, cols]),
                                          f == 0 and j % 2 == 0, f == FO - 1)
                if f == FO - 1:
                    last.then_inc(y_complete, 1)

            def start(n, u, k):
                pe.wait_ge(block_in[u], 3 * 16 * (k + 1))
                first_layer(n, u, 0)

            def body(n, u, k, start_next):
                for i in range(1, NL):
                    first_layer(n, u, i)
                    second_layer(n, i - 1)
                start_next()
                second_layer(n, NL - 1)
            pipeline(pe, start, body)


def transformer_block(nc, w, out):
    parts_dram = nc.dram_tensor("parts_dram", (2, PARTS, 2, DHE, H, B * T), BF16).ap()
    v_dram = nc.dram_tensor("v_dram", (HG, P, B * T // P, GH, VW), F32).ap()
    minus_dram = [nc.dram_tensor(f"minus_dram{late}", (PARTS, GH, n, P), BF16).ap()
                  for late, n in enumerate((EARLY, QT - EARLY))]
    y_dram = nc.dram_tensor("y_dram", (B * T, C), F32).ap()
    project(nc, w["L0_attn_x"], (w["L0_attn_Wq_down"], w["L0_attn_Wk_down"], w["L0_attn_Wv_down"]),
            ((w["L0_attn_Wq_up_c"], w["L0_attn_Wq_up_e"]), (w["L0_attn_Wk_up_c"], w["L0_attn_Wk_up_e"]),
             (w["L0_attn_Wv_up"],)), w["rope_cos"], w["rope_sin"], parts_dram, v_dram)
    attend(nc, parts_dram, v_dram, minus_dram, y_dram)
    xt_dram = nc.dram_tensor("xt_dram", (2, NB, P, CC, TB), F32).ap()
    x1_dram = nc.dram_tensor("x1_dram", (B * T, C), F32).ap()
    with ExitStack() as ctx:
        w_sb = [ctx.enter_context(nc.sbuf_tensor(f"experts_{half}", [P, 2 * E * F * C // (P * WCH), WCH], F32R))
                for half in ("hi", "lo")]
        logits = ctx.enter_context(nc.sbuf_tensor("logits", [P, NB * TILES, E], F32))
        mix(nc, w["L0_attn_x"], y_dram, w["L0_attn_Wc"], w["L0_ffn_Wr"], w["L0_ffn_br"], w["L0_ffn_W1"],
            w["L0_ffn_W2"], w_sb, logits, xt_dram, x1_dram)
        experts(nc, w_sb, logits, w["L0_ffn_b1"], w["L0_ffn_b2"], xt_dram, x1_dram, out)


_INS = ["L0_attn_x", "L0_attn_Wq_down", "L0_attn_Wk_down", "L0_attn_Wv_down", "L0_attn_Wq_up_c",
        "L0_attn_Wq_up_e", "L0_attn_Wk_up_c", "L0_attn_Wk_up_e", "L0_attn_Wv_up", "L0_attn_Wc",
        "L0_ffn_Wr", "L0_ffn_br", "L0_ffn_W1", "L0_ffn_b1", "L0_ffn_W2", "L0_ffn_b2"]


def kernel(**inputs):
    import numpy as np
    import concourse.bacc as bacc
    from concourse.bass_utils import run_bass_kernel_spmd

    nc = bacc.Bacc("TRN2", target_bir_lowering=False, num_devices=1)
    arrays = {name: np.ascontiguousarray(inputs[name]) for name in _INS}
    inverse = np.float32(1.0) / np.float32(10000.0) ** (np.arange(0, DHE, 2, dtype=np.float32) / np.float32(DHE))
    angle = np.arange(T, dtype=np.float32)[None, :] * np.concatenate((inverse, inverse))[:, None]
    sign = np.where(np.arange(DHE) % 2 == 0, np.float32(-1.0), np.float32(1.0))
    arrays["rope_cos"] = np.repeat(np.cos(angle).astype(np.float32), H, axis=0)
    arrays["rope_sin"] = np.repeat((np.sin(angle) * sign[:, None]).astype(np.float32), H, axis=0)
    args = {name: nc.dram_tensor(f"in_{name}", a.shape, mybir.dt.from_np(a.dtype), kind="ExternalInput").ap()
            for name, a in arrays.items()}
    out = nc.dram_tensor("out_0", (B, T, C), F32, kind="ExternalOutput").ap()
    transformer_block(nc, args, out)
    feeds = {f"in_{name}": a for name, a in arrays.items()}
    return run_bass_kernel_spmd(nc, [feeds], core_ids=[0]).results[0]["out_0"]
```

```python
from contextlib import ExitStack

import concourse.bass as bass
from concourse import mybir

P = 128
B, T, C = 4, 2048, 256
H, L, DH = 16, 64, 16
DHE = DH // 2
E, F = 8, 512
EPS = 1e-5
TB = 512
TILES = TB // P
CH = T // TB
NB = B * CH
QT = T // P
CC = C // P
HP = H // 2
GH = 4
HG = H // GH
NG = B * HG
VW = DH + 1
PARTS = 3

PRIMED = 1

ALU = mybir.AluOpType
ACT = mybir.ActivationFunctionType
AX = mybir.AxisListType
F32 = mybir.dt.float32
F32R = mybir.dt.float32r
BF16 = mybir.dt.bfloat16
I32 = mybir.dt.int32
RSQRT_MAGIC = float(0x5F3759DF)


class Steps:

    def __init__(self, engine, sem, base=0):
        self.engine, self.sem, self.base, self.n = engine, sem, base, 0

    def done(self, instruction):
        instruction.then_inc(self.sem, 1)
        self.n += 1
        self.engine.wait_ge(self.sem, self.base + self.n)


def layer_norm_stats(nc, steps, x, stats, mv, var, rstd, tmp, alone):
    for j in range(TILES):
        last = nc.vector.bn_stats(stats[:, j, :], x[:, j, :])
    steps.done(last)
    steps.engine.sem_inc(alone, 1)
    for j in range(TILES):
        last = nc.vector.bn_aggr(mv[:, j, :], stats[:, j, :])
    steps.done(last)
    steps.done(nc.vector.tensor_scalar(var[:, :], mv[:, :, 1], EPS, None, ALU.add))
    steps.done(nc.vector.tensor_scalar(tmp[:, :].bitcast(I32), var[:, :].bitcast(I32), 1, None,
                                       ALU.logical_shift_right))
    steps.done(nc.vector.tensor_scalar(rstd[:, :].bitcast(I32), tmp[:, :].bitcast(I32), -1.0, RSQRT_MAGIC,
                                       ALU.mult, ALU.add))
    for _ in range(3):
        steps.done(nc.vector.tensor_tensor(tmp[:, :], rstd[:, :], rstd[:, :], ALU.mult))
        steps.done(nc.vector.scalar_tensor_tensor(out=tmp[:, :], in0=tmp[:, :], scalar=-0.5, in1=var[:, :],
                                                  op0=ALU.mult, op1=ALU.mult))
        steps.done(nc.vector.scalar_tensor_tensor(out=rstd[:, :], in0=tmp[:, :], scalar=1.5, in1=rstd[:, :],
                                                  op0=ALU.add, op1=ALU.mult))


LN_STEPS = 5 + 9


def three_products(nc, out, stationary, moving, first, last):
    (s_hi, s_lo), (m_hi, m_lo) = stationary, moving
    nc.tensor.matmul(out, s_lo, m_hi, start=first, stop=False, skip_group_check=True)
    nc.tensor.matmul(out, s_hi, m_lo, start=False, stop=False, skip_group_check=True)
    return nc.tensor.matmul(out, s_hi, m_hi, start=False, stop=last, skip_group_check=True)


def make_identity(nc, eng, ident, sem):
    nc.gpsimd.memset(ident[:, :], 0.0).then_inc(sem, 1)
    eng.wait_ge(sem, 1)
    nc.gpsimd.affine_select(out=ident[:, :], in_=ident[:, :], compare_op=ALU.not_equal, fill=1.0, base=0,
                            pattern=[[-1, P]], channel_multiplier=1).then_inc(sem, 1)


def pipeline(eng, first, body):
    first(0, 0, 0)
    with eng.Fori(0, NB // 2 - 1) as k:
        body(2 * k, 0, k, lambda: first(2 * k + 1, 1, k))
        body(2 * k + 1, 1, k, lambda: first(2 * k + 2, 0, k + 1))
    last = NB // 2 - 1
    body(NB - 2, 0, last, lambda: first(NB - 1, 1, last))
    body(NB - 1, 1, last, lambda: None)


def project(nc, x, downs, ups, rope_cos, rope_sin, parts_dram, v_dram):
    NDOWN = 3
    with ExitStack() as ctx:
        def sb(name, shape, dt):
            return ctx.enter_context(nc.sbuf_tensor(name, shape, dt))

        def sem(name):
            return ctx.enter_context(nc.semaphore(name))

        def bank(name):
            return ctx.enter_context(nc.psum_tensor(name, [P, 512], F32))

        ident = sb("ident1", [P, P], F32)
        down = sb("down", [P, NDOWN, CC, H * L], F32)
        down_t = sb("down_t", [P, NDOWN, HP, C], F32)
        up = sb("up", [P, 2, 2, 2, DHE], F32)
        up_v = sb("up_v", [P, 2, DH], F32)
        w_hi = sb("w_hi", [P, NDOWN, CC, C], F32R)
        w_lo = sb("w_lo", [P, NDOWN, CC, C], F32R)
        cos = sb("cos", [P, T], F32)
        sin = sb("sin", [P, T], F32)
        xin = sb("xin", [P, 2, TILES, C], F32)
        xn = sb("xn", [P, 2, TILES, C], F32)
        stats = sb("stats", [P, TILES, 6], F32)
        mv = sb("mv", [P, TILES, 2], F32)
        var = sb("var", [P, TILES], F32)
        rstd = sb("rstd", [P, TILES], F32)
        tmp = sb("tmp", [P, TILES], F32)
        xt_hi = sb("xt_hi", [P, 2, CC, TB], F32R)
        xt_lo = sb("xt_lo", [P, 2, CC, TB], F32R)
        raw = sb("raw", [P, 2, TB], F32)
        swapped = sb("swapped", [P, 2, TB], F32)
        turned = sb("turned", [P, 2, TB], F32)
        rest = sb("rest", [P, 4, TB], F32)
        parts = sb("parts", [P, 2, 4, PARTS, TB], BF16)
        v_out = sb("v_out", [P, 2, HG, TILES, GH, VW], F32)

        ps_t = [bank(f"ps_t{i}") for i in range(CC)]
        ps_p = [bank(f"ps_p{i}") for i in range(4)]
        ps_v = [bank(f"ps_v{i}") for i in range(2)]

        ident_made = sem("ident_made")
        up_clear = sem("up_clear")
        ups_in = sem("ups_in")
        downs_in = sem("downs_in")
        rope_in = sem("rope_in")
        down_turned = sem("down_turned")
        down_copied = sem("down_copied")
        folded = sem("folded")
        w_hi_made = sem("w_hi_made")
        w_made = sem("w_made")
        ones_set = sem("ones_set")
        x_in = [sem(f"x_in{u}") for u in range(2)]
        dve_step = sem("dve_step1")
        rest_step = sem("rest_step")
        dve_alone = sem("dve_alone1")
        pool_alone = sem("pool_alone1")
        xn_made = sem("xn_made1")
        xt_turned = sem("xt_turned1")
        xt_hi_made = sem("xt_hi_made1")
        xt_lo_made = sem("xt_lo_made1")
        projected = sem("projected")
        v_projected = sem("v_projected")
        raw_copied = sem("raw_copied")
        part1_made = sem("part1_made")
        plain_rest = sem("plain_rest")
        part2_made = sem("part2_made")
        part3_made = sem("part3_made")
        swap_made = sem("swap_made")
        sine_made = sem("sine_made")
        raw_read = sem("raw_read")
        turned_made = sem("turned_made")
        v_copied = sem("v_copied")
        parts_out = [sem(f"parts_out{u}") for u in range(2)]
        v_stored = [sem(f"v_stored{u}") for u in range(2)]

        x_v = x.rearrange("b (c j p) d -> (b c) p j d", p=P, j=TILES)
        PROJ = [(0, 0), (1, 0), (0, 1), (1, 1)]

        block = ctx.enter_context(nc.Block())

        @block.sync
        def _(sp):
            for u in range(2):
                sp.sem_inc(parts_out[u], 16 * PRIMED)
                sp.sem_inc(v_stored[u], 16 * PRIMED)
            for m in range(NDOWN):
                sp.dma_start(down[:, m, :, :], downs[m].rearrange("(a p) n -> p a n", p=P)).then_inc(downs_in, 16)
            for u in range(2):
                sp.dma_start(xin[:, u, :, :], x_v[u, :, :, :]).then_inc(x_in[u], 16)
            sp.wait_ge(up_clear, 2)
            for m, halves in enumerate(ups):
                for half, w in enumerate(halves):
                    for h2 in range(2):
                        rows = slice(h2 * L, (h2 + 1) * L)
                        to = up[rows, m, half, h2, :] if m < 2 else up_v[rows, h2, :]
                        sp.dma_start(to, w).then_inc(ups_in, 16)

            def load_x(n, u):
                sp.dma_start(xin[:, u, :, :], x_v[n, :, :, :]).then_inc(x_in[u], 16)

            def store(n, u):
                sp.wait_ge(part3_made, 4 * n + 4 + PRIMED)
                for i, (t, half) in enumerate(PROJ):
                    to = parts_dram[t, :, half, :, :, bass.ds(n * TB, TB)]
                    sp.dma_start(to.rearrange("s j h n -> (j h) s n"),
                                 parts[:, u, i, :, :]).then_inc(parts_out[u], 16)
                sp.wait_ge(v_copied, 2 * n + 2 + PRIMED)
                sp.dma_start(v_dram[:, :, bass.ds(n * TILES, TILES), :, :].rearrange("a p j h d -> p a (j h d)"),
                             v_out[:, u, :, :, :, :].rearrange("p a j h d -> p a (j h d)")).then_inc(v_stored[u], 16)

            with sp.Fori(0, NB // 2 - 1) as k:
                for u in range(2):
                    sp.wait_ge(xn_made, 2 * k + u + 1)
                    load_x(2 * k + 2 + u, u)
                    store(2 * k + u, u)
            for u in range(2):
                store(NB - 2 + u, u)
            for u in range(2):
                sp.wait_ge(parts_out[u], NB // 2 * 4 * 16 + 16 * PRIMED)
                sp.wait_ge(v_stored[u], NB // 2 * 16 + 16 * PRIMED)

        @block.gpsimd
        def _(pool):
            pool.sem_inc(part3_made, PRIMED)
            nc.gpsimd.memset(up[:, :, :, :, :], 0.0).then_inc(up_clear, 1)
            nc.gpsimd.memset(up_v[:, :, :], 0.0).then_inc(up_clear, 1)
            make_identity(nc, pool, ident, ident_made)
            nc.gpsimd.memset(v_out[:, :, :, :, :, :], 1.0).then_inc(ones_set, 1)
            for table, src in ((cos, rope_cos), (sin, rope_sin)):
                pool.dma_start(table[:, :], src).then_inc(rope_in, 16)
            pool.wait_ge(rope_in, 2 * 16)
            with pool.Fori(0, B) as b:
                with pool.Fori(0, CH // 2) as c2:
                    for u in range(2):
                        n = (b * (CH // 2) + c2) * 2 + u
                        for i in range(2):
                            pool.wait_ge(swap_made, 2 * n + i + 1)
                            pool.sem_inc(pool_alone, 1)
                            nc.gpsimd.tensor_tensor(out=swapped[:, i, :], in0=swapped[:, i, :],
                                                    in1=sin[:, bass.ds((c2 * 2 + u) * TB, TB)],
                                                    op=ALU.mult).then_inc(sine_made, 1)
                        for i in range(4):
                            pool.wait_ge(part2_made, 4 * n + i + 1)
                            if i == 0:
                                pool.wait_ge(parts_out[u], (b * (CH // 2) + c2) * (4 * 16) + 16 * PRIMED)
                            nc.gpsimd.tensor_tensor(out=parts[:, u, i, 2, :], in0=rest[:, i, :],
                                                    in1=parts[:, u, i, 1, :],
                                                    op=ALU.subtract).then_inc(part3_made, 1)

        @block.scalar
        def _(act):
            act.sem_inc(raw_copied, PRIMED)
            act.sem_inc(v_copied, PRIMED)
            for g in range(NDOWN * 4):
                act.wait_ge(down_turned, g + 1)
                nc.scalar.copy(down_t[:, g // 4, 2 * (g % 4):2 * (g % 4) + 2, :].rearrange("p a n -> p (a n)"),
                               ps_p[g % 4][:, :]).then_inc(down_copied, 1)
            for m in range(NDOWN):
                act.wait_ge(folded, m + 1)
                nc.scalar.copy(w_hi[:, m, :, :].rearrange("p a n -> p (a n)"), ps_p[m][:, :]).then_inc(w_hi_made, 1)
            act.wait_ge(ones_set, 1)

            def turn_rows(n, u, k):
                for a in range(CC):
                    act.wait_ge(xt_turned, CC * n + a + 1 + PRIMED)
                    nc.scalar.copy(xt_hi[:, u, a, :], ps_t[a][:, :]).then_inc(xt_hi_made, 1)

            def body(n, u, k, start_next):
                act.wait_ge(parts_out[u], k * (4 * 16) + 16 * PRIMED)
                act.wait_ge(v_stored[u], k * 16 + 16 * PRIMED)
                for i in range(2):
                    act.wait_ge(projected, 4 * n + i + 1)
                    nc.scalar.copy(parts[:, u, i, 0, :], ps_p[i][:, :]).then_inc(part1_made, 1)
                act.wait_ge(raw_read, 2 * n + PRIMED)
                for i in range(2):
                    act.wait_ge(projected, 4 * n + i + 3)
                    nc.scalar.copy(raw[:, i, :], ps_p[2 + i][:, :]).then_inc(raw_copied, 1)
                for j in range(2):
                    act.wait_ge(v_projected, 2 * n + j + 1)
                    for s in range(2):
                        last = nc.scalar.copy(
                            v_out[:, u, :, 2 * j + s, :, 0:DH],
                            ps_v[j][:, s * C:(s + 1) * C].rearrange("p (a h d) -> p a h d", a=HG, h=GH))
                    last.then_inc(v_copied, 1)
                start_next()
                for i in range(2):
                    act.wait_ge(turned_made, 2 * n + i + 1)
                    nc.scalar.copy(parts[:, u, 2 + i, 0, :], turned[:, i, :]).then_inc(part1_made, 1)
            pipeline(act, turn_rows, body)

        @block.vector
        def _(dve):
            for s in (raw_read, plain_rest, xt_lo_made):
                dve.sem_inc(s, PRIMED)

            def fold_low():
                for m in range(NDOWN):
                    dve.wait_ge(w_hi_made, m + 1)
                    nc.vector.tensor_tensor(out=w_lo[:, m, :, :].rearrange("p a n -> p (a n)"), in0=ps_p[m][:, :],
                                            in1=w_hi[:, m, :, :].bitcast(F32).rearrange("p a n -> p (a n)"),
                                            op=ALU.subtract).then_inc(w_made, 1)
                dve.wait_ge(rope_in, 2 * 16)

            def normalise(n, u, k):
                steps = Steps(dve, dve_step, n * LN_STEPS)
                dve.wait_ge(x_in[u], 16 * k + 16)
                layer_norm_stats(nc, steps, xin[:, u, :, :], stats, mv, var, rstd, tmp, dve_alone)
                dve.wait_ge(xt_turned, CC * n + PRIMED)
                for j in range(TILES):
                    last = nc.vector.tensor_scalar(xn[:, u, j, :], xin[:, u, j, :], mv[:, j, 0:1],
                                                   rstd[:, j:j + 1], ALU.subtract, ALU.mult)
                last.then_inc(xn_made, 1)
                if isinstance(n, int) and n == 0:
                    fold_low()

            def body(n, u, k, start_next):
                for a in range(CC):
                    dve.wait_ge(xt_hi_made, CC * n + a + 1)
                    nc.vector.tensor_tensor(out=xt_lo[:, u, a, :], in0=ps_t[a][:, :],
                                            in1=xt_hi[:, u, a, :].bitcast(F32),
                                            op=ALU.subtract).then_inc(xt_lo_made, 1)
                start_next()
                for i in range(2):
                    dve.wait_ge(raw_copied, 2 * n + i + 1 + PRIMED)
                    dve.sem_inc(dve_alone, 1)
                    nc.vector.stream_shuffle(swapped[:, i, :], raw[:, i, :],
                                             [j ^ H for j in range(32)]).then_inc(swap_made, 1)
                    nc.vector.tensor_tensor(out=turned[:, i, :], in0=raw[:, i, :],
                                            in1=cos[:, bass.ds(n % CH * TB, TB)],
                                            op=ALU.mult).then_inc(raw_read, 1)
                dve.wait_ge(part3_made, 4 * n + PRIMED)
                for i in range(2):
                    dve.wait_ge(part1_made, 4 * n + i + 1)
                    last = nc.vector.tensor_tensor(out=rest[:, i, :], in0=ps_p[i][:, :],
                                                   in1=parts[:, u, i, 0, :], op=ALU.subtract)
                    last.then_inc(plain_rest, 1)
                    dve.wait_ge(plain_rest, 2 * n + i + 1 + PRIMED)
                    nc.vector.tensor_copy(parts[:, u, i, 1, :], rest[:, i, :]).then_inc(part2_made, 1)
                for i in range(2):
                    dve.wait_ge(raw_read, 2 * n + i + 1 + PRIMED)
                    dve.wait_ge(sine_made, 2 * n + i + 1)
                    nc.vector.tensor_tensor(out=turned[:, i, :], in0=turned[:, i, :],
                                            in1=swapped[:, i, :], op=ALU.add).then_inc(turned_made, 1)
                steps = Steps(dve, rest_step, 2 * n)
                for i in range(2):
                    dve.wait_ge(part1_made, 4 * n + i + 3)
                    steps.done(nc.vector.tensor_tensor(out=rest[:, 2 + i, :], in0=turned[:, i, :],
                                                       in1=parts[:, u, 2 + i, 0, :], op=ALU.subtract))
                    nc.vector.tensor_copy(parts[:, u, 2 + i, 1, :], rest[:, 2 + i, :]).then_inc(part2_made, 1)
            pipeline(dve, normalise, body)

        @block.tensor
        def _(pe):
            pe.sem_inc(xt_turned, PRIMED)
            pe.wait_ge(ident_made, 2)
            pe.wait_ge(downs_in, NDOWN * 16)
            for g in range(NDOWN * 4):
                if g >= 4:
                    pe.wait_ge(down_copied, g - 3)
                for s in range(2):
                    pair = 2 * (g % 4) + s
                    for a in range(CC):
                        at = s * C + a * P
                        last = nc.tensor.transpose(ps_p[g % 4][:, at:at + P],
                                                   down[:, g // 4, a, pair * P:(pair + 1) * P], ident[:, :])
                last.then_inc(down_turned, 1)
            pe.wait_ge(down_copied, NDOWN * 4)
            pe.wait_ge(ups_in, 5 * 2 * 16)
            for m in range(NDOWN):
                for a in range(CC):
                    for pair in range(HP):
                        to = ps_p[m][:, a * C:(a + 1) * C]
                        if m < 2:
                            to = to.rearrange("p (f j h) -> p f j h", f=2, j=DHE)[:, :, :, 2 * pair:2 * pair + 2]
                        else:
                            to = to[:, pair * 2 * DH:(pair + 1) * 2 * DH]
                        last = nc.tensor.matmul(to, down_t[:, m, pair, a * P:(a + 1) * P],
                                                up[:, m, :, :, :].rearrange("p f h j -> p f j h") if m < 2 else
                                                up_v[:, :, :].rearrange("p h d -> p (h d)"),
                                                start=(a == 0 and pair == 0), stop=(a == 1 and pair == HP - 1),
                                                skip_group_check=True)
                last.then_inc(folded, 1)
            pe.wait_ge(w_made, NDOWN)
            with pe.Fori(0, NB // 2) as k:
                for u in range(2):
                    n = 2 * k + u
                    pe.wait_ge(xn_made, n + 1)
                    pe.wait_ge(xt_lo_made, CC * n + PRIMED)
                    for a in range(CC):
                        for j in range(TILES):
                            last = nc.tensor.transpose(ps_t[a][:, j * P:(j + 1) * P],
                                                       xn[:, u, j, a * P:(a + 1) * P], ident[:, :])
                        last.then_inc(xt_turned, 1)
                    pe.wait_ge(xt_lo_made, CC * n + CC + PRIMED)
                    for i, (m, half) in enumerate(PROJ):
                        pe.wait_ge(plain_rest if i < 2 else raw_copied, 2 * n + PRIMED)
                        for a in range(CC):
                            cols = slice(half * P, (half + 1) * P)
                            last = three_products(nc, ps_p[i][:, :],
                                                  (w_hi[:, m, a, cols], w_lo[:, m, a, cols]),
                                                  (xt_hi[:, u, a, :], xt_lo[:, u, a, :]), a == 0, a == CC - 1)
                        last.then_inc(projected, 1)
                    pe.wait_ge(v_copied, 2 * n + PRIMED)
                    for j in range(TILES):
                        for a in range(CC):
                            cols = slice(j * P, (j + 1) * P)
                            last = three_products(nc, ps_v[j // 2][:, (j % 2) * C:(j % 2 + 1) * C],
                                                  (xt_hi[:, u, a, cols], xt_lo[:, u, a, cols]),
                                                  (w_hi[:, 2, a, :], w_lo[:, 2, a, :]),
                                                  a == 0 and j % 2 == 0, a == CC - 1)
                        if j % 2:
                            last.then_inc(v_projected, 1)


STACK = 6 * DH
ROWS = STACK + PARTS
EARLY = 12
NEG = -3.0e38
RING = 3
AHEAD = 12


def attention_plan():
    steps = [(c, kt) for c in range(CH) for kt in range((c + 1) * TILES)]

    def pieces(tiles):
        return [("max", qt, h, kc) for qt in tiles for h in range(GH) for kc in range(qt // TILES + 1)]

    def width(e):
        _, qt, _, kc = e[:4]
        return TB if kc < qt // TILES else (qt % TILES + 1) * P

    late = [e + (False,) for e in pieces(range(EARLY, QT))]
    early = [e + (True,) for e in pieces(range(EARLY))]
    late_ahead = [e[:4] + (True,) for e in late[:AHEAD]]
    maxes = late[AHEAD:] + [("chain", True)] + early[:3] + [("turn_max", True)] + early[3:] + [
        ("chain", False)] + late_ahead[:3] + [("turn_max", False)] + late_ahead[3:]
    scores = [(s, pair) for s in range(len(steps)) for pair in range(2)]
    lo = [max(0, kt - c * TILES) * P for c, kt in steps]
    plan, now, vector, scalar = [], 0.0, 0.0, 0.0
    exp_end, taken = [0.0, 0.0], [0.0] * RING
    outs, i, s, at, copied = [], 0, 0, 0, 0.0
    out_ready, rows_ready, late_ready = 0.0, 0.0, 0.0
    while i < len(scores) or s < len(steps) or at < len(maxes) or outs:
        ready = {}
        if outs:
            ready["turn_out"] = max(out_ready, taken[-RING])
        if at < len(maxes):
            ready["max"] = (0.0 if maxes[at][0] == "chain" else taken[-RING] if maxes[at][0] == "max" else
                            max(taken[-RING], rows_ready))
        if i < len(scores) and scores[i][0] < s + 4:
            ready["scores"] = max(exp_end[-2], late_ready if steps[scores[i][0]][0] == CH - 1 else 0.0)
        if s < len(steps) and i > 2 * s + 1:
            ready["sum"] = exp_end[2 * s + 3] + (900 if lo[s] or steps[s][1] == steps[s][0] * TILES else 0)
            if steps[s][1] == 0:
                ready["sum"] = max(ready["sum"], copied)
        kind = min(ready, key=lambda k: (max(now, ready[k]), list(ready).index(k)))
        now = max(now, ready[kind])
        if kind == "max":
            e = maxes[at]
            at += 1
            plan.append(e)
            if e[0] == "chain":
                rows_ready = taken[-1] + 1000
                vector = max(vector, taken[-1]) + 600
            else:
                now += width(e) / 2.4 if e[0] == "max" else 200
                vector = max(vector, now + 130) + (width(e) if e[0] == "max" else 400) / 0.96 + 70
                taken.append(vector + 60)
                if e[0] == "turn_max" and e[1]:
                    late_ready = vector + 6000
        elif kind == "scores":
            plan.append(("scores",) + scores[i])
            w = TB - lo[scores[i][0]]
            i += 1
            now += 2 * w / 2.4
            scalar = max(scalar, now + 100) + 2 * w / 1.2 + 50
            exp_end.append(scalar + 60)
        elif kind == "sum":
            plan.append(("sum", s))
            now += 4 * (TB - lo[s]) / 2.2
            if lo[s] == (TILES - 1) * P:
                outs.append(steps[s][0])
                scalar = max(scalar, now + 150) + 480
                copied = scalar + 60
                out_ready = copied
            s += 1
        else:
            plan.append(("turn_out", outs.pop(0)))
            now += 450
            vector = max(vector, now + 100) + 900
            taken.append(vector + 60)
    return steps, plan, early, late_ahead, width


def attend(nc, parts_dram, v_dram, minus_dram, y_dram):
    STEPS, PLAN, EARLY_PIECES, LATE_AHEAD, width = attention_plan()
    NSTEP = len(STEPS)
    NITEM = 2 * NSTEP
    PLACES = {"max": 1, "turn_max": 2, "turn_out": 1}
    NRING = sum(PLACES.get(e[0], 0) for e in PLAN)
    NDIAG = 2 * QT
    assert NRING % RING == 0 and NSTEP % 4 == 0
    NEARLY = len(EARLY_PIECES) + PLACES["turn_max"]
    RING0 = NEARLY + AHEAD
    CHAIN_STEPS = 4
    LOADS = 10

    with ExitStack() as ctx:
        def sb(name, shape, dt):
            return ctx.enter_context(nc.sbuf_tensor(name, shape, dt))

        def sem(name):
            return ctx.enter_context(nc.semaphore(name))

        q_st = sb("q_st", [ROWS, 2, GH, T], BF16)
        k_st = sb("k_st", [ROWS, 2, GH, T], BF16)
        v_sb = sb("v_sb", [P, 2, QT, GH, VW], F32)
        prob = sb("prob", [P, 4, GH, TB], F32)
        out_sb = sb("out_sb", [P, 2, TB], F32)
        y_sb = sb("y_sb", [P, 2, TILES, GH, DH], F32)
        rec = sb("rec", [P, 2, TILES, GH], F32)
        ident = sb("ident2", [P, P], F32)
        ident_bf = sb("ident_bf", [P, P], BF16)
        causal = sb("causal", [P, TB], F32)
        junk = sb("junk", [P, RING, TB], F32)
        maxes = sb("maxes", [P, GH, QT, CH], F32)
        minus = sb("minus", [P, GH, EARLY], F32)
        left = sb("left", [P, GH, EARLY], F32)
        minus_parts = sb("minus_parts", [P, PARTS, GH * EARLY], BF16)
        minus_rows = sb("minus_rows", [GH * EARLY, PARTS, P], BF16)

        ps_s = [ctx.enter_context(nc.psum_tensor(f"ps_s{i}", [P, 2, 512], F32)) for i in range(2)]
        ps_m = [ctx.enter_context(nc.psum_tensor(f"ps_m{i}", [P, 512], F32)) for i in range(RING)]
        ps_o = ctx.enter_context(nc.psum_tensor("ps_o", [P, 512], F32))

        ident_made = sem("ident_made2")
        ident_bf_made = sem("ident_bf_made2")
        causal_made = sem("causal_made")
        ones_made = sem("ones_made")
        maxes_clear = sem("maxes_clear")
        banks_clear = sem("banks_clear")
        loaded = sem("loaded")
        scores_made = sem("scores_made")
        exp_made = sem("exp_made")
        masked = sem("masked")
        summed = sem("summed")
        out_copied = sem("out_copied")
        y_stored = [sem(f"y_stored{i}") for i in range(2)]
        rec_made = sem("rec_made")
        pe_alone = sem("pe_alone2")
        dve_alone = sem("dve_alone2")
        pool_alone = sem("pool_alone2")
        piece_made = sem("piece_made")
        piece_taken = sem("piece_taken")
        minus_made = sem("minus_made")
        rows_out = sem("rows_out")
        rows_in = sem("rows_in")
        dve_step = sem("dve_step2")

        block = ctx.enter_context(nc.Block())

        def windows(eng, body):
            with eng.Fori(0, NG // 2 - 1) as k:
                for u in range(2):
                    body(2 * k + u, u, False)
            for u in range(2):
                body(NG - 2 + u, u, u == 1)

        def plan_of(last):
            ring = 0
            for e in PLAN:
                if last and (e[0] == "max" and e[4] or e[0] in ("chain", "turn_max") and not e[1]):
                    continue
                yield e, ring
                ring += PLACES.get(e[0], 0)

        @block.sync
        def _(sp):
            for i in range(2):
                sp.sem_inc(y_stored[i], 16 * PRIMED)
            sp.sem_inc(rows_in, 16 * PRIMED)

            def load(g, u):
                b, hg = g // HG, g % HG
                at = 0
                for i in range(PARTS):
                    n = PARTS - i
                    q_rows, k_rows = (parts_dram[t, :, :, :, bass.ds(hg * GH, GH), bass.ds(b * T, T)]
                                      for t in range(2))
                    for _ in range(n):
                        sp.dma_start(q_st[at:at + DH, u, :, :],
                                     q_rows[i].rearrange("f j h n -> (f j) h n")).then_inc(loaded, 16)
                        at += DH
                    sp.dma_start(k_st[at - n * DH:at, u, :, :],
                                 k_rows[0:n].rearrange("s f j h n -> (s f j) h n")).then_inc(loaded, 16)
                sp.dma_start(v_sb[:, u, :, :, :].rearrange("p k h d -> p (k h d)"),
                             v_dram[hg, :, bass.ds(b * QT, QT), :, :].rearrange("p k h d -> p (k h d)")
                             ).then_inc(loaded, 16)

            def place_minus(u, late, number):
                lo, n = (EARLY, QT - EARLY) if late else (0, EARLY)
                sp.dma_start(minus_dram[late][:, :, :, :].rearrange("s h k n -> (h k) s n"),
                             minus_rows[0:GH * n, :, :]).then_inc(rows_out, 16)
                sp.wait_ge(rows_out, 16 * number)
                sp.dma_start(q_st[STACK:ROWS, u, :, lo * P:(lo + n) * P],
                             minus_dram[late][:, :, :, :].rearrange("s h k n -> s h (k n)")).then_inc(rows_in, 16)

            load(0, 0)
            sp.wait_ge(piece_taken, NEARLY + RING * PRIMED)
            place_minus(0, False, 1)

            def body(w, u, last):
                if not last:
                    sp.wait_ge(summed, NSTEP * w + 4 * PRIMED)
                    load(w + 1, 1 - u)
                for e, ring in plan_of(last):
                    if e[0] == "turn_max":
                        sp.wait_ge(piece_taken, RING0 + NRING * w + ring + 2 + RING * PRIMED)
                        place_minus(u if e[1] else 1 - u, e[1], 2 * w + (2 if e[1] else 3))
                    elif e[0] == "turn_out":
                        c = e[1]
                        sp.wait_ge(piece_taken, RING0 + NRING * w + ring + 1 + RING * PRIMED)
                        to = y_dram[bass.ds((w // HG) * T + c * TB, TB), bass.ds((w % HG) * (GH * DH), GH * DH)]
                        sp.dma_start(to.rearrange("(j p) n -> p j n", p=P),
                                     y_sb[:, c % 2, :, :, :].rearrange("p j h d -> p j (h d)")
                                     ).then_inc(y_stored[c % 2], 16)
            windows(sp, body)
            for i in range(2):
                sp.wait_ge(y_stored[i], 16 * (NG * CH // 2 + PRIMED))

        @block.gpsimd
        def _(pool):
            make_identity(nc, pool, ident, ident_made)
            nc.gpsimd.memset(maxes[:, :, :, :], NEG).then_inc(maxes_clear, 1)
            nc.gpsimd.memset(causal[:, :], 0.0).then_inc(causal_made, 1)
            pool.wait_ge(causal_made, 1)
            nc.gpsimd.affine_select(out=causal[:, TB - P:TB], in_=causal[:, TB - P:TB], compare_op=ALU.is_ge,
                                    fill=NEG, base=0, pattern=[[-1, P]],
                                    channel_multiplier=1).then_inc(causal_made, 1)

            def body(w, u, last):
                diag = 0
                for s, (c, kt) in enumerate(STEPS):
                    r = kt - c * TILES
                    if r < 0:
                        continue
                    for pair in range(2):
                        pool.wait_ge(exp_made, NITEM * w + 2 * s + pair + 1 + 2 * PRIMED)
                        pool.sem_inc(pool_alone, 1)
                        tile = prob[:, s % 4, 2 * pair:2 * pair + 2, r * P:(r + 1) * P]
                        nc.gpsimd.affine_select(out=tile, in_=tile, compare_op=ALU.is_ge, fill=0.0, base=0,
                                                pattern=[[0, 2], [1, P]],
                                                channel_multiplier=-1).then_inc(masked, 1)
                        diag += 1
                assert diag == NDIAG
            windows(pool, body)

        @block.scalar
        def _(act):
            act.sem_inc(exp_made, 2 * PRIMED)

            act.sem_inc(out_copied, PRIMED)

            def body(w, u, last):
                for e, _ in plan_of(last):
                    if e[0] == "scores":
                        _, s, pair = e
                        c, kt = STEPS[s]
                        lo = max(0, kt - c * TILES) * P
                        n = 2 * s + pair
                        if pair == 0:
                            act.wait_ge(summed, NSTEP * w + s + PRIMED)
                        act.wait_ge(scores_made, NITEM * w + n + 1)
                        nc.scalar.activation(prob[:, s % 4, 2 * pair:2 * pair + 2, lo:TB],
                                             ps_s[n % 2][:, :, lo:TB], ACT.Exp,
                                             scale=DH ** -0.5).then_inc(exp_made, 1)
                    elif e[0] == "sum" and STEPS[e[1]][1] == (STEPS[e[1]][0] + 1) * TILES - 1:
                        s = e[1]
                        act.wait_ge(summed, NSTEP * w + s + 1 + 4 * PRIMED)
                        nc.scalar.copy(out_sb[:, STEPS[s][0] % 2, :], ps_o[:, :]).then_inc(out_copied, 1)
            windows(act, body)

        @block.vector
        def _(dve):
            dve.sem_inc(piece_taken, RING * PRIMED)
            nc.vector.memset(ps_o[:, :], 0.0).then_inc(banks_clear, 1)
            nc.vector.memset(k_st[STACK:ROWS, :, :, :], 1.0).then_inc(ones_made, 1)
            dve.wait_ge(ident_made, 2)
            nc.vector.tensor_copy(ident_bf[:, :], ident[:, :]).then_inc(ident_bf_made, 1)
            dve.wait_ge(causal_made, 2)
            dve.wait_ge(maxes_clear, 1)

            def take(e, parity):
                _, qt, h, kc = e[:4]
                w = width(e)
                to = maxes[:, h, qt, kc:kc + 1]
                bank = ps_m[parity]
                if kc < qt // TILES:
                    return nc.vector.tensor_reduce(to, bank[:, 0:w], AX.X, ALU.max)
                return nc.vector.tensor_tensor_reduce(junk[:, parity, 0:w], bank[:, 0:w], causal[:, TB - w:TB], 1.0, NEG,
                                                      ALU.add, ALU.max, to)

            def split_minus(steps, late):
                lo, n = (EARLY, QT - EARLY) if late else (0, EARLY)
                m, rest = minus[:, :, 0:n], left[:, :, 0:n]
                parts = [minus_parts[:, i, 0:GH * n].rearrange("p (h n) -> p h n", h=GH) for i in range(PARTS)]
                steps.done(nc.vector.tensor_reduce(m, maxes[:, :, lo:lo + n, :], AX.X, ALU.max, negate=True))
                steps.done(nc.vector.tensor_copy(parts[0], m))
                steps.done(nc.vector.tensor_tensor(out=rest, in0=m, in1=parts[0], op=ALU.subtract))
                steps.done(nc.vector.tensor_copy(parts[1], rest))
                nc.vector.tensor_tensor(out=parts[2], in0=rest, in1=parts[1], op=ALU.subtract).then_inc(minus_made, 1)

            def copy_minus(bank, late):
                n = QT - EARLY if late else EARLY
                src = bank[:, :].bitcast(BF16)[0:GH * n, 0:PARTS * P].rearrange("p (s n) -> p s n", s=PARTS)
                nc.vector.tensor_copy(minus_rows[0:GH * n, :, :], src).then_inc(piece_taken, 2)

            for i, e in enumerate(EARLY_PIECES):
                dve.wait_ge(piece_made, i + 1)
                take(e, i % RING).then_inc(piece_taken, 1)
            dve.wait_ge(piece_taken, len(EARLY_PIECES) + RING * PRIMED)
            steps = Steps(dve, dve_step)
            split_minus(steps, False)
            dve.wait_ge(piece_made, NEARLY)
            copy_minus(ps_m[len(EARLY_PIECES) % RING], False)
            for i, e in enumerate(LATE_AHEAD, NEARLY):
                dve.wait_ge(piece_made, i + 1)
                take(e, i % RING).then_inc(piece_taken, 1)

            def body(w, u, last):
                steps = Steps(dve, dve_step, CHAIN_STEPS + 2 * CHAIN_STEPS * w)
                for e, ring in plan_of(last):
                    n = RING0 + NRING * w + ring
                    bank = ps_m[(RING0 + ring) % RING]
                    if e[0] == "max":
                        dve.wait_ge(piece_made, n + 1)
                        if e[3] == e[1] // TILES:
                            dve.sem_inc(dve_alone, 1)
                        take(e, (RING0 + ring) % RING).then_inc(piece_taken, 1)
                    elif e[0] == "chain":
                        dve.wait_ge(piece_taken, n + RING * PRIMED)
                        split_minus(steps, e[1])
                    elif e[0] == "turn_max":
                        dve.wait_ge(piece_made, n + 2)
                        k = 2 * w + (1 if e[1] else 2)
                        dve.wait_ge(rows_in, 16 * k + 16 * PRIMED)
                        copy_minus(bank, e[1])
                    elif e[0] == "turn_out":
                        c = e[1]
                        src = bank[:, :].rearrange("p (j h d) -> p j h d", j=TILES, h=GH)
                        dve.wait_ge(piece_made, n + 1)
                        nc.vector.reciprocal(rec[:, c % 2, :, :], src[:, :, :, DH]).then_inc(rec_made, 1)
                        dve.wait_ge(rec_made, CH * w + c + 1)
                        dve.wait_ge(y_stored[c % 2], 16 * (2 * w + c // 2) + 16 * PRIMED)
                        nc.vector.tensor_tensor(out=y_sb[:, c % 2, :, :, :], in0=src[:, :, :, 0:DH],
                                                in1=rec[:, c % 2, :, :].unsqueeze(3).broadcast_to([P, TILES, GH, DH]),
                                                op=ALU.mult).then_inc(piece_taken, 1)
            windows(dve, body)

        @block.tensor
        def _(pe):
            pe.sem_inc(summed, 4 * PRIMED)
            pe.wait_ge(ident_bf_made, 1)
            pe.wait_ge(ones_made, 1)
            pe.wait_ge(banks_clear, 1)

            def piece(e, bank, u):
                _, qt, h, kc = e[:4]
                return nc.tensor.matmul(bank[:, 0:width(e)], q_st[0:STACK, u, h, qt * P:(qt + 1) * P],
                                        k_st[0:STACK, u, h, kc * TB:kc * TB + width(e)], start=True, stop=True)

            def turn_max(bank, late):
                n = GH * (QT - EARLY if late else EARLY)
                for part in range(PARTS):
                    last = nc.tensor.transpose(bank[:, :].bitcast(BF16)[0:n, part * P:(part + 1) * P],
                                               minus_parts[:, part, 0:n], ident_bf[:, :])
                return last

            pe.wait_ge(loaded, LOADS * 16)
            for i, e in enumerate(EARLY_PIECES):
                pe.wait_ge(piece_taken, i + 1)
                piece(e, ps_m[i % RING], 0).then_inc(piece_made, 1)
            pe.wait_ge(minus_made, 1)
            pe.wait_ge(piece_taken, len(EARLY_PIECES) + 1)
            turn_max(ps_m[len(EARLY_PIECES) % RING], False).then_inc(piece_made, PLACES["turn_max"])
            for i, e in enumerate(LATE_AHEAD, NEARLY):
                pe.wait_ge(piece_taken, i + 1)
                piece(e, ps_m[i % RING], 0).then_inc(piece_made, 1)

            def body(w, u, last):
                ahead = False
                for e, ring in plan_of(last):
                    n = RING0 + NRING * w + ring
                    bank = ps_m[(RING0 + ring) % RING]
                    if e[0] == "scores":
                        s = e[1]
                        c, kt = STEPS[s]
                        lo = max(0, kt - c * TILES) * P
                        if s == 0 and e[2] == 0:
                            pe.wait_ge(rows_in, 16 * (2 * w + 1) + 16 * PRIMED)
                        if c == EARLY // TILES and kt == 0 and e[2] == 0:
                            pe.wait_ge(rows_in, 16 * (2 * w + 2) + 16 * PRIMED)
                        i = 2 * s + e[2]
                        pe.wait_ge(exp_made, NITEM * w + i + 1)
                        for h2 in range(2):
                            h = 2 * e[2] + h2
                            mm = nc.tensor.matmul(ps_s[i % 2][:, h2, lo:TB], k_st[:, u, h, kt * P:(kt + 1) * P],
                                                  q_st[:, u, h, c * TB + lo:(c + 1) * TB], start=True, stop=True)
                        mm.then_inc(scores_made, 1)
                    elif e[0] == "sum":
                        s = e[1]
                        c, kt = STEPS[s]
                        r = kt - c * TILES
                        lo = max(0, r) * P
                        if kt == 0:
                            pe.wait_ge(out_copied, CH * w + c + PRIMED)
                        pe.wait_ge(exp_made, NITEM * w + 2 * s + 2 + 2 * PRIMED)
                        if r >= 0:
                            pe.wait_ge(masked, NDIAG * w + 2 * (c * TILES + r) + 2)
                        for h in range(GH):
                            mm = nc.tensor.matmul(ps_o[32 * h:32 * h + VW, lo:TB], v_sb[:, u, kt, h, :],
                                                  prob[:, s % 4, h, lo:TB], start=(kt == 0),
                                                  stop=(r == TILES - 1), skip_group_check=True)
                        mm.then_inc(summed, 1)
                    elif e[0] == "turn_out":
                        c = e[1]
                        pe.wait_ge(out_copied, CH * w + c + 1 + PRIMED)
                        pe.wait_ge(piece_taken, n + 1)
                        pe.sem_inc(pe_alone, 1)
                        for j in range(TILES):
                            mm = nc.tensor.transpose(bank[:, j * P:(j + 1) * P],
                                                     out_sb[:, c % 2, j * P:(j + 1) * P], ident[:, :])
                        mm.then_inc(piece_made, 1)
                    elif e[0] == "max":
                        if e[4] and not ahead:
                            pe.wait_ge(loaded, LOADS * 16 * (w + 2))
                            ahead = True
                        pe.wait_ge(piece_taken, n + 1)
                        piece(e, bank, 1 - u if e[4] else u).then_inc(piece_made, 1)
                    elif e[0] == "turn_max":
                        pe.wait_ge(minus_made, 2 * w + (2 if e[1] else 3))
                        pe.wait_ge(piece_taken, n + 1)
                        pe.sem_inc(pe_alone, 1)
                        turn_max(bank, e[1]).then_inc(piece_made, PLACES["turn_max"])
            windows(pe, body)


WCH = 512
W_PER_LOOP = 2
TOP = 2
SLOT_TILES = TOP * B * T // P + E
CLEAR = 8


def mix(nc, x, y_dram, wc, wr, br, w1, w2, w_sb, logits, xn_dram, x1_dram, xs_dram):
    w_hi, w_lo = w_sb
    with ExitStack() as ctx:
        def sb(name, shape, dt):
            return ctx.enter_context(nc.sbuf_tensor(name, shape, dt))

        def sem(name):
            return ctx.enter_context(nc.semaphore(name))

        def bank(name):
            return ctx.enter_context(nc.psum_tensor(name, [P, 512], F32))

        ident = sb("ident3", [P, P], F32)
        wc_sb = sb("wc_sb", [P, CC, C], F32)
        wr_sb = sb("wr_sb", [P, CC, E], F32)
        br_sb = sb("br_sb", [E, 1], F32)
        raw = sb("w_raw", [P, 2 * W_PER_LOOP, WCH], F32)
        y_in = sb("y_in", [P, 2, TILES, C], F32)
        x_in = sb("x_in", [P, 2, TILES, C], F32)
        yt = sb("yt", [P, 1, CC, TB], F32)
        stats = sb("stats3", [P, TILES, 6], F32)
        mv = sb("mv3", [P, TILES, 2], F32)
        var = sb("var3", [P, TILES], F32)
        rstd = sb("rstd3", [P, TILES], F32)
        tmp = sb("tmp3", [P, TILES], F32)
        xt = sb("xt", [P, 1, CC, TB], F32)
        zeros = sb("zeros", [P, CLEAR, C], F32)
        by_expert = sb("by_expert", [E, TB], F32)

        ps_t = [bank(f"ps_yt{i}") for i in range(CC)]
        ps_x = [bank(f"ps_x{i}") for i in range(2)]
        ps_u = [bank(f"ps_u{i}") for i in range(CC)]
        ps_r = bank("ps_r")
        ps_l = bank("ps_l")

        ident_made = sem("ident_made3")
        weights_in = sem("weights_in3")
        y_loaded = [sem(f"y_loaded{u}") for u in range(2)]
        raw_in = sem("raw_in")
        w_hi_made = sem("w_hi_made3")
        w_lo_made = sem("w_lo_made3")
        y_turned = sem("y_turned")
        yt_made = sem("yt_made")
        mixed = sem("mixed")
        x1_made = sem("x1_made")
        dve_step = sem("dve_step3")
        dve_alone = sem("dve_alone3")
        sp_alone = sem("sp_alone3")
        pool_alone = sem("pool_alone3")
        pe_alone = sem("pe_alone3")
        xn_made = sem("xn_made3")
        xn_turned = sem("xn_turned")
        xt_made = sem("xt_made")
        routed = sem("routed")
        by_expert_made = sem("by_expert_made")
        logits_turned = sem("logits_turned")
        logits_made = sem("logits_made")
        x1_stored = sem("x1_stored")
        xn_stored = sem("xn_stored")
        zeros_made = sem("zeros_made")
        cleared = sem("cleared")

        x_v = x.rearrange("b (c j p) d -> (b c) p j d", p=P, j=TILES)
        y_v = y_dram.rearrange("(n j p) d -> n p j d", p=P, j=TILES)
        xn_v = xn_dram.rearrange("(n j p) d -> n p j d", p=P, j=TILES)
        x1_v = x1_dram.rearrange("(n j p) d -> n p j d", p=P, j=TILES)
        w1_v = w1.rearrange("e (a p) f -> (e a) p f", p=P)
        w2_v = w2.rearrange("e (a o p) c -> (e a) p o c", p=P, o=WCH // C)

        block = ctx.enter_context(nc.Block())

        def staged(eng, first, second):
            first(0, 0, 0)
            with eng.Fori(0, NB // 2 - 1) as k:
                first(2 * k + 1, 1, k)
                second(2 * k, 0, k)
                first(2 * k + 2, 0, k + 1)
                second(2 * k + 1, 1, k)
            first(NB - 1, 1, NB // 2 - 1)
            second(NB - 2, 0, NB // 2 - 1)
            second(NB - 1, 1, NB // 2 - 1)

        @block.sync
        def _(sp):
            sp.sem_inc(x1_stored, 16 * PRIMED)
            sp.sem_inc(xn_stored, 16 * PRIMED)
            sp.dma_start(wc_sb[:, :, :], wc.rearrange("(a p) n -> p a n", p=P)).then_inc(weights_in, 16)
            sp.dma_start(wr_sb[:, :, :], wr.rearrange("(a p) n -> p a n", p=P)).then_inc(weights_in, 16)
            sp.dma_start(br_sb[:, :], br.rearrange("(e a) -> e a", a=1)).then_inc(weights_in, 16)

            def load(n, u):
                sp.dma_start(y_in[:, u, :, :], y_v[n, :, :, :]).then_inc(y_loaded[u], 16)
                sp.dma_start(x_in[:, u, :, :], x_v[n, :, :, :]).then_inc(y_loaded[u], 16)

            def load_weights(k):
                sp.wait_ge(w_lo_made, 2 * W_PER_LOOP * k + PRIMED)
                sp.sem_inc(sp_alone, 1)
                for i in range(W_PER_LOOP):
                    sp.dma_start(raw[:, i, :], w1_v[W_PER_LOOP * k + i, :, :]).then_inc(raw_in, 16)
                    sp.dma_start(raw[:, W_PER_LOOP + i, :].rearrange("p (o c) -> p o c", c=C),
                                 w2_v[W_PER_LOOP * k + i, :, :, :]).then_inc(raw_in, 16)

            def store_x1(n, u):
                sp.wait_ge(x1_made, 2 * n + 2 + PRIMED)
                sp.sem_inc(sp_alone, 1)
                sp.dma_start(x1_v[n, :, :, :], x_in[:, u, :, :]).then_inc(x1_stored, 16)

            def store_xn(n, u):
                sp.wait_ge(xn_made, n + 1)
                sp.sem_inc(sp_alone, 1)
                sp.dma_start(xn_v[n, :, :, :], y_in[:, u, :, :]).then_inc(xn_stored, 16)

            def turn_over(n, u):
                store_x1(n, u)
                store_xn(n, u)
                sp.wait_ge(x1_stored, 16 * (n + 1) + 16 * PRIMED)
                sp.sem_inc(sp_alone, 1)
                sp.wait_ge(xn_stored, 16 * (n + 1) + 16 * PRIMED)
                sp.sem_inc(sp_alone, 1)
                sp.wait_ge(xn_turned, CC * (n + 1))
                sp.sem_inc(sp_alone, 1)
                load(n + 2, u)

            for u in range(2):
                load(u, u)
            load_weights(0)
            turn_over(0, 0)
            with sp.Fori(1, NB // 2 - 1) as k:
                turn_over(2 * k - 1, 1)
                load_weights(k)
                turn_over(2 * k, 0)
            turn_over(NB - 3, 1)
            load_weights(NB // 2 - 1)
            store_x1(NB - 2, 0)
            store_xn(NB - 2, 0)
            store_x1(NB - 1, 1)
            store_xn(NB - 1, 1)
            sp.wait_ge(x1_stored, 16 * (NB + PRIMED))
            sp.wait_ge(xn_stored, 16 * (NB + PRIMED))
            sp.wait_ge(cleared, 16 * (SLOT_TILES // CLEAR))

        @block.gpsimd
        def _(pool):
            pool.sem_inc(w_lo_made, PRIMED)
            nc.gpsimd.memset(zeros[:, :, :], 0.0).then_inc(zeros_made, 1)
            make_identity(nc, pool, ident, ident_made)
            with pool.Fori(0, NB // 2) as k:
                def split(i):
                    chunk = W_PER_LOOP * k + (i % W_PER_LOOP) + (i // W_PER_LOOP) * (NB // 2 * W_PER_LOOP)
                    pool.wait_ge(raw_in, 16 * 2 * W_PER_LOOP * (k + 1))
                    pool.sem_inc(pool_alone, 1)
                    nc.gpsimd.tensor_copy(w_hi[:, bass.ds(chunk, 1), :].rearrange("p a n -> p (a n)"),
                                          raw[:, i, :]).then_inc(w_hi_made, 1)
                    pool.wait_ge(w_hi_made, 2 * W_PER_LOOP * k + i + 1)
                    pool.sem_inc(pool_alone, 1)
                    nc.gpsimd.tensor_tensor(
                        out=w_lo[:, bass.ds(chunk, 1), :].rearrange("p a n -> p (a n)"), in0=raw[:, i, :],
                        in1=w_hi[:, bass.ds(chunk, 1), :].bitcast(F32).rearrange("p a n -> p (a n)"),
                        op=ALU.subtract).then_inc(w_lo_made, 1)

                for u in range(2):
                    for i in range(W_PER_LOOP):
                        split(W_PER_LOOP * u + i)

        @block.scalar
        def _(act):
            act.wait_ge(zeros_made, 1)
            xs_v = xs_dram.rearrange("(g j p) d -> g p j d", p=P, j=CLEAR)
            for g in range(SLOT_TILES // CLEAR):
                act.dma_start(xs_v[g, :, :, :], zeros[:, :, :]).then_inc(cleared, 16)
            act.wait_ge(weights_in, 3 * 16)

            def first(n, u, k):
                for a in range(CC):
                    act.wait_ge(y_turned, CC * n + a + 1)
                    nc.scalar.copy(yt[:, 0, a, :], ps_t[a][:, :]).then_inc(yt_made, 1)

            def second(n, u, k):
                for a in range(CC):
                    act.wait_ge(xn_turned, CC * n + a + 1)
                    nc.scalar.copy(xt[:, 0, a, :], ps_u[a][:, :]).then_inc(xt_made, 1)
                act.wait_ge(routed, n + 1)
                nc.scalar.activation(by_expert[:, :], ps_r[0:E, :], ACT.Identity,
                                     bias=br_sb[:, 0:1]).then_inc(by_expert_made, 1)
            staged(act, first, second)

        @block.vector
        def _(dve):
            NSTEP = LN_STEPS
            dve.sem_inc(logits_made, PRIMED)
            dve.sem_inc(x1_made, PRIMED)

            def first(n, u, k):
                steps = Steps(dve, dve_step, n * NSTEP)
                dve.wait_ge(y_loaded[u], 32 * (k + 1))
                for i in range(2):
                    dve.wait_ge(mixed, 2 * n + i + 1)
                    part = x_in[:, u, 2 * i:2 * i + 2, :].rearrange("p j d -> p (j d)")
                    nc.vector.tensor_tensor(out=part, in0=ps_x[i][:, :], in1=part, op=ALU.add).then_inc(x1_made, 1)
                dve.wait_ge(x1_made, 2 * n + 2 + PRIMED)
                dve.sem_inc(dve_alone, 1)
                layer_norm_stats(nc, steps, x_in[:, u, :, :], stats, mv, var, rstd, tmp, dve_alone)
                for j in range(TILES):
                    last = nc.vector.tensor_scalar(y_in[:, u, j, :], x_in[:, u, j, :], mv[:, j, 0:1],
                                                   rstd[:, j:j + 1], ALU.subtract, ALU.mult)
                last.then_inc(xn_made, 1)
                dve.wait_ge(xn_made, n + 1)
                dve.sem_inc(dve_alone, 1)

            def second(n, u, k):
                dve.wait_ge(logits_turned, n + 1)
                nc.vector.tensor_copy(logits[:, bass.ds(n * TILES, TILES), :],
                                      ps_l[:, 0:TILES * E].rearrange("p (j e) -> p j e", e=E)
                                      ).then_inc(logits_made, 1)
            staged(dve, first, second)

        @block.tensor
        def _(pe):
            pe.wait_ge(ident_made, 2)
            pe.wait_ge(weights_in, 3 * 16)

            def turn(banks, u):
                for a in range(CC):
                    for j in range(TILES):
                        last = nc.tensor.transpose(banks[a][:, j * P:(j + 1) * P],
                                                   y_in[:, u, j, a * P:(a + 1) * P], ident[:, :])
                    yield last

            def first(n, u, k):
                pe.wait_ge(y_loaded[u], 32 * (k + 1))
                for last in turn(ps_t, u):
                    last.then_inc(y_turned, 1)
                pe.wait_ge(yt_made, CC * n + CC)
                pe.sem_inc(pe_alone, 1)
                pe.wait_ge(x1_made, 2 * n + PRIMED)
                for j in range(TILES):
                    for a in range(CC):
                        last = nc.tensor.matmul(ps_x[j // 2][:, (j % 2) * C:(j % 2 + 1) * C],
                                                yt[:, 0, a, j * P:(j + 1) * P], wc_sb[:, a, :],
                                                start=(j % 2 == 0 and a == 0), stop=(a == CC - 1),
                                                skip_group_check=True)
                    if j % 2:
                        last.then_inc(mixed, 1)

            def second(n, u, k):
                pe.wait_ge(xn_made, n + 1)
                for last in turn(ps_u, u):
                    last.then_inc(xn_turned, 1)
                pe.wait_ge(xt_made, CC * n + CC)
                for a in range(CC):
                    last = nc.tensor.matmul(ps_r[0:E, :], wr_sb[:, a, :], xt[:, 0, a, :],
                                            start=(a == 0), stop=(a == CC - 1))
                last.then_inc(routed, 1)
                pe.wait_ge(by_expert_made, n + 1)
                pe.sem_inc(pe_alone, 1)
                pe.wait_ge(logits_made, n + PRIMED)
                pe.sem_inc(pe_alone, 1)
                for j in range(TILES):
                    last = nc.tensor.transpose(ps_l[:, j * E:(j + 1) * E], by_expert[:, j * P:(j + 1) * P],
                                               ident[0:E, 0:E])
                last.then_inc(logits_turned, 1)
            staged(pe, first, second)


def dispatch(nc, logits, tile_numbers, slots, shares, expert_of, xn_dram, xs_dram):
    NT = NB * TILES
    with ExitStack() as ctx:
        def sb(name, shape, dt=F32):
            return ctx.enter_context(nc.sbuf_tensor(name, shape, dt))

        def sem(name):
            return ctx.enter_context(nc.semaphore(name))

        rank = sb("rank", [P, E])
        hot = [sb(f"hot{i}", [P, NT, E]) for i in range(TOP)]
        score = sb("score", [P, NT, E])
        rest = sb("rest4", [P, NT, E])
        best = [sb(f"best{i}", [P, NT]) for i in range(TOP)]
        top = sb("top", [P, NT])
        ratio = sb("ratio", [P, NT])
        chosen = sb("chosen", [P, NT, E])
        running = [sb(f"running{i}", [P, NT, E]) for i in range(2)]
        ones = sb("ones4", [P, P])
        above = sb("above", [P, P])
        counts = sb("counts", [P, E])
        total_i = sb("total_i", [P, E], I32)
        tiles = sb("tiles", [P, E])
        ends = [sb(f"ends{i}", [P, E]) for i in range(2)]
        base = sb("base", [P, E])
        slot = sb("slot", [P, NT])
        numbers = sb("numbers", [P, SLOT_TILES])
        passed = sb("passed", [P, SLOT_TILES, E])
        expert = sb("expert", [P, SLOT_TILES])
        clipped = sb("clipped", [P, SLOT_TILES + 2])
        xn_rows = sb("xn_rows", [P, 2, TILES, C])
        block_slots = sb("block_slots", [P, 2, TOP, TILES], I32)
        ps = ctx.enter_context(nc.psum_tensor("ps_counts", [P, 512], F32))

        numbers_in = sem("numbers_in")
        masks_made = sem("masks_made")
        step = sem("gate_step")
        distance_made = sem("distance_made")
        ratio_made = sem("ratio_made")
        counts_made = sem("counts_made")
        counted = sem("counted")
        rows_loaded = [sem(f"rows_loaded{u}") for u in range(2)]
        slots_copied = sem("slots_copied")
        scattered = [sem(f"scattered{u}") for u in range(2)]
        pool_alone = sem("pool_alone4")
        sp_alone = sem("sp_alone4")
        dve_alone = sem("dve_alone4")
        xn_v = xn_dram.rearrange("(n j p) d -> n p j d", p=P, j=TILES)
        SCATTERS = 16 * TOP * TILES

        block = ctx.enter_context(nc.Block())

        @block.sync
        def _(sp):
            sp.dma_start(numbers[:, :], tile_numbers).then_inc(numbers_in, 16)
            for u in range(2):
                sp.dma_start(xn_rows[:, u, :, :], xn_v[u, :, :, :]).then_inc(rows_loaded[u], 16)
            with sp.Fori(0, NB // 2 - 1) as k:
                for u in range(2):
                    sp.wait_ge(scattered[u], SCATTERS * (k + 1))
                    sp.sem_inc(sp_alone, 1)
                    sp.dma_start(xn_rows[:, u, :, :], xn_v[2 * k + 2 + u, :, :, :]).then_inc(rows_loaded[u], 16)
            for u in range(2):
                sp.wait_ge(scattered[u], SCATTERS * (NB // 2))

        @block.gpsimd
        def _(pool):
            nc.gpsimd.memset(ones[:, :], 1.0).then_inc(masks_made, 1)
            pool.wait_ge(masks_made, 1)
            nc.gpsimd.affine_select(out=above[:, :], in_=ones[:, :], compare_op=ALU.is_ge, fill=0.0, base=-1,
                                    pattern=[[1, P]], channel_multiplier=-1).then_inc(masks_made, 1)
            with pool.Fori(0, NB // 2) as k:
                for u in range(2):
                    pool.wait_ge(rows_loaded[u], 16 * (k + 1))
                    pool.sem_inc(pool_alone, 1)
                    pool.wait_ge(slots_copied, 2 * k + u + 1)
                    pool.sem_inc(pool_alone, 1)
                    for i in range(TOP):
                        for j in range(TILES):
                            pool.indirect_dma_start(
                                xs_dram[:, :], bass.IndirectOffsetOnAxis(ap=block_slots[:, u, i, j:j + 1], axis=0),
                                xn_rows[:, u, j, :], None).then_inc(scattered[u], 16)

        @block.scalar
        def _(act):
            act.wait_ge(distance_made, 1)
            nc.scalar.activation(ratio[:, :], ratio[:, :], ACT.Exp).then_inc(ratio_made, 1)

        @block.tensor
        def _(pe):
            pe.wait_ge(masks_made, 2)
            pe.wait_ge(counts_made, 1)
            nc.tensor.matmul(ps[:, 0:E], above[:, :], counts[:, :], start=True, stop=False, skip_group_check=True)
            nc.tensor.matmul(ps[:, E:2 * E], ones[:, :], counts[:, :], start=False, stop=True,
                             skip_group_check=True).then_inc(counted, 1)

        @block.vector
        def _(dve):
            steps = Steps(dve, step)
            tt, ts = nc.vector.tensor_tensor, nc.vector.tensor_scalar
            for e in range(E):
                last = nc.vector.memset(rank[:, e:e + 1], float(E - e))
            nc.vector.memset(clipped[:, :], 0.0)
            steps.done(last)
            tokens = [P, NT, E]
            for i in range(TOP):
                values = logits if i == 0 else rest
                steps.done(nc.vector.tensor_reduce(best[i][:, :], values[:, :, :], AX.X, ALU.max))
                steps.done(tt(out=score[:, :, :], in0=values[:, :, :],
                              in1=best[i][:, :].unsqueeze(2).broadcast_to(tokens), op=ALU.is_equal))
                steps.done(tt(out=score[:, :, :], in0=score[:, :, :],
                              in1=rank[:, :].unsqueeze(1).broadcast_to(tokens), op=ALU.mult))
                steps.done(nc.vector.tensor_reduce(top[:, :], score[:, :, :], AX.X, ALU.max))
                steps.done(tt(out=hot[i][:, :, :], in0=score[:, :, :],
                              in1=top[:, :].unsqueeze(2).broadcast_to(tokens), op=ALU.is_equal))
                if i == 0:
                    steps.done(nc.vector.scalar_tensor_tensor(out=rest[:, :, :], in0=hot[0][:, :, :], scalar=NEG,
                                                              in1=logits[:, :, :], op0=ALU.mult, op1=ALU.add))
            tt(out=ratio[:, :], in0=best[1][:, :], in1=best[0][:, :], op=ALU.subtract).then_inc(distance_made, 1)
            dve.wait_ge(ratio_made, 1)
            steps.done(ts(top[:, :], ratio[:, :], 1.0, None, ALU.add))
            steps.done(nc.vector.reciprocal(shares[0][:, :], top[:, :]))
            steps.done(tt(out=shares[1][:, :], in0=ratio[:, :], in1=shares[0][:, :], op=ALU.mult))
            steps.done(tt(out=chosen[:, :, :], in0=hot[0][:, :, :], in1=hot[1][:, :, :], op=ALU.add))
            old, at = chosen, 0
            d = 1
            while d < NT:
                new = running[at]
                nc.vector.tensor_copy(new[:, 0:d, :], old[:, 0:d, :])
                steps.done(tt(out=new[:, d:NT, :], in0=old[:, d:NT, :], in1=old[:, 0:NT - d, :], op=ALU.add))
                old, at, d = new, 1 - at, 2 * d
            nc.vector.tensor_copy(counts[:, :], old[:, NT - 1, :]).then_inc(counts_made, 1)
            dve.wait_ge(counts_made, 1)
            steps.done(tt(out=old[:, :, :], in0=old[:, :, :], in1=chosen[:, :, :], op=ALU.subtract))
            dve.wait_ge(counted, 1)
            steps.done(ts(total_i[:, :], ps[:, E:2 * E], float(P - 1), None, ALU.add))
            steps.done(ts(total_i[:, :], total_i[:, :], P.bit_length() - 1, None, ALU.logical_shift_right))
            steps.done(nc.vector.tensor_copy(tiles[:, :], total_i[:, :]))
            end, at, d = tiles, 0, 1
            while d < E:
                new = ends[at]
                nc.vector.tensor_copy(new[:, 0:d], end[:, 0:d])
                steps.done(tt(out=new[:, d:E], in0=end[:, d:E], in1=end[:, 0:E - d], op=ALU.add))
                end, at, d = new, 1 - at, 2 * d
            steps.done(tt(out=base[:, :], in0=end[:, :], in1=tiles[:, :], op=ALU.subtract))
            steps.done(nc.vector.scalar_tensor_tensor(out=base[:, :], in0=base[:, :], scalar=float(P),
                                                      in1=ps[:, 0:E], op0=ALU.mult, op1=ALU.add))
            steps.done(tt(out=old[:, :, :], in0=old[:, :, :], in1=base[:, :].unsqueeze(1).broadcast_to(tokens),
                          op=ALU.add))
            for i in range(TOP):
                steps.done(tt(out=score[:, :, :], in0=hot[i][:, :, :], in1=old[:, :, :], op=ALU.mult))
                steps.done(nc.vector.tensor_reduce(slot[:, :], score[:, :, :], AX.X, ALU.add))
                steps.done(nc.vector.tensor_copy(slots[:, i, :], slot[:, :]))

            def place(n, u):
                nc.vector.tensor_copy(block_slots[:, u, :, :],
                                      slots[:, :, bass.ds(n * TILES, TILES)]).then_inc(slots_copied, 1)

            for u in range(2):
                place(u, u)
            with dve.Fori(1, NB // 2) as k:
                for u in range(2):
                    dve.wait_ge(scattered[u], SCATTERS * k)
                    dve.sem_inc(dve_alone, 1)
                    place(2 * k + u, u)
            dve.wait_ge(numbers_in, 16)
            table = [P, SLOT_TILES, E]
            steps.done(tt(out=passed[:, :, :], in0=numbers[:, :].unsqueeze(2).broadcast_to(table),
                          in1=end[:, :].unsqueeze(1).broadcast_to(table), op=ALU.is_ge))
            steps.done(nc.vector.tensor_reduce(expert[:, :], passed[:, :, :], AX.X, ALU.add))
            steps.done(ts(clipped[:, 0:SLOT_TILES], expert[:, :], float(E - 1), None, ALU.min))
            nxt = [clipped[:, i:i + SLOT_TILES] for i in range(3)]
            steps.done(nc.vector.scalar_tensor_tensor(out=expert[:, :], in0=nxt[2], scalar=float(E), in1=nxt[1],
                                                      op0=ALU.mult, op1=ALU.add))
            steps.done(nc.vector.scalar_tensor_tensor(out=expert_of[:, :], in0=expert[:, :], scalar=float(E),
                                                      in1=nxt[0], op0=ALU.mult, op1=ALU.add))


def experts(nc, w_sb, expert_of, b1, b2, xs_dram, ys_dram):
    w_hi, w_lo = w_sb
    FO = F // P
    HALF = NB // 2 * W_PER_LOOP
    with ExitStack() as ctx:
        def sb(name, shape, dt=F32):
            return ctx.enter_context(nc.sbuf_tensor(name, shape, dt))

        def sem(name):
            return ctx.enter_context(nc.semaphore(name))

        def banks(name):
            return [ctx.enter_context(nc.psum_tensor(f"{name}{i}", [P, 512], F32)) for i in range(2)]

        b1_sb = sb("b1_sb", [P, E, F])
        b2_sb = sb("b2_sb", [P, E, C])
        ident = sb("ident5", [P, P])
        rows = sb("rows", [P, 2, C])
        x_hi = sb("x_hi", [P, 2, C], F32R)
        x_lo = sb("x_lo", [P, 2, C], F32R)
        h = sb("h", [P, 2, F])
        h_hi = sb("h_hi", [P, 2, F], F32R)
        h_lo = sb("h_lo", [P, 2, F], F32R)
        y = sb("y", [P, 2, C])
        ps_x, ps_h, ps_t, ps_y = (banks(name) for name in ("ps_rows", "ps_hidden", "ps_turned", "ps_out"))

        ident_made = sem("ident_made5")
        biases_in = sem("biases_in")
        rows_in = [sem(f"rows_in{u}") for u in range(2)]
        x_turned = sem("x_turned")
        x_hi_made = sem("x_hi_made")
        x_lo_made = sem("x_lo_made")
        h_summed = sem("h_summed")
        h_made = sem("h_made")
        h_turned = sem("h_turned")
        h_hi_made = sem("h_hi_made")
        h_lo_made = sem("h_lo_made")
        y_summed = sem("y_summed")
        y_made = sem("y_made")
        y_stored = [sem(f"ys_stored{u}") for u in range(2)]
        pe_alone = sem("pe_alone5")
        sp_alone = sem("sp_alone5")
        dve_alone = sem("dve_alone5")
        act_alone = sem("act_alone5")

        xs_v = xs_dram.rearrange("(s p) d -> s p d", p=P)
        ys_v = ys_dram.rearrange("(s p) d -> s p d", p=P)
        LAST = SLOT_TILES - 1

        block = ctx.enter_context(nc.Block())

        def tiles_of(eng, body):
            with eng.Fori(0, SLOT_TILES // 2 - 1) as k:
                es = experts_at(eng, 2 * k)
                for u in range(2):
                    body(2 * k + u, u, k, es[u:u + 2])

        def experts_at(eng, s):
            if eng is not nc.tensor and eng is not nc.vector:
                return [None] * 3
            word = eng.value_load(expert_of[0:1, bass.ds(s, 1)], min_val=0, max_val=E ** 3 - 1)
            return [word % E, word // E % E, word // (E * E)]

        @block.sync
        def _(sp):
            def load(s, u):
                sp.dma_start(rows[:, u, :], xs_v[s, :, :]).then_inc(rows_in[u], 16)

            def step(s, u, k, es):
                sp.wait_ge(x_turned, s + 1)
                sp.sem_inc(sp_alone, 1)
                load(s + 2, u)

            for u in range(2):
                sp.sem_inc(y_stored[u], 16 * PRIMED)
                load(u, u)
            for bias, to, width in ((b1, b1_sb, F), (b2, b2_sb, C)):
                sp.dma_start(to[:, :, :].rearrange("p e n -> p (e n)"),
                             bias.rearrange("(a e) n -> a (e n)", a=1).broadcast_to([P, E * width])
                             ).then_inc(biases_in, 16)
            tiles_of(sp, step)
            for u in range(2):
                sp.wait_ge(y_stored[u], 16 * (SLOT_TILES // 2 + PRIMED))

        @block.gpsimd
        def _(pool):
            make_identity(nc, pool, ident, ident_made)

        @block.scalar
        def _(act):
            def high_rows(s, u):
                act.wait_ge(x_turned, s + 1)
                nc.scalar.copy(x_hi[:, u, :], ps_x[u][:, 0:C]).then_inc(x_hi_made, 1)

            def high_hidden(s, u):
                act.wait_ge(h_turned, s + 1)
                nc.scalar.activation(h_hi[:, u, :], ps_t[u][:, :], ACT.Relu).then_inc(h_hi_made, 1)

            def store(s, u):
                act.wait_ge(y_made, s + 1 + 2 * PRIMED)
                act.sem_inc(act_alone, 1)
                act.dma_start(ys_v[s, :, :], y[:, u, :]).then_inc(y_stored[u], 16)

            def step(s, u, k, es):
                high_rows(s + 2, u)
                high_hidden(s + 1, 1 - u)
                store(s, u)

            for u in range(2):
                high_rows(u, u)
            high_hidden(0, 0)
            tiles_of(act, step)
            high_hidden(LAST, 1)
            for u in range(2):
                store(LAST - 1 + u, u)

        @block.vector
        def _(dve):
            dve.sem_inc(x_lo_made, 2 * PRIMED)
            dve.sem_inc(h_made, 2 * PRIMED)
            dve.sem_inc(h_lo_made, 2 * PRIMED)
            dve.sem_inc(y_made, 2 * PRIMED)

            def low_rows(s, u):
                dve.wait_ge(x_hi_made, s + 1)
                nc.vector.tensor_tensor(out=x_lo[:, u, :], in0=ps_x[u][:, 0:C], in1=x_hi[:, u, :].bitcast(F32),
                                        op=ALU.subtract).then_inc(x_lo_made, 1)

            def add_bias(s, u, e):
                dve.wait_ge(h_summed, s + 1)
                dve.sem_inc(dve_alone, 1)
                nc.vector.tensor_tensor(out=h[:, u, :], in0=ps_h[u][:, :],
                                        in1=b1_sb[:, bass.ds(e, 1), :].rearrange("p a n -> p (a n)"),
                                        op=ALU.add).then_inc(h_made, 1)

            def low_hidden(s, u):
                dve.wait_ge(h_hi_made, s + 1)
                nc.vector.scalar_tensor_tensor(out=h_lo[:, u, :], in0=ps_t[u][:, :], scalar=0.0,
                                               in1=h_hi[:, u, :].bitcast(F32), op0=ALU.max,
                                               op1=ALU.subtract).then_inc(h_lo_made, 1)

            def finish(s, u, k, e):
                dve.wait_ge(y_summed, s + 1)
                dve.sem_inc(dve_alone, 1)
                dve.wait_ge(y_stored[u], 16 * k + 16 * PRIMED)
                dve.sem_inc(dve_alone, 1)
                nc.vector.tensor_tensor(out=y[:, u, :], in0=ps_y[u][:, 0:C],
                                        in1=b2_sb[:, bass.ds(e, 1), :].rearrange("p a n -> p (a n)"),
                                        op=ALU.add).then_inc(y_made, 1)

            def step(s, u, k, es):
                add_bias(s + 1, 1 - u, es[1])
                low_rows(s + 2, u)
                finish(s, u, k, es[0])
                low_hidden(s + 1, 1 - u)

            dve.wait_ge(biases_in, 32)
            for u in range(2):
                low_rows(u, u)
            add_bias(0, 0, experts_at(dve, 0)[0])
            low_hidden(0, 0)
            tiles_of(dve, step)
            es = experts_at(dve, LAST - 1)
            add_bias(LAST, 1, es[1])
            finish(LAST - 1, 0, SLOT_TILES // 2 - 1, es[0])
            low_hidden(LAST, 1)
            finish(LAST, 1, SLOT_TILES // 2 - 1, es[1])

        @block.tensor
        def _(pe):
            def turn_rows(s, u, k):
                pe.wait_ge(rows_in[u], 16 * (k + 1))
                pe.sem_inc(pe_alone, 1)
                pe.wait_ge(x_lo_made, s + PRIMED)
                pe.sem_inc(pe_alone, 1)
                for a in range(CC):
                    last = nc.tensor.transpose(ps_x[u][:, a * P:(a + 1) * P], rows[:, u, a * P:(a + 1) * P],
                                               ident[:, :])
                last.then_inc(x_turned, 1)

            def first_layer(s, u, e):
                pe.wait_ge(x_lo_made, s + 1 + 2 * PRIMED)
                pe.sem_inc(pe_alone, 1)
                pe.wait_ge(h_made, s + PRIMED)
                pe.sem_inc(pe_alone, 1)
                for a in range(CC):
                    chunk = bass.ds(e * CC + a, 1)
                    cols = slice(a * P, (a + 1) * P)
                    last = three_products(nc, ps_h[u][:, :], (x_hi[:, u, cols], x_lo[:, u, cols]),
                                          tuple(w[:, chunk, :].rearrange("p a n -> p (a n)") for w in (w_hi, w_lo)),
                                          a == 0, a == CC - 1)
                last.then_inc(h_summed, 1)

            def turn_hidden(s, u):
                pe.wait_ge(h_made, s + 1 + 2 * PRIMED)
                pe.sem_inc(pe_alone, 1)
                pe.wait_ge(h_lo_made, s + PRIMED)
                pe.sem_inc(pe_alone, 1)
                for f in range(FO):
                    last = nc.tensor.transpose(ps_t[u][:, f * P:(f + 1) * P], h[:, u, f * P:(f + 1) * P],
                                               ident[:, :])
                last.then_inc(h_turned, 1)

            def second_layer(s, u, e):
                pe.wait_ge(h_lo_made, s + 1 + 2 * PRIMED)
                pe.sem_inc(pe_alone, 1)
                pe.wait_ge(y_made, s + PRIMED)
                pe.sem_inc(pe_alone, 1)
                for f in range(FO):
                    chunk = bass.ds(e * 2 + HALF + f // 2, 1)
                    cols, to = slice(f * P, (f + 1) * P), slice((f % 2) * C, (f % 2 + 1) * C)
                    last = three_products(nc, ps_y[u][:, 0:C], (h_hi[:, u, cols], h_lo[:, u, cols]),
                                          tuple(w[:, chunk, to].rearrange("p a n -> p (a n)") for w in (w_hi, w_lo)),
                                          f == 0, f == FO - 1)
                last.then_inc(y_summed, 1)

            def step(s, u, k, es):
                first_layer(s + 1, 1 - u, es[1])
                turn_rows(s + 2, u, k + 1)
                second_layer(s, u, es[0])
                turn_hidden(s + 1, 1 - u)

            pe.wait_ge(ident_made, 2)
            for u in range(2):
                turn_rows(u, u, 0)
            first_layer(0, 0, experts_at(pe, 0)[0])
            turn_hidden(0, 0)
            tiles_of(pe, step)
            es = experts_at(pe, LAST - 1)
            first_layer(LAST, 1, es[1])
            second_layer(LAST - 1, 0, es[0])
            turn_hidden(LAST, 1)
            second_layer(LAST, 1, es[1])


def combine(nc, slots, shares, ys_dram, x1_dram, out):
    with ExitStack() as ctx:
        def sb(name, shape, dt=F32):
            return ctx.enter_context(nc.sbuf_tensor(name, shape, dt))

        def sem(name):
            return ctx.enter_context(nc.semaphore(name))

        acc = sb("acc", [P, 2, TILES, C])
        found = sb("found", [P, 2, TOP, TILES, C])
        block_slots = sb("block_slots6", [P, 2, TOP, TILES], I32)
        block_shares = sb("block_shares", [P, 2, TOP, TILES])
        x1_in = [sem(f"x1_in{u}") for u in range(2)]
        copied = sem("slots_copied6")
        shares_copied = sem("shares_copied")
        gathered = [sem(f"gathered{u}") for u in range(2)]
        half_made = sem("half_made")
        acc_made = sem("acc_made")
        out_stored = [sem(f"out_stored{u}") for u in range(2)]
        sp_alone, pool_alone, dve_alone = sem("sp_alone6"), sem("pool_alone6"), sem("dve_alone6")
        out_v = out.rearrange("b (c j p) d -> (b c) p j d", p=P, j=TILES)
        x1_v = x1_dram.rearrange("(n j p) d -> n p j d", p=P, j=TILES)
        GATHERS = 16 * TOP * TILES

        block = ctx.enter_context(nc.Block())

        @block.sync
        def _(sp):
            def load(n, u):
                sp.dma_start(acc[:, u, :, :], x1_v[n, :, :, :]).then_inc(x1_in[u], 16)

            def store(n, u):
                sp.wait_ge(acc_made, n + 1 + 2 * PRIMED)
                sp.sem_inc(sp_alone, 1)
                sp.dma_start(out_v[n, :, :, :], acc[:, u, :, :]).then_inc(out_stored[u], 16)

            for u in range(2):
                load(u, u)
            with sp.Fori(0, NB // 2 - 1) as k:
                for u in range(2):
                    store(2 * k + u, u)
                    sp.wait_ge(out_stored[u], 16 * (k + 1))
                    sp.sem_inc(sp_alone, 1)
                    load(2 * k + 2 + u, u)
            for u in range(2):
                store(NB - 2 + u, u)
            for u in range(2):
                sp.wait_ge(out_stored[u], 16 * (NB // 2))

        @block.gpsimd
        def _(pool):
            with pool.Fori(0, NB // 2) as k:
                for u in range(2):
                    pool.wait_ge(copied, 2 * k + u + 1)
                    pool.sem_inc(pool_alone, 1)
                    for i in range(TOP):
                        for j in range(TILES):
                            pool.indirect_dma_start(
                                found[:, u, i, j, :], None, ys_dram[:, :],
                                bass.IndirectOffsetOnAxis(ap=block_slots[:, u, i, j:j + 1], axis=0)
                                ).then_inc(gathered[u], 16)

        @block.vector
        def _(dve):
            dve.sem_inc(acc_made, 2 * PRIMED)

            def places(n, u):
                dve.wait_ge(acc_made, n - 1 + 2 * PRIMED)
                dve.sem_inc(dve_alone, 1)
                for i in range(TOP):
                    last = nc.vector.tensor_copy(block_shares[:, u, i, :], shares[i][:, bass.ds(n * TILES, TILES)])
                last.then_inc(shares_copied, 1)
                nc.vector.tensor_copy(block_slots[:, u, :, :],
                                      slots[:, :, bass.ds(n * TILES, TILES)]).then_inc(copied, 1)

            def body(n, u, k, start_next):
                start_next()
                dve.wait_ge(x1_in[u], 16 * (k + 1))
                dve.sem_inc(dve_alone, 1)
                dve.wait_ge(shares_copied, n + 1)
                dve.sem_inc(dve_alone, 1)
                dve.wait_ge(gathered[u], GATHERS * (k + 1))
                dve.sem_inc(dve_alone, 1)
                for i in range(TOP):
                    for j in range(TILES):
                        last = nc.vector.scalar_tensor_tensor(
                            out=acc[:, u, j, :], in0=found[:, u, i, j, :], scalar=block_shares[:, u, i, j:j + 1],
                            in1=acc[:, u, j, :], op0=ALU.mult, op1=ALU.add)
                    if i == 0:
                        last.then_inc(half_made, 1)
                        dve.wait_ge(half_made, n + 1)
                        dve.sem_inc(dve_alone, 1)
                last.then_inc(acc_made, 1)
            pipeline(dve, lambda n, u, k: places(n, u), body)


def transformer_block(nc, w, out):
    parts_dram = nc.dram_tensor("parts_dram", (2, PARTS, 2, DHE, H, B * T), BF16).ap()
    v_dram = nc.dram_tensor("v_dram", (HG, P, B * T // P, GH, VW), F32).ap()
    minus_dram = [nc.dram_tensor(f"minus_dram{late}", (PARTS, GH, n, P), BF16).ap()
                  for late, n in enumerate((EARLY, QT - EARLY))]
    y_dram = nc.dram_tensor("y_dram", (B * T, C), F32).ap()
    project(nc, w["L0_attn_x"], (w["L0_attn_Wq_down"], w["L0_attn_Wk_down"], w["L0_attn_Wv_down"]),
            ((w["L0_attn_Wq_up_c"], w["L0_attn_Wq_up_e"]), (w["L0_attn_Wk_up_c"], w["L0_attn_Wk_up_e"]),
             (w["L0_attn_Wv_up"],)), w["rope_cos"], w["rope_sin"], parts_dram, v_dram)
    attend(nc, parts_dram, v_dram, minus_dram, y_dram)
    xn_dram, x1_dram = (nc.dram_tensor(name, (B * T, C), F32).ap() for name in ("xn_dram", "x1_dram"))
    xs_dram, ys_dram = (nc.dram_tensor(name, (SLOT_TILES * P, C), F32).ap() for name in ("xs_dram", "ys_dram"))
    with ExitStack() as ctx:
        w_sb = [ctx.enter_context(nc.sbuf_tensor(f"experts_{half}", [P, 2 * E * F * C // (P * WCH), WCH], F32R))
                for half in ("hi", "lo")]
        logits = ctx.enter_context(nc.sbuf_tensor("logits", [P, NB * TILES, E], F32))
        slots = ctx.enter_context(nc.sbuf_tensor("slots", [P, TOP, NB * TILES], I32))
        shares = [ctx.enter_context(nc.sbuf_tensor(f"shares{i}", [P, NB * TILES], F32)) for i in range(TOP)]
        expert_of = ctx.enter_context(nc.sbuf_tensor("expert_of", [P, SLOT_TILES], I32))
        mix(nc, w["L0_attn_x"], y_dram, w["L0_attn_Wc"], w["L0_ffn_Wr"], w["L0_ffn_br"], w["L0_ffn_W1"],
            w["L0_ffn_W2"], w_sb, logits, xn_dram, x1_dram, xs_dram)
        dispatch(nc, logits, w["tile_numbers"], slots, shares, expert_of, xn_dram, xs_dram)
        experts(nc, w_sb, expert_of, w["L0_ffn_b1"], w["L0_ffn_b2"], xs_dram, ys_dram)
        combine(nc, slots, shares, ys_dram, x1_dram, out)


_INS = ["L0_attn_x", "L0_attn_Wq_down", "L0_attn_Wk_down", "L0_attn_Wv_down", "L0_attn_Wq_up_c",
        "L0_attn_Wq_up_e", "L0_attn_Wk_up_c", "L0_attn_Wk_up_e", "L0_attn_Wv_up", "L0_attn_Wc",
        "L0_ffn_Wr", "L0_ffn_br", "L0_ffn_W1", "L0_ffn_b1", "L0_ffn_W2", "L0_ffn_b2"]


def kernel(**inputs):
    import numpy as np
    import concourse.bacc as bacc
    from concourse.bass_utils import run_bass_kernel_spmd

    nc = bacc.Bacc("TRN2", target_bir_lowering=False, num_devices=1)
    arrays = {name: np.ascontiguousarray(inputs[name]) for name in _INS}
    inverse = np.float32(1.0) / np.float32(10000.0) ** (np.arange(0, DHE, 2, dtype=np.float32) / np.float32(DHE))
    angle = np.arange(T, dtype=np.float32)[None, :] * np.concatenate((inverse, inverse))[:, None]
    sign = np.where(np.arange(DHE) % 2 == 0, np.float32(-1.0), np.float32(1.0))
    arrays["rope_cos"] = np.repeat(np.cos(angle).astype(np.float32), H, axis=0)
    arrays["rope_sin"] = np.repeat((np.sin(angle) * sign[:, None]).astype(np.float32), H, axis=0)
    arrays["tile_numbers"] = np.tile(np.arange(SLOT_TILES, dtype=np.float32), (P, 1))
    args = {name: nc.dram_tensor(f"in_{name}", a.shape, mybir.dt.from_np(a.dtype), kind="ExternalInput").ap()
            for name, a in arrays.items()}
    out = nc.dram_tensor("out_0", (B, T, C), F32, kind="ExternalOutput").ap()
    transformer_block(nc, args, out)
    feeds = {f"in_{name}": a for name, a in arrays.items()}
    return run_bass_kernel_spmd(nc, [feeds], core_ids=[0]).results[0]["out_0"]
```
